# Optimizing a Trainium2 kernel written in Bass

```python
import numpy as np
import jax
import jax.numpy as jnp

def _softmax(x, axis=-1):
    return jax.nn.softmax(x, axis=axis)

def _gelu(x):
    return jax.nn.gelu(x, approximate=True)

def _silu(x):
    return jax.nn.silu(x)

def _sigmoid(x):
    return jax.nn.sigmoid(x)

def _layernorm(x, axis=-1, eps=1e-05):
    m = jnp.mean(x, axis=axis, keepdims=True)
    v = jnp.var(x, axis=axis, keepdims=True)
    return (x - m) / jnp.sqrt(v + eps)

def _scatter_add(tgt, idx, src, axis=0):
    return tgt.at[idx].add(src)

def _segment_sum(src, seg, n):
    return jax.ops.segment_sum(src, seg, n)
kernel_name = 'mk_adj_ffn_d2_adj_r2_bdb41e'

def setup_inputs(seed: int=0):
    np.random.seed(seed)
    _w = jnp.asarray

    def _rec_inputs():
        import jax
        import jax.numpy as jnp
        _gk = jax.random.key(seed)
        x = 7.22e-05 + 1 * jax.random.normal(jax.random.fold_in(_gk, 1), (32, 256, 128), jnp.float32)
        _a = jax.random.bernoulli(jax.random.fold_in(_gk, 2), 0.03125, (32, 256, 256))
        _a = jnp.logical_or(_a, jnp.swapaxes(_a, -1, -2))
        _a = jnp.logical_or(_a, jnp.eye(256, dtype=bool))
        _af = _a.astype(jnp.float32)
        adj = _af
        return (x, adj)
    x, adj = _rec_inputs()

    def _L0_gnn_setup():
        import jax, jax.numpy as jnp
        import numpy as np
        from jax import lax
        DIM = 128
        EPS = 1e-05

        def _bn(h, g, b, m, v):
            scale = g / jnp.sqrt(v + EPS)
            return h * scale[None, :, None] + (b - m * scale)[None, :, None]

        def _conv1d(h, w, pad):
            return lax.conv_general_dilated(h, w, window_strides=(1,), padding=[(pad, pad)], dimension_numbers=('NCH', 'OIH', 'NCH'))
        key = jax.random.key(seed)
        ks = jax.random.split(key, 16)
        bs, n, d = (16, 1024, DIM)
        s = 0.05
        return {'x': jax.random.normal(ks[0], (bs, n, d), jnp.float32), 'mask': jnp.ones((bs, n, n), jnp.float32), 'w_se': jax.random.normal(ks[1], (3, d), jnp.float32) * s, 'b_se': jnp.zeros((3,), jnp.float32), 'conv1_w': jax.random.normal(ks[2], (d, d, 1), jnp.float32) * s, 'bn1_g': jnp.ones((d,), jnp.float32), 'bn1_b': jnp.zeros((d,), jnp.float32), 'bn1_m': jnp.zeros((d,), jnp.float32), 'bn1_v': jnp.ones((d,), jnp.float32), 'conv2_w': jax.random.normal(ks[3], (d, d, 17), jnp.float32) * s, 'bn2_g': jnp.ones((d,), jnp.float32), 'bn2_b': jnp.zeros((d,), jnp.float32), 'bn2_m': jnp.zeros((d,), jnp.float32), 'bn2_v': jnp.ones((d,), jnp.float32), 'w_msg': jax.random.normal(ks[4], (d, d), jnp.float32) * s, 'b_msg': jnp.zeros((d,), jnp.float32), 'w_ih': jax.random.normal(ks[5], (3 * d, 2 * d), jnp.float32) * s, 'b_ih': jnp.zeros((3 * d,), jnp.float32), 'w_hh': jax.random.normal(ks[6], (3 * d, d), jnp.float32) * s, 'b_hh': jnp.zeros((3 * d,), jnp.float32)}
    _L0_gnn_all = _L0_gnn_setup()
    _L0_gnn_in = {k: v for k, v in _L0_gnn_all.items() if k in ('w_se', 'b_se', 'conv1_w', 'bn1_g', 'bn1_b', 'bn1_m', 'bn1_v', 'conv2_w', 'bn2_g', 'bn2_b', 'bn2_m', 'bn2_v', 'w_msg', 'b_msg', 'w_ih', 'b_ih', 'w_hh', 'b_hh')}
    del _L0_gnn_all

    def _L0_ffn_setup():
        import jax, jax.numpy as jnp
        import numpy as np
        C = 128
        EPS = 1e-05
        N_ITERS = 30

        def _layernorm(x, w, bias):
            mu = jnp.mean(x, axis=-1, keepdims=True)
            var = jnp.mean(jnp.square(x - mu), axis=-1, keepdims=True)
            return (x - mu) * jax.lax.rsqrt(var + EPS) * w + bias
        key = jax.random.key(seed)
        kx, kw, kb, klw, klb = jax.random.split(key, 5)
        x = jax.random.normal(kx, (8, 1024, C), dtype=jnp.float32)
        bound = 1.0 / np.sqrt(C)
        W = jax.random.uniform(kw, (C, C), minval=-bound, maxval=bound, dtype=jnp.float32)
        b = jax.random.uniform(kb, (C,), minval=-bound, maxval=bound, dtype=jnp.float32)
        ln_w = jnp.ones((C,), dtype=jnp.float32)
        ln_b = jnp.zeros((C,), dtype=jnp.float32)
        return {'x': x, 'ln_w': ln_w, 'ln_b': ln_b, 'W': W, 'b': b}
    _L0_ffn_all = _L0_ffn_setup()
    _L0_ffn_in = {k: v for k, v in _L0_ffn_all.items() if k in ('ln_w', 'ln_b', 'W', 'b')}
    del _L0_ffn_all

    def _L1_gnn_setup():
        import jax, jax.numpy as jnp
        import numpy as np
        H = 4
        LN_EPS = 1e-05

        def _heads(x, B, N):
            return x.reshape(B, N, H, -1).transpose(0, 2, 1, 3)
        key = jax.random.key(seed)
        ks = jax.random.split(key, 6)
        B, N, IN, OUT = (4, 1024, 128, 128)
        return {'node_feats': jax.random.normal(ks[0], (B, N, IN), dtype=jnp.float32), 'adj_matrix': jax.random.uniform(ks[1], (B, N, N), dtype=jnp.float32), 'W_lin': jax.random.normal(ks[2], (IN, OUT), dtype=jnp.float32) * IN ** (-0.5), 'b_lin': jnp.zeros((OUT,), dtype=jnp.float32), 'W_q': jax.random.normal(ks[3], (IN, OUT), dtype=jnp.float32) * IN ** (-0.5), 'W_k': jax.random.normal(ks[4], (IN, OUT), dtype=jnp.float32) * IN ** (-0.5), 'ln_g': jnp.ones((OUT,), dtype=jnp.float32), 'ln_b': jnp.zeros((OUT,), dtype=jnp.float32)}
    _L1_gnn_all = _L1_gnn_setup()
    _L1_gnn_in = {k: v for k, v in _L1_gnn_all.items() if k in ('W_lin', 'b_lin', 'W_q', 'W_k', 'ln_g', 'ln_b')}
    del _L1_gnn_all

    def _L1_ffn_setup():
        import jax, jax.numpy as jnp
        import numpy as np
        B, S, H, NH, NE = (4, 512, 128, 4, 4)
        D = H // NH
        EPS = 1e-08

        def layernorm(x, g, b):
            m = jnp.mean(x, axis=-1, keepdims=True)
            v = jnp.mean((x - m) ** 2, axis=-1, keepdims=True)
            return (x - m) / jnp.sqrt(v + EPS) * g + b
        key = jax.random.key(seed)
        ks = jax.random.split(key, 18)
        sc = 0.05
        return {'x': jax.random.normal(ks[0], (B, S, H), jnp.float32), 'hl_w': jax.random.normal(ks[1], (NH, D, H), jnp.float32) * sc, 'hl_b': jax.random.normal(ks[2], (NH, D), jnp.float32) * sc, 'wq': jax.random.normal(ks[3], (NH, NE, D, D), jnp.float32) * sc, 'wk': jax.random.normal(ks[4], (NH, D, D), jnp.float32) * sc, 'wv': jax.random.normal(ks[5], (NH, D, D), jnp.float32) * sc, 'gate_w': jax.random.normal(ks[6], (NH, NE, NE * D), jnp.float32) * sc, 'gate_b': jax.random.normal(ks[7], (NH, NE), jnp.float32) * sc, 'ln_g': jnp.ones((D,), jnp.float32), 'ln_b': jnp.zeros((D,), jnp.float32), 'fc1_w': jax.random.normal(ks[8], (D, D), jnp.float32) * sc, 'fc1_b': jax.random.normal(ks[9], (D,), jnp.float32) * sc, 'fc2_w': jax.random.normal(ks[10], (D, D), jnp.float32) * sc, 'fc2_b': jax.random.normal(ks[11], (D,), jnp.float32) * sc, 'fnorm_g': jnp.ones((D,), jnp.float32), 'fnorm_b': jnp.zeros((D,), jnp.float32), 'fgate_w': jax.random.normal(ks[12], (NH, H), jnp.float32) * sc}
    _L1_ffn_all = _L1_ffn_setup()
    _L1_ffn_in = {k: v for k, v in _L1_ffn_all.items() if k in ('hl_w', 'hl_b', 'wq', 'wk', 'wv', 'gate_w', 'gate_b', 'ln_g', 'ln_b', 'fc1_w', 'fc1_b', 'fc2_w', 'fc2_b', 'fnorm_g', 'fnorm_b', 'fgate_w')}
    del _L1_ffn_all
    return {'x': x, 'adj': adj, 'L0_gnn_w_se': _L0_gnn_in['w_se'], 'L0_gnn_b_se': _L0_gnn_in['b_se'], 'L0_gnn_conv1_w': _L0_gnn_in['conv1_w'], 'L0_gnn_bn1_g': _L0_gnn_in['bn1_g'], 'L0_gnn_bn1_b': _L0_gnn_in['bn1_b'], 'L0_gnn_bn1_m': _L0_gnn_in['bn1_m'], 'L0_gnn_bn1_v': _L0_gnn_in['bn1_v'], 'L0_gnn_conv2_w': _L0_gnn_in['conv2_w'], 'L0_gnn_bn2_g': _L0_gnn_in['bn2_g'], 'L0_gnn_bn2_b': _L0_gnn_in['bn2_b'], 'L0_gnn_bn2_m': _L0_gnn_in['bn2_m'], 'L0_gnn_bn2_v': _L0_gnn_in['bn2_v'], 'L0_gnn_w_msg': _L0_gnn_in['w_msg'], 'L0_gnn_b_msg': _L0_gnn_in['b_msg'], 'L0_gnn_w_ih': _L0_gnn_in['w_ih'], 'L0_gnn_b_ih': _L0_gnn_in['b_ih'], 'L0_gnn_w_hh': _L0_gnn_in['w_hh'], 'L0_gnn_b_hh': _L0_gnn_in['b_hh'], 'L0_ffn_ln_w': _L0_ffn_in['ln_w'], 'L0_ffn_ln_b': _L0_ffn_in['ln_b'], 'L0_ffn_W': _L0_ffn_in['W'], 'L0_ffn_b': _L0_ffn_in['b'], 'L1_gnn_W_lin': _L1_gnn_in['W_lin'], 'L1_gnn_b_lin': _L1_gnn_in['b_lin'], 'L1_gnn_W_q': _L1_gnn_in['W_q'], 'L1_gnn_W_k': _L1_gnn_in['W_k'], 'L1_gnn_ln_g': _L1_gnn_in['ln_g'], 'L1_gnn_ln_b': _L1_gnn_in['ln_b'], 'L1_ffn_hl_w': _L1_ffn_in['hl_w'], 'L1_ffn_hl_b': _L1_ffn_in['hl_b'], 'L1_ffn_wq': _L1_ffn_in['wq'], 'L1_ffn_wk': _L1_ffn_in['wk'], 'L1_ffn_wv': _L1_ffn_in['wv'], 'L1_ffn_gate_w': _L1_ffn_in['gate_w'], 'L1_ffn_gate_b': _L1_ffn_in['gate_b'], 'L1_ffn_ln_g': _L1_ffn_in['ln_g'], 'L1_ffn_ln_b': _L1_ffn_in['ln_b'], 'L1_ffn_fc1_w': _L1_ffn_in['fc1_w'], 'L1_ffn_fc1_b': _L1_ffn_in['fc1_b'], 'L1_ffn_fc2_w': _L1_ffn_in['fc2_w'], 'L1_ffn_fc2_b': _L1_ffn_in['fc2_b'], 'L1_ffn_fnorm_g': _L1_ffn_in['fnorm_g'], 'L1_ffn_fnorm_b': _L1_ffn_in['fnorm_b'], 'L1_ffn_fgate_w': _L1_ffn_in['fgate_w']}

def reference(x, adj, L0_gnn_w_se, L0_gnn_b_se, L0_gnn_conv1_w, L0_gnn_bn1_g, L0_gnn_bn1_b, L0_gnn_bn1_m, L0_gnn_bn1_v, L0_gnn_conv2_w, L0_gnn_bn2_g, L0_gnn_bn2_b, L0_gnn_bn2_m, L0_gnn_bn2_v, L0_gnn_w_msg, L0_gnn_b_msg, L0_gnn_w_ih, L0_gnn_b_ih, L0_gnn_w_hh, L0_gnn_b_hh, L0_ffn_ln_w, L0_ffn_ln_b, L0_ffn_W, L0_ffn_b, L1_gnn_W_lin, L1_gnn_b_lin, L1_gnn_W_q, L1_gnn_W_k, L1_gnn_ln_g, L1_gnn_ln_b, L1_ffn_hl_w, L1_ffn_hl_b, L1_ffn_wq, L1_ffn_wk, L1_ffn_wv, L1_ffn_gate_w, L1_ffn_gate_b, L1_ffn_ln_g, L1_ffn_ln_b, L1_ffn_fc1_w, L1_ffn_fc1_b, L1_ffn_fc2_w, L1_ffn_fc2_b, L1_ffn_fnorm_g, L1_ffn_fnorm_b, L1_ffn_fgate_w):
    import jax
    import jax.numpy as jnp

    def _L0_gnn_ref(x, mask, w_se, b_se, conv1_w, bn1_g, bn1_b, bn1_m, bn1_v, conv2_w, bn2_g, bn2_b, bn2_m, bn2_v, w_msg, b_msg, w_ih, b_ih, w_hh, b_hh):
        import jax, jax.numpy as jnp
        import numpy as np
        from jax import lax
        DIM = 128
        EPS = 1e-05

        def _bn(h, g, b, m, v):
            scale = g / jnp.sqrt(v + EPS)
            return h * scale[None, :, None] + (b - m * scale)[None, :, None]

        def _conv1d(h, w, pad):
            return lax.conv_general_dilated(h, w, window_strides=(1,), padding=[(pad, pad)], dimension_numbers=('NCH', 'OIH', 'NCH'))
        d = x.shape[-1]
        xc = jnp.transpose(x, (0, 2, 1))
        h = _bn(_conv1d(xc, conv1_w, 0), bn1_g, bn1_b, bn1_m, bn1_v)
        h = jax.nn.relu(h)
        h = _bn(_conv1d(h, conv2_w, 8), bn2_g, bn2_b, bn2_m, bn2_v)
        x_conv = jnp.transpose(jax.nn.relu(h + xc), (0, 2, 1))
        s = x @ w_se.T + b_se
        sq = jnp.sum(s * s, axis=-1)
        dist = sq[:, :, None] + sq[:, None, :] - 2.0 * jnp.einsum('bnd,bmd->bnm', s, s)
        A = jnp.exp(-dist) * mask
        msg = jax.nn.relu(x @ w_msg.T + b_msg)
        x_nmp = jnp.einsum('bnm,bmd->bnd', A, msg)
        x_in = jnp.concatenate([x_conv, x_nmp], axis=-1)
        gi = x_in @ w_ih.T + b_ih
        gh = x @ w_hh.T + b_hh
        gi_r, gi_z, gi_n = (gi[..., :d], gi[..., d:2 * d], gi[..., 2 * d:])
        gh_r, gh_z, gh_n = (gh[..., :d], gh[..., d:2 * d], gh[..., 2 * d:])
        r = jax.nn.sigmoid(gi_r + gh_r)
        z = jax.nn.sigmoid(gi_z + gh_z)
        nn_ = jnp.tanh(gi_n + r * gh_n)
        return (1.0 - z) * nn_ + z * x

    def _L0_ffn_ref(x, ln_w, ln_b, W, b):
        import jax, jax.numpy as jnp
        import numpy as np
        C = 128
        EPS = 1e-05
        N_ITERS = 30

        def _layernorm(x, w, bias):
            mu = jnp.mean(x, axis=-1, keepdims=True)
            var = jnp.mean(jnp.square(x - mu), axis=-1, keepdims=True)
            return (x - mu) * jax.lax.rsqrt(var + EPS) * w + bias

        def step(h, _):
            h = h + 0.01 * jnp.tanh(h)
            h = h * jax.nn.sigmoid(h)
            h = _layernorm(h, ln_w, ln_b)
            h = jnp.einsum('bsc,dc->bsd', h, W) + b
            return (h, None)
        x, _ = jax.lax.scan(step, x, None, length=N_ITERS)
        return x

    def _L1_gnn_ref(node_feats, adj_matrix, W_lin, b_lin, W_q, W_k, ln_g, ln_b):
        import jax, jax.numpy as jnp
        import numpy as np
        H = 4
        LN_EPS = 1e-05

        def _heads(x, B, N):
            return x.reshape(B, N, H, -1).transpose(0, 2, 1, 3)
        B, N, _ = node_feats.shape
        out_dim = W_lin.shape[1]
        hd = out_dim // H
        scale = hd ** (-0.5)
        lrelu = lambda z: jax.nn.leaky_relu(z, 0.01)
        X = _heads(lrelu(node_feats @ W_lin + b_lin), B, N)
        q = _heads(lrelu(node_feats @ W_q), B, N)
        k = _heads(lrelu(node_feats @ W_k), B, N)
        att = jax.nn.sigmoid(jnp.einsum('bhxd,bhyd->bhxy', q, k) * scale)
        adj_h = adj_matrix[:, None] * att
        deg = jnp.sum(adj_h, axis=-1)
        dis = jnp.where(deg > 0, deg ** (-0.5), 0.0)
        A = dis[..., :, None] * adj_h * dis[..., None, :]
        Y = jnp.einsum('bhxy,bhyd->bhxd', A, X)
        Y = Y.transpose(0, 2, 1, 3).reshape(B, N, out_dim)
        mu = jnp.mean(Y, axis=-1, keepdims=True)
        var = jnp.mean((Y - mu) ** 2, axis=-1, keepdims=True)
        return (Y - mu) * jax.lax.rsqrt(var + LN_EPS) * ln_g + ln_b

    def _L1_ffn_ref(x, hl_w, hl_b, wq, wk, wv, gate_w, gate_b, ln_g, ln_b, fc1_w, fc1_b, fc2_w, fc2_b, fnorm_g, fnorm_b, fgate_w):
        import jax, jax.numpy as jnp
        import numpy as np
        B, S, H, NH, NE = (4, 512, 128, 4, 4)
        D = H // NH
        EPS = 1e-08

        def layernorm(x, g, b):
            m = jnp.mean(x, axis=-1, keepdims=True)
            v = jnp.mean((x - m) ** 2, axis=-1, keepdims=True)
            return (x - m) / jnp.sqrt(v + EPS) * g + b
        b, s, h = x.shape
        nh, d, _ = wk.shape
        ne = wq.shape[1]
        sx = jnp.einsum('bsh,ndh->bnsd', x, hl_w) + hl_b[None, :, None, :]
        pad = sx == 0
        q = jnp.einsum('bnsd,neod->bneso', sx, wq)
        k = jnp.einsum('bnsd,nod->bnso', sx, wk)
        v = jnp.einsum('bnsd,nod->bnso', sx, wv)
        causal = jnp.where(jnp.tril(jnp.ones((s, s), bool)), 0.0, -jnp.inf).astype(x.dtype)
        scores = jnp.einsum('bnesd,bntd->bnest', q, k) * d ** 0.5 + causal
        att = jax.nn.softmax(scores, axis=-1)
        qkv = jnp.einsum('bnest,bntd->bnesd', att, v)
        qkv = jnp.where(pad[:, :, None], 0.0, qkv)
        out = jnp.transpose(qkv, (0, 1, 3, 2, 4)).reshape(b, nh, s, ne * d)
        gs = jax.nn.softmax(jnp.einsum('bnsf,nef->bnse', out, gate_w) + gate_b[None, :, None, :], axis=-1)
        mixed = jnp.einsum('bnsed,bnse->bnsd', out.reshape(b, nh, s, ne, d), gs)
        resid = sx[jnp.arange(nh), jnp.arange(nh)]
        hn = layernorm(mixed + resid, ln_g, ln_b)
        f_n = jnp.transpose(hn, (0, 2, 1, 3)).reshape(b, s, h)
        fx = f_n.reshape(b, s, nh, d)
        pm = fx == 0
        hx = jnp.where(pm, 0.0, fx @ fc1_w.T + fc1_b)
        hx = jax.nn.relu(hx)
        hx = jnp.where(pm, 0.0, hx @ fc2_w.T + fc2_b)
        hx = layernorm(hx + fx, fnorm_g, fnorm_b)
        fout = hx.reshape(b, s, h)
        fg = jax.nn.softmax(fout @ fgate_w.T, axis=-1)
        return (fout.reshape(b, s, nh, d) * fg[..., None]).reshape(b, s, h)
    x = x + _L0_gnn_ref(_layernorm(x, axis=-1), adj, L0_gnn_w_se, L0_gnn_b_se, L0_gnn_conv1_w, L0_gnn_bn1_g, L0_gnn_bn1_b, L0_gnn_bn1_m, L0_gnn_bn1_v, L0_gnn_conv2_w, L0_gnn_bn2_g, L0_gnn_bn2_b, L0_gnn_bn2_m, L0_gnn_bn2_v, L0_gnn_w_msg, L0_gnn_b_msg, L0_gnn_w_ih, L0_gnn_b_ih, L0_gnn_w_hh, L0_gnn_b_hh)
    x = x + _L0_ffn_ref(_layernorm(x, axis=-1), L0_ffn_ln_w, L0_ffn_ln_b, L0_ffn_W, L0_ffn_b)
    x = x + _L1_gnn_ref(_layernorm(x, axis=-1), adj, L1_gnn_W_lin, L1_gnn_b_lin, L1_gnn_W_q, L1_gnn_W_k, L1_gnn_ln_g, L1_gnn_ln_b)
    x = x + _L1_ffn_ref(_layernorm(x, axis=-1), L1_ffn_hl_w, L1_ffn_hl_b, L1_ffn_wq, L1_ffn_wk, L1_ffn_wv, L1_ffn_gate_w, L1_ffn_gate_b, L1_ffn_ln_g, L1_ffn_ln_b, L1_ffn_fc1_w, L1_ffn_fc1_b, L1_ffn_fc2_w, L1_ffn_fc2_b, L1_ffn_fnorm_g, L1_ffn_fnorm_b, L1_ffn_fgate_w)
    return x

_drawn_inputs = setup_inputs


def setup_inputs(seed=0):
    import zlib

    import numpy as np

    out = dict(_drawn_inputs(seed))
    spreads = {'L0_gnn_b_se': (0.0, 2.0),
     'L0_gnn_bn1_g': (1.0, 0.2),
     'L0_gnn_bn1_b': (0.0, 0.274),
     'L0_gnn_bn1_m': (0.0, 0.1),
     'L0_gnn_bn1_v': (1.0, 0.6),
     'L0_gnn_bn2_g': (1.0, 0.2),
     'L0_gnn_bn2_b': (0.0, 0.402),
     'L0_gnn_bn2_m': (0.0, 0.344),
     'L0_gnn_bn2_v': (1.0, 0.6),
     'L0_gnn_b_msg': (0.0, 0.1),
     'L0_gnn_b_ih': (0.0, 0.1),
     'L0_gnn_b_hh': (0.0, 0.1),
     'L0_ffn_ln_w': (1.0, 0.2),
     'L0_ffn_ln_b': (0.0, 0.1),
     'L1_gnn_b_lin': (0.0, 0.1),
     'L1_gnn_ln_g': (1.0, 0.2),
     'L1_gnn_ln_b': (0.0, 0.1),
     'L1_ffn_ln_g': (1.0, 0.548),
     'L1_ffn_ln_b': (0.0, 0.532),
     'L1_ffn_fnorm_g': (1.0, 0.561),
     'L1_ffn_fnorm_b': (0.0, 0.516)}
    factors = {'L1_ffn_hl_b': 3.771,
     'L1_ffn_wq': 8.0,
     'L1_ffn_wk': 8.0,
     'L1_ffn_wv': 2.818,
     'L1_ffn_gate_w': 8.0,
     'L1_ffn_gate_b': 35.365,
     'L1_ffn_fc1_w': 8.0,
     'L1_ffn_fc1_b': 8.0,
     'L1_ffn_fc2_w': 8.0,
     'L1_ffn_fc2_b': 25.325}
    for name, (base, spread) in spreads.items():
        noise = np.random.default_rng([zlib.crc32(name.encode()), seed]).standard_normal(out[name].shape)
        drawn = base * np.exp(spread * noise) if base else spread * noise
        out[name] = jnp.asarray(drawn.astype(out[name].dtype))
    for name, factor in factors.items():
        out[name] = (out[name] * factor).astype(out[name].dtype)
    return out
```

```python
from contextlib import ExitStack, contextmanager

import concourse.bass as bass
from concourse import mybir

ALU = mybir.AluOpType
ACT = mybir.ActivationFunctionType
AX = mybir.AxisListType
F32 = mybir.dt.float32
BF16 = mybir.dt.bfloat16

P = 128
B = 32
N = 256
D = 128
J = N // P
TILES = B * J
TAPS = 17
PAD = TAPS // 2
SE = 3
STEPS = 30
H = 4
HD = D // H
E = 4
LN_EPS = 1e-5
NORM_EPS = 1e-8


@contextmanager
def stage_semaphores(nc, prefix):
    made = []

    def sem(name):
        made.append(nc.alloc_semaphore(name=prefix + name))
        return made[-1]

    yield sem
    nc.clear_and_free_semaphores(made)
    nc.all_engine_barrier()


def outer_norm(nc, ctx, sem, x_stats, rstd, shift, name):
    std = ctx.enter_context(nc.sbuf_tensor(f"{name}_std", [P, TILES], F32))
    eps = ctx.enter_context(nc.sbuf_tensor(f"{name}_eps", [P, 1], F32))
    eps_set, std_done, rstd_done, norm_ready = (
        sem(f"ln_{n}") for n in ("eps_set", "std_done", "rstd_done", "ready"))

    def on_scalar(act):
        act.wait_ge(eps_set, 1)
        act.activation(std[:, :], x_stats[:, :, 1], ACT.Sqrt, bias=eps[:, 0:1]).then_inc(std_done, 1)

    def on_vector(dve):
        dve.memset(eps[:, :], LN_EPS).then_inc(eps_set, 1)
        dve.wait_ge(std_done, 1)
        dve.reciprocal(rstd[:, :], std[:, :]).then_inc(rstd_done, 1)
        dve.wait_ge(rstd_done, 1)
        dve.scalar_tensor_tensor(shift[:, :], x_stats[:, :, 0], -1.0, rstd[:, :], ALU.mult, ALU.mult)\
           .then_inc(norm_ready, 1)

    return on_scalar, on_vector, norm_ready


def after(eng, sem, count):
    if not (isinstance(count, int) and count < 1):
        eng.wait_ge(sem, count)


def keep_stats(dve, c, b, mean_var):
    return dve.tensor_scalar(c["x_stats"][:, bass.ds(b * J, J), :], mean_var, 1.0, None, ALU.mult)


def stage_setup(nc, d, c):
    CHUNKS = 4
    PER = B // CHUNKS
    with ExitStack() as ctx:
        def sb(n, s, t=F32):
            return ctx.enter_context(nc.sbuf_tensor(n, s, t))

        sem = ctx.enter_context(stage_semaphores(nc, "setup_"))
        x_loaded = [sem(f"x_loaded{k}") for k in range(CHUNKS)]
        ident_zeroed, ident_done, ones_done = sem("ident_zeroed"), sem("ident_done"), sem("ones_done")
        stats_half, stats_done = sem("stats_half"), sem("stats_done")
        stats_kept = sem("stats_kept")
        bn6, mean_var = sb("setup_bn6", [P, J, 6]), sb("setup_mean_var", [P, J, 2])
        block = ctx.enter_context(nc.Block())

        @block.sync
        def _(sp):
            for k in range(CHUNKS):
                sp.dma_start(c["x"][:, k * PER * J:(k + 1) * PER * J, :].rearrange("p (b j) d -> p b j d", j=J),
                             d["x"][k * PER:(k + 1) * PER].rearrange("b (j p) d -> p b j d", p=P))\
                  .then_inc(x_loaded[k], 16)

        @block.gpsimd
        def _(pool):
            pool.memset(c["ident"][:, :], 0.0).then_inc(ident_zeroed, 1)
            pool.wait_ge(ident_zeroed, 1)
            pool.affine_select(out=c["ident"][:, :], in_=c["ident"][:, :], compare_op=ALU.not_equal, fill=1.0,
                               base=0, pattern=[[-1, P]], channel_multiplier=1).then_inc(ident_done, 1)
            pool.wait_ge(ident_done, 1)

        @block.vector
        def _(dve):
            dve.memset(c["ones"][:, :], 1.0).then_inc(ones_done, 1)
            dve.memset(c["ones3"][:, :], 1.0).then_inc(ones_done, 1)
            dve.memset(c["minus_half"][:, :], -0.5).then_inc(ones_done, 1)
            dve.wait_ge(ones_done, 3)
            dve.sem_inc(stats_kept, 1)
            for k in range(CHUNKS):
                dve.wait_ge(x_loaded[k], 16)
                with dve.Fori(k * PER + 1, (k + 1) * PER + 1) as n:
                    b = n - 1
                    dve.wait_ge(ones_done, 3)
                    dve.wait_ge(stats_kept, n)
                    for j in range(J):
                        last = dve.bn_stats(bn6[:, j, :], c["x"][:, b * J + j, :])
                    last.then_inc(stats_half, 1)
                    dve.wait_ge(ones_done, 3)
                    dve.wait_ge(stats_half, n)
                    for j in range(J):
                        last = dve.bn_aggr(mean_var[:, j, :], bn6[:, j, :])
                    last.then_inc(stats_done, 1)
                    dve.wait_ge(stats_done, n)
                    keep_stats(dve, c, b, mean_var[:, :, :]).then_inc(stats_kept, 1)
            dve.wait_ge(stats_kept, B + 1)


def split_rows(dve, row, work, parts, done):
    dve.tensor_copy(parts[0], row).then_inc(done, 1)
    dve.wait_ge(done, 1)
    dve.tensor_tensor(work, row, parts[0], ALU.subtract).then_inc(done, 1)
    dve.wait_ge(done, 2)
    dve.tensor_copy(parts[1], work).then_inc(done, 1)
    dve.wait_ge(done, 3)
    dve.tensor_tensor(work, work, parts[1], ALU.subtract).then_inc(done, 1)
    dve.wait_ge(done, 4)
    dve.tensor_copy(parts[2], work).then_inc(done, 1)


def each(eng, batch):
    batch(0, 0)
    batch(1, 1)
    with eng.Fori(1, B // 2) as i:
        for q in range(2):
            batch(i * 2 + q, q)


def adj_count(b, q):
    return 16 * (b // 2 + 1) if isinstance(b, int) else (b - q) * 8 + 16


def stage_gated_conv(nc, d, c):
    G = 4 * D
    with ExitStack() as ctx:
        def sb(n, s, t=F32):
            return ctx.enter_context(nc.sbuf_tensor("g_" + n, s, t))

        def ps(n, s):
            return ctx.enter_context(nc.psum_tensor("g_" + n, s, F32))

        sem = ctx.enter_context(stage_semaphores(nc, "g_"))
        x, ident = c["x"], c["ident"]
        w1, w2 = sb("w1", [P, D]), sb("w2", [P, TAPS, D])
        wmsg, wih, whh, wse = sb("wmsg", [P, D]), sb("wih", [P, 2, 3 * D]), sb("whh", [P, 3 * D]), sb("wse", [P, SE])
        bse = sb("bse", [SE, 1])
        bn = sb("bn", [P, 2, 4])
        bn_work = sb("bn_work", [P, 2, 2])
        bn_scale, bn_shift = sb("bn_scale", [P, 2, 1]), sb("bn_shift", [P, 2, 1])
        eps = sb("eps", [P, 1])
        row = sb("row", [1, G + D])
        hidden_row = sb("hidden_row", [1, 3 * D])
        row_work = sb("row_work", [1, G + D])
        row_parts = sb("row_parts", [1, 3, G + D], BF16)
        bias3 = sb("bias3", [3, G + D], BF16)
        mhalf3, neg3 = sb("mhalf3", [SE, P]), sb("neg3", [SE, 1])

        xn = sb("xn", [P, 2, J, D])
        xT = sb("xT", [P, 2, N])
        h1 = sb("h1", [P, 2, N + 2 * PAD])
        sT, s2T = sb("sT", [SE, 2, N]), sb("s2T", [SE, 2, N])
        nsq = sb("nsq", [P, 2, J])
        msg = sb("msg", [P, 2, J, D])
        adj = sb("adj", [P, 2, J, N])
        expo = sb("expo", [P, 2, J, N])
        aT = sb("aT", [P, 2, J, N])
        pre = sb("pre", [P, 2, N])
        convT = sb("convT", [P, 2, N])
        nmpT = sb("nmpT", [P, 2, N])
        rz = sb("rz", [P, 2, J, 2 * D])
        cand, cand2, nn = sb("cand", [P, 2, J, D]), sb("cand2", [P, 2, J, D]), sb("nn", [P, 2, J, D])
        diff, mix, upd = sb("diff", [P, 2, J, D]), sb("mix", [P, 2, J, D]), sb("upd", [P, 2, J, D])
        bn6, mean_var = sb("bn6", [P, 2, J, 6]), sb("mean_var", [P, J, 2])

        p_xT = ps("p_xT", [P, 512])
        p_h1 = ps("p_h1", [P, 512])
        p_adj = ps("p_adj", [P, 512])
        p_dist = ps("p_dist", [P, 512])
        p_conv = ps("p_conv", [P, 512])
        p_nmp = ps("p_nmp", [P, 512])
        p_gate = ps("p_gate", [P, J, 512])

        small_loaded, hidden_loaded, w_loaded = sem("small_loaded"), sem("hidden_loaded"), sem("w_loaded")
        parts_done, parts_moved, row_ready = sem("parts_done"), sem("parts_moved"), sem("row_ready")
        eps_set, bn_std, bn_ready, bn_steps, consts_set = (sem("eps_set"), sem("bn_std"), sem("bn_ready"),
                                                           sem("bn_steps"), sem("consts_set"))
        adj_loaded = [sem("adj_loaded0"), sem("adj_loaded1")]
        names = ("xn_ready xT_psum xT_ready h1_psum h1_ready sT_psum sT_ready nsq_psum nsq_ready adj_psum "
                 "dist_psum expo_ready aT_ready msg_psum msg_ready conv_psum pre_ready conv_ready nmp_psum "
                 "nmp_ready gates_psum rz_ready cand_half cand_ready nn_ready diff_ready mix_ready "
                 "upd_ready x_ready stats_half stats_done stats_kept").split()
        s = {n: sem(n) for n in names}
        ln_act, ln_dve, norm_ready = outer_norm(nc, ctx, sem, c["x_stats"], c["rstd"], c["shift"], "g_ln")
        block = ctx.enter_context(nc.Block())

        @block.sync
        def _(sp):
            for dst, src in ((w1[:, :], d["conv1"]), (wmsg[:, :], d["wmsg"]),
                             (w2[:, :, :], d["conv2"]), (wih[:, :, :], d["wih"].rearrange("(a p) n -> p a n", p=P)),
                             (whh[:, :], d["whh"]), (wse[:, :], d["wse"]), (bse[:, :], d["bse"])):
                sp.dma_start(dst, src).then_inc(w_loaded, 16)
            def batch(b, q):
                after(sp, s["adj_psum"], b - 1)
                sp.dma_start(adj[:, q, :, :], d["adj"][b].rearrange("(j p) m -> p j m", p=P))\
                  .then_inc(adj_loaded[q], 16)

            each(sp, batch)

        @block.gpsimd
        def _(pool):
            for n, src in enumerate(("bn1_g", "bn1_b", "bn1_m", "bn1_v")):
                pool.dma_start(bn[:, 0, n:n + 1], d[src]).then_inc(small_loaded, 16)
            for n, src in enumerate(("bn2_g", "bn2_b", "bn2_m", "bn2_v")):
                pool.dma_start(bn[:, 1, n:n + 1], d[src]).then_inc(small_loaded, 16)
            pool.dma_start(row[:, 0:3 * D], d["bih"]).then_inc(hidden_loaded, 16)
            pool.dma_start(row[:, 3 * D:G], d["bhh"][:, 2 * D:3 * D]).then_inc(hidden_loaded, 16)
            pool.dma_start(row[:, G:G + D], d["bmsg"]).then_inc(hidden_loaded, 16)
            pool.dma_start(hidden_row[:, :], d["bhh"]).then_inc(hidden_loaded, 16)
            pool.memset(h1[:, :, 0:PAD], 0.0).then_inc(consts_set, 1)
            pool.memset(h1[:, :, PAD + N:], 0.0).then_inc(consts_set, 1)
            pool.memset(mhalf3[:, :], -0.5).then_inc(consts_set, 1)
            pool.memset(neg3[:, :], -1.0).then_inc(consts_set, 1)
            pool.wait_ge(parts_done, 5)
            for n in range(3):
                pool.dma_start(bias3[n:n + 1, :], row_parts[:, n, :]).then_inc(parts_moved, 16)
            def batch(b, q):
                pool.wait_ge(s["nn_ready"], b + 1)
                after(pool, s["mix_ready"], b)
                pool.tensor_tensor(diff[:, q, :, :], xn[:, q, :, :], nn[:, q, :, :], ALU.subtract)\
                    .then_inc(s["diff_ready"], 1)
                pool.wait_ge(s["upd_ready"], b + 1)
                pool.tensor_tensor(x[:, bass.ds(b * J, J), :], x[:, bass.ds(b * J, J), :], upd[:, q, :, :],
                                   ALU.add).then_inc(s["x_ready"], 1)

            each(pool, batch)

        @block.scalar
        def _(act):
            ln_act(act)
            act.wait_ge(eps_set, 1)
            act.wait_ge(small_loaded, 16 * 8)
            act.activation(bn_work[:, :, 0:1], bn[:, :, 3:4], ACT.Sqrt, bias=eps[:, 0:1]).then_inc(bn_std, 1)
            act.wait_ge(bn_ready, 1)
            act.wait_ge(consts_set, 4)
            act.wait_ge(w_loaded, 16 * 7)
            def batch(b, q):
                act.wait_ge(s["xT_psum"], b + 1)
                act.activation(xT[:, q, :], p_xT[:, 0:N], ACT.Copy).then_inc(s["xT_ready"], 1)
                act.wait_ge(s["sT_psum"], b + 1)
                act.activation(sT[:, q, :], p_h1[0:SE, N:2 * N], ACT.Identity, bias=bse[:, 0:1]).then_inc(s["sT_ready"], 1)
                act.activation(s2T[:, q, :], p_h1[0:SE, N:2 * N], ACT.Square, bias=bse[:, 0:1]).then_inc(s["sT_ready"], 1)
                act.activation(h1[:, q, PAD:PAD + N], p_h1[:, 0:N], ACT.Relu, bias=bn_shift[:, 0, :],
                               scale=bn_scale[:, 0, :]).then_inc(s["h1_ready"], 1)
                act.wait_ge(s["msg_psum"], b + 1)
                act.activation(msg[:, q, :, :], p_xT[:, N:2 * N].rearrange("p (j d) -> p j d", j=J), ACT.Relu)\
                   .then_inc(s["msg_ready"], 1)
                act.wait_ge(s["nsq_psum"], b + 1)
                act.activation(nsq[:, q, :], p_nmp[:, N:N + J], ACT.Copy).then_inc(s["nsq_ready"], 1)
                act.wait_ge(s["dist_psum"], b + 1)
                act.wait_ge(s["nsq_ready"], b + 1)
                for j in range(J):
                    act.activation(expo[:, q, j, :], p_dist[:, j * N:(j + 1) * N], ACT.Exp, scale=2.0,
                                   bias=nsq[:, q, j:j + 1]).then_inc(s["expo_ready"], 1)
                act.wait_ge(s["pre_ready"], b + 1)
                act.activation(convT[:, q, :], pre[:, q, :], ACT.Relu, bias=bn_shift[:, 1, :]).then_inc(s["conv_ready"], 1)
                act.wait_ge(s["nmp_psum"], b + 1)
                act.activation(nmpT[:, q, :], p_nmp[:, 0:N], ACT.Copy).then_inc(s["nmp_ready"], 1)
                act.wait_ge(s["gates_psum"], b + 1)
                act.activation(rz[:, q, :, :], p_gate[:, :, 0:2 * D], ACT.Tanh, scale=0.5).then_inc(s["rz_ready"], 1)
                act.wait_ge(s["cand_ready"], b + 1)
                act.activation(nn[:, q, :, :], cand2[:, q, :, :], ACT.Tanh).then_inc(s["nn_ready"], 1)

            each(act, batch)

        @block.vector
        def _(dve):
            dve.memset(eps[:, :], LN_EPS).then_inc(eps_set, 1)
            ln_dve(dve)
            dve.wait_ge(bn_std, 1)
            dve.reciprocal(bn_work[:, :, 1:2], bn_work[:, :, 0:1]).then_inc(bn_steps, 1)
            dve.wait_ge(bn_steps, 1)
            dve.tensor_tensor(bn_scale[:, :, :], bn[:, :, 0:1], bn_work[:, :, 1:2], ALU.mult).then_inc(bn_steps, 1)
            dve.wait_ge(bn_steps, 2)
            dve.tensor_tensor(bn_work[:, :, 0:1], bn[:, :, 2:3], bn_scale[:, :, :], ALU.mult).then_inc(bn_steps, 1)
            dve.wait_ge(bn_steps, 3)
            dve.tensor_tensor(bn_shift[:, :, :], bn[:, :, 1:2], bn_work[:, :, 0:1], ALU.subtract).then_inc(bn_ready, 1)
            dve.wait_ge(hidden_loaded, 16 * 4)
            dve.tensor_tensor(row[:, 0:2 * D], row[:, 0:2 * D], hidden_row[:, 0:2 * D], ALU.add).then_inc(row_ready, 1)
            dve.wait_ge(row_ready, 1)
            split_rows(dve, row[:, :], row_work[:, :], [row_parts[:, n, :] for n in range(3)], parts_done)
            dve.wait_ge(norm_ready, 1)
            dve.wait_ge(bn_ready, 1)
            def batch(b, q):
                after(dve, s["diff_ready"], b)
                for j in range(J):
                    t = b * J + j
                    dve.tensor_scalar(xn[:, q, j, :], x[:, t, :], c["rstd"][:, bass.ds(t, 1)],
                                      c["shift"][:, bass.ds(t, 1)], ALU.mult, ALU.add).then_inc(s["xn_ready"], 1)
                dve.wait_ge(s["adj_psum"], b + 1)
                dve.wait_ge(s["expo_ready"], (b + 1) * J)
                dve.tensor_tensor(aT[:, q, :, :], expo[:, q, :, :], p_adj[:, :].rearrange("p (j n) -> p j n", j=J),
                                  ALU.mult).then_inc(s["aT_ready"], 1)
                dve.wait_ge(s["conv_psum"], b + 1)
                dve.scalar_tensor_tensor(pre[:, q, :], p_conv[:, 0:N], bn_scale[:, 1, :], xT[:, q, :],
                                         ALU.mult, ALU.add).then_inc(s["pre_ready"], 1)
                dve.wait_ge(s["rz_ready"], b + 1)
                dve.scalar_tensor_tensor(cand[:, q, :, :], rz[:, q, :, 0:D], 1.0, p_gate[:, :, 3 * D:G],
                                         ALU.add, ALU.mult).then_inc(s["cand_half"], 1)
                dve.wait_ge(s["cand_half"], b + 1)
                dve.scalar_tensor_tensor(cand2[:, q, :, :], cand[:, q, :, :], 0.5, p_gate[:, :, 2 * D:3 * D],
                                         ALU.mult, ALU.add).then_inc(s["cand_ready"], 1)
                dve.wait_ge(s["diff_ready"], b + 1)
                dve.scalar_tensor_tensor(mix[:, q, :, :], rz[:, q, :, D:2 * D], 1.0, diff[:, q, :, :],
                                         ALU.add, ALU.mult).then_inc(s["mix_ready"], 1)
                after(dve, s["stats_kept"], b)
                dve.wait_ge(s["mix_ready"], b + 1)
                dve.scalar_tensor_tensor(upd[:, q, :, :], mix[:, q, :, :], 0.5, nn[:, q, :, :],
                                         ALU.mult, ALU.add).then_inc(s["upd_ready"], 1)
                dve.wait_ge(norm_ready, 1)
                dve.wait_ge(s["x_ready"], b + 1)
                for j in range(J):
                    last = dve.bn_stats(bn6[:, q, j, :], x[:, b * J + j, :])
                last.then_inc(s["stats_half"], 1)
                dve.wait_ge(norm_ready, 1)
                dve.wait_ge(s["stats_half"], b + 1)
                for j in range(J):
                    dve.bn_aggr(mean_var[:, j, :], bn6[:, q, j, :]).then_inc(s["stats_done"], 1)
                dve.wait_ge(s["stats_done"], (b + 1) * J)
                keep_stats(dve, c, b, mean_var[:, :, :]).then_inc(s["stats_kept"], 1)

            each(dve, batch)
            dve.wait_ge(s["stats_kept"], B)

        @block.tensor
        def _(pe):
            pe.wait_ge(w_loaded, 16 * 7)
            pe.wait_ge(consts_set, 4)
            pe.wait_ge(parts_moved, 16 * 3)
            def batch(b, q):
                after(pe, s["msg_ready"], b)
                pe.wait_ge(s["xn_ready"], (b + 1) * J)
                for j in range(J):
                    last = pe.transpose(p_xT[:, j * P:(j + 1) * P], xn[:, q, j, :], ident[:, :])
                last.then_inc(s["xT_psum"], 1)
                after(pe, s["aT_ready"], b)
                pe.wait_ge(adj_loaded[q], adj_count(b, q))
                for m in range(J):
                    for j in range(J):
                        last = pe.transpose(p_adj[:, m * N + j * P:m * N + (j + 1) * P],
                                            adj[:, q, j, m * P:(m + 1) * P], ident[:, :])
                last.then_inc(s["adj_psum"], 1)
                after(pe, s["h1_ready"], b)
                pe.wait_ge(s["xT_ready"], b + 1)
                pe.matmul(p_h1[:, 0:N], w1[:, :], xT[:, q, :], start=True, stop=True)
                pe.matmul(p_h1[0:SE, N:2 * N], wse[:, :], xT[:, q, :], start=True, stop=True,
                          skip_group_check=True).then_inc(s["sT_psum"], 1)
                for j in range(J):
                    part = p_xT[:, N + j * D:N + (j + 1) * D]
                    pe.matmul(part, c["ones3"][0:3, :], bias3[:, G:G + D], start=True, stop=False,
                              skip_group_check=True)
                    last = pe.matmul(part, xT[:, q, j * P:(j + 1) * P], wmsg[:, :], start=False, stop=True,
                                     skip_group_check=True)
                last.then_inc(s["msg_psum"], 1)
                after(pe, s["nmp_ready"], b)
                pe.wait_ge(s["sT_ready"], (b + 1) * 2)
                for j in range(J):
                    last = pe.matmul(p_nmp[:, N + j:N + j + 1], s2T[:, q, j * P:(j + 1) * P], neg3[:, :],
                                     start=True, stop=True)
                last.then_inc(s["nsq_psum"], 1)
                after(pe, s["expo_ready"], b * J)
                for j in range(J):
                    part = p_dist[:, j * N:(j + 1) * N]
                    pe.matmul(part, sT[:, q, j * P:(j + 1) * P], sT[:, q, :], start=True, stop=False)
                    last = pe.matmul(part, mhalf3[:, :], s2T[:, q, :], start=False, stop=True)
                last.then_inc(s["dist_psum"], 1)
                pe.wait_ge(s["h1_ready"], b + 1)
                after(pe, s["pre_ready"], b)
                for k in range(TAPS):
                    last = pe.matmul(p_conv[:, 0:N], w2[:, k, :], h1[:, q, k:k + N], start=k == 0, stop=k == TAPS - 1)
                last.then_inc(s["conv_psum"], 1)
                pe.wait_ge(s["nsq_ready"], b + 1)
                pe.wait_ge(s["msg_ready"], b + 1)
                pe.wait_ge(s["aT_ready"], b + 1)
                for m in range(J):
                    last = pe.matmul(p_nmp[:, 0:N], msg[:, q, m, :], aT[:, q, m, :], start=m == 0, stop=m == J - 1)
                last.then_inc(s["nmp_psum"], 1)
                after(pe, s["cand_ready"], b)
                for j in range(J):
                    pe.matmul(p_gate[:, j, :], c["ones3"][0:3, :], bias3[:, 0:G], start=True, stop=False,
                              skip_group_check=True)
                    xTj = xT[:, q, j * P:(j + 1) * P]
                    pe.matmul(p_gate[:, j, 0:2 * D], xTj, whh[:, 0:2 * D], start=False, stop=False,
                              skip_group_check=True)
                    pe.matmul(p_gate[:, j, 3 * D:G], xTj, whh[:, 2 * D:3 * D], start=False, stop=True,
                              skip_group_check=True)
                pe.wait_ge(s["conv_ready"], b + 1)
                for j in range(J):
                    pe.matmul(p_gate[:, j, 0:3 * D], convT[:, q, j * P:(j + 1) * P], wih[:, 0, :], start=False,
                              stop=False, skip_group_check=True)
                pe.wait_ge(s["nmp_ready"], b + 1)
                for j in range(J):
                    last = pe.matmul(p_gate[:, j, 0:3 * D], nmpT[:, q, j * P:(j + 1) * P], wih[:, 1, :],
                                     start=False, stop=True, skip_group_check=True)
                last.then_inc(s["gates_psum"], 1)

            each(pe, batch)


def stage_recurrent(nc, d, c):
    TG = 8
    GROUPS = TILES // TG
    HALF = TG // 2
    with ExitStack() as ctx:
        def sb(n, s, t=F32):
            return ctx.enter_context(nc.sbuf_tensor("r_" + n, s, t))

        sem = ctx.enter_context(stage_semaphores(nc, "r_"))
        x, ident = c["x"], c["ident"]
        w, w_gain, w_mid = sb("w", [P, D]), sb("w_gain", [P, D]), sb("w_mid", [P, D])
        ln_w, ln_b = sb("ln_w", [P, 1]), sb("ln_b", [P, 1])
        row, row_work = sb("row", [1, D]), sb("row_work", [1, D])
        row_parts, bias3 = sb("row_parts", [1, 3, D], BF16), sb("bias3", [3, HALF, D], BF16)
        h = sb("h", [P, GROUPS, TG, D])
        hT = sb("hT", [P, 2, TG, D])
        bn6 = sb("bn6", [P, 2, TG, 6])
        gap, ss, gap2 = sb("gap", [P, TG]), sb("ss", [P, TG]), sb("gap2", [P, TG])
        spread = sb("spread", [P, GROUPS, TG])
        scale = sb("scale", [P, GROUPS, TG])
        mean_var = sb("mean_var", [P, 2, TG, 2])
        p_hT = ctx.enter_context(nc.psum_tensor("r_p_hT", [P, 2, TG, D], F32))
        p_z = ctx.enter_context(nc.psum_tensor("r_p_z", [P, 2, TG, D], F32))

        loaded, mean_psum, bias_psum, w_steps, bias_row = (sem("loaded"), sem("mean_psum"), sem("bias_psum"),
                                                          sem("w_steps"), sem("bias_row"))
        parts_done, parts_moved = sem("parts_done"), sem("parts_moved")
        h_start = sem("h_start")
        scale_done, scaled, turned, copied, product = (sem("scale_done"), sem("scaled"), sem("turned"),
                                                       sem("copied"), sem("product"))
        tanh_done, mixed, silu_done, bn_done, gap_done, gap2_done, spread_done = (
            sem("tanh_done"), sem("mixed"), sem("silu_done"), sem("bn_done"), sem("gap_done"), sem("gap2_done"),
            sem("spread_done"))
        x_done, x_bn, x_aggr, x_kept = sem("x_done"), sem("x_bn"), sem("x_aggr"), sem("x_kept")
        ln_act, ln_dve, norm_ready = outer_norm(nc, ctx, sem, c["x_stats"], c["rstd"], c["shift"], "r_ln")
        CREDIT = 2
        block = ctx.enter_context(nc.Block())

        def front(step, g):
            return (step - 1) * GROUPS + g

        def back(step, g):
            return step * GROUPS + g

        @block.sync
        def _(sp):
            sp.dma_start(w[:, :], d["ffn_w"]).then_inc(loaded, 16)
            sp.dma_start(ln_w[:, :], d["ffn_ln_w"]).then_inc(loaded, 16)
            sp.dma_start(ln_b[:, :], d["ffn_ln_b"]).then_inc(loaded, 16)
            sp.dma_start(row[:, :], d["ffn_b"]).then_inc(loaded, 16)
            sp.wait_ge(parts_done, 5)
            for n in range(3):
                for t in range(HALF):
                    sp.dma_start(bias3[n:n + 1, t, :], row_parts[:, n, :]).then_inc(parts_moved, 16)

        @block.gpsimd
        def _(pool):
            def rescale(step, g):
                n = front(step, g) + 1
                pool.wait_ge(spread_done, n)
                pool.tensor_tensor(scale[:, g, :], spread[:, g, :], c["minus_half"][:, 0:TG], ALU.pow)\
                    .then_inc(scale_done, 1)
                pool.wait_ge(norm_ready, 1)
                pool.wait_ge(scale_done, n)
                for t in range(TG):
                    last = pool.tensor_scalar(h[:, g, t, :], h[:, g, t, :], scale[:, g, t:t + 1], float(D) ** 0.5,
                                              ALU.mult, ALU.mult)
                last.then_inc(scaled, 1)

            with pool.Fori(1, STEPS) as step:
                for g in range(GROUPS):
                    rescale(step, g)
            for g in range(GROUPS):
                rescale(STEPS, g)

        @block.tensor
        def _(pe):
            pe.wait_ge(w_steps, 1)
            pe.matmul(p_z[:, 0, 0, :], c["ones"][:, :], w_gain[:, :], start=True, stop=True).then_inc(mean_psum, 1)
            pe.matmul(p_hT[0:1, 0, 0, :], ln_b[:, :], w[:, :], start=True, stop=True).then_inc(bias_psum, 1)
            pe.sem_inc(product, CREDIT)
            pe.wait_ge(w_steps, 3)
            pe.wait_ge(bias_row, 1)
            pe.wait_ge(parts_moved, 16 * 3 * HALF)

            def turn(step, g):
                pe.wait_ge(scaled, front(step, g) + 1)
                pe.wait_ge(copied, front(step, g) + 1)
                for t in range(TG):
                    last = pe.transpose(p_hT[:, g % 2, t, :], h[:, g, t, :], ident[:, :])
                last.then_inc(turned, 1)

            def multiply(step, g):
                pe.wait_ge(copied, front(step, g) + 1 + CREDIT)
                pe.wait_ge(mixed, back(step, g) - 2 + 1)
                for a in range(0, TG, HALF):
                    pe.matmul(p_z[:, g % 2, a:a + HALF, :], c["ones3"][:, :], bias3[:, :, :], start=True, stop=False,
                              skip_group_check=True)
                    for t in range(a, a + HALF):
                        last = pe.matmul(p_z[:, g % 2, t, :], hT[:, g % 2, t, :], w[:, :], start=False, stop=True,
                                         skip_group_check=True)
                last.then_inc(product, 1)

            def all_groups(step):
                for g in range(GROUPS + 1):
                    if g < GROUPS:
                        turn(step, g)
                    if g >= 1:
                        multiply(step, g - 1)

            with pe.Fori(1, STEPS) as step:
                all_groups(step)
            all_groups(STEPS)

        @block.scalar
        def _(act):
            ln_act(act)
            act.sem_inc(copied, CREDIT)

            def copy_turned(step, g):
                act.wait_ge(turned, front(step, g) + 1)
                act.wait_ge(product, front(step, g) + 1)
                act.activation(hT[:, g % 2, :, :], p_hT[:, g % 2, :, :], ACT.Copy).then_inc(copied, 1)

            def tanh(step, g, src):
                act.activation(h[:, g, :, :], src, ACT.Tanh).then_inc(tanh_done, 1)

            def silu(step, g):
                act.wait_ge(mixed, back(step, g) + 1)
                act.activation(h[:, g, :, :], h[:, g, :, :], ACT.Silu).then_inc(silu_done, 1)

            for g in range(GROUPS + 1):
                if g < GROUPS:
                    act.wait_ge(h_start, g + 1)
                    act.activation(hT[:, g % 2, :, :], h[:, g, :, :], ACT.Tanh).then_inc(tanh_done, 1)
                if g >= 1:
                    silu(0, g - 1)
            with act.Fori(1, STEPS) as step:
                for g in range(GROUPS + 2):
                    if g < GROUPS:
                        copy_turned(step, g)
                    if 1 <= g <= GROUPS:
                        act.wait_ge(product, front(step, g - 1) + 1 + CREDIT)
                        tanh(step, g - 1, p_z[:, (g - 1) % 2, :, :])
                    if g >= 2:
                        silu(step, g - 2)
            for g in range(GROUPS):
                copy_turned(STEPS, g)

        @block.vector
        def _(dve):
            ln_dve(dve)
            dve.wait_ge(loaded, 16 * 4)
            dve.tensor_scalar(w_gain[:, :], w[:, :], ln_w[:, 0:1], None, ALU.mult).then_inc(w_steps, 1)
            dve.wait_ge(bias_psum, 1)
            dve.tensor_tensor(row[:, :], row[:, :], p_hT[0:1, 0, 0, :], ALU.add).then_inc(bias_row, 1)
            dve.wait_ge(mean_psum, 1)
            dve.tensor_scalar(w_mid[:, :], p_z[:, 0, 0, :], 1.0 / D, None, ALU.mult).then_inc(w_steps, 1)
            dve.wait_ge(w_steps, 2)
            dve.tensor_tensor(w[:, :], w_gain[:, :], w_mid[:, :], ALU.subtract).then_inc(w_steps, 1)
            dve.wait_ge(bias_row, 1)
            split_rows(dve, row[:, :], row_work[:, :], [row_parts[:, n, :] for n in range(3)], parts_done)
            dve.wait_ge(norm_ready, 1)

            def start(g):
                for t in range(TG):
                    a = g * TG + t
                    last = dve.tensor_scalar(h[:, g, t, :], x[:, a, :], c["rstd"][:, a:a + 1], c["shift"][:, a:a + 1],
                                             ALU.mult, ALU.add)
                last.then_inc(h_start, 1)

            def mix(step, g):
                dve.wait_ge(tanh_done, back(step, g) + 1)
                dve.scalar_tensor_tensor(h[:, g, :, :], h[:, g, :, :], 0.01, p_z[:, g % 2, :, :], ALU.mult, ALU.add)\
                   .then_inc(mixed, 1)

            def stats(step, g):
                n = back(step, g)
                dve.wait_ge(silu_done, n + 1)
                for t in range(TG):
                    last = dve.bn_stats(bn6[:, g % 2, t, :], h[:, g, t, :])
                last.then_inc(bn_done, 1)
                dve.wait_ge(bn_done, n + 1)
                dve.tensor_tensor(gap[:, :], bn6[:, g % 2, :, 1], bn6[:, g % 2, :, 4], ALU.subtract)
                dve.tensor_tensor(ss[:, :], bn6[:, g % 2, :, 2], bn6[:, g % 2, :, 5], ALU.add).then_inc(gap_done, 1)
                dve.wait_ge(gap_done, n + 1)
                dve.scalar_tensor_tensor(gap2[:, :], gap[:, :], D / 4.0, gap[:, :], ALU.mult, ALU.mult).then_inc(gap2_done, 1)
                dve.wait_ge(gap2_done, n + 1)
                dve.scalar_tensor_tensor(spread[:, g, :], gap2[:, :], D * LN_EPS, ss[:, :], ALU.add, ALU.add)\
                   .then_inc(spread_done, 1)

            for g in range(GROUPS + 2):
                if g < GROUPS:
                    start(g)
                if 1 <= g <= GROUPS:
                    dve.wait_ge(tanh_done, g)
                    dve.scalar_tensor_tensor(h[:, g - 1, :, :], hT[:, (g - 1) % 2, :, :], 0.01, h[:, g - 1, :, :],
                                             ALU.mult, ALU.add).then_inc(mixed, 1)
                if g >= 2:
                    stats(0, g - 2)
            with dve.Fori(1, STEPS) as step:
                for g in range(1, GROUPS + 2):
                    if g <= GROUPS:
                        mix(step, g - 1)
                    if g >= 2:
                        stats(step, g - 2)
            for g in range(GROUPS):
                dve.wait_ge(product, front(STEPS, g) + 1 + CREDIT)
                xg = x[:, g * TG:(g + 1) * TG, :]
                dve.tensor_tensor(xg, xg, p_z[:, g % 2, :, :], ALU.add).then_inc(mixed, 1)
                dve.wait_ge(mixed, back(STEPS, g) + 1)
                for t in range(TG):
                    last = dve.bn_stats(bn6[:, g % 2, t, :], x[:, g * TG + t, :])
                last.then_inc(x_bn, 1)
                dve.wait_ge(x_bn, g + 1)
                for t in range(TG):
                    last = dve.bn_aggr(c["x_stats"][:, g * TG + t, :], bn6[:, g % 2, t, :])
            last.then_inc(x_kept, 1)
            dve.wait_ge(x_kept, 1)


def skewed(eng, front, back):
    front(0, 0)
    front(1, 1)
    back(0, 0)
    with eng.Fori(1, B // 2) as i:
        for q in range(2):
            front(i * 2 + q, q)
            back(i * 2 + q - 1, 1 - q)
    back(B - 1, 1)


def stage_graph_attention(nc, d, c):
    with ExitStack() as ctx:
        def sb(n, s, t=F32):
            return ctx.enter_context(nc.sbuf_tensor("a_" + n, s, t))

        def ps(n, s):
            return ctx.enter_context(nc.psum_tensor("a_" + n, s, F32))

        sem = ctx.enter_context(stage_semaphores(nc, "a_"))
        x, ident = c["x"], c["ident"]
        w = sb("w", [P, 3, D])
        row, row_work = sb("row", [1, D]), sb("row_work", [1, D])
        row_parts, bias3 = sb("row_parts", [1, 3, D], BF16), sb("bias3", [3, J, D], BF16)
        gain, offset = sb("gain", [P, J, D]), sb("offset", [P, J, D])
        minus_half = c["minus_half"]
        xn = sb("xn", [P, 2, J, D])
        xT = sb("xT", [P, 2, N])
        adj = sb("adj", [P, 2, J, N])
        relu_qk, relu_x = sb("relu_qk", [P, 2, N]), sb("relu_x", [P, J, D])
        qkT = sb("qkT", [P, 2, 2, N])
        lin = sb("lin", [P, 2, J, D])
        att = sb("att", [P, 2, H, J * N])
        ah = sb("ah", [P, 2, H, J * N])
        degree, linked, root, dis = (sb("degree", [P, J * H]), sb("linked", [P, J * H]), sb("root", [P, J * H]),
                                     sb("dis", [P, 2, J * H]))
        lin_dis = sb("lin_dis", [P, 2, J, D])
        y, yn, yg, x_off = sb("y", [P, J, D]), sb("yn", [P, J, D]), sb("yg", [P, J, D]), sb("x_off", [P, J, D])
        y6, y_stats, y_var, y_rstd = sb("y6", [P, J, 6]), sb("y_stats", [P, J, 2]), sb("y_var", [P, J]), sb("y_rstd", [P, J])
        bn6, mean_var = sb("bn6", [P, J, 6]), sb("mean_var", [P, J, 2])

        p_xT = ps("p_xT", [P, 512])
        p_qk = ps("p_qk", [P, 2, N])
        p_adj = ps("p_adj", [P, J * N])
        p_s = ps("p_s", [P, H, J * N])
        p_y = ps("p_y", [P, 512])

        loaded, parts_done, parts_moved = sem("loaded"), sem("parts_done"), sem("parts_moved")
        adj_loaded = [sem("adj_loaded0"), sem("adj_loaded1")]
        names = ("xn_ready xT_psum xT_ready adj_psum qk_psum lin_psum relu_ready qk_ready lin_ready s_psum att_ready "
                 "ah_ready degree_psum degree_ready root_ready dis_ready lin_dis_ready y_psum y_ready y_bn y_aggr "
                 "y_var_ready y_rstd_ready yn_ready yg_ready off_ready x_ready x_bn x_aggr x_kept").split()
        s = {n: sem(n) for n in names}
        ln_act, ln_dve, norm_ready = outer_norm(nc, ctx, sem, c["x_stats"], c["rstd"], c["shift"], "a_ln")
        block = ctx.enter_context(nc.Block())

        def heads(t):
            return t.rearrange("p j (h e) -> p (j h) e", h=H)

        def per_head(t):
            return t.rearrange("p (g o) -> p g o", o=1).broadcast_to([P, J * H, HD])

        @block.sync
        def _(sp):
            for n, name in enumerate(("att_lin", "att_q", "att_k")):
                sp.dma_start(w[:, n, :], d[name]).then_inc(loaded, 16)
            sp.dma_start(row[:, :], d["att_b"]).then_inc(loaded, 16)
            for j in range(J):
                sp.dma_start(gain[:, j, :], d["att_g"]).then_inc(loaded, 16)
                sp.dma_start(offset[:, j, :], d["att_o"]).then_inc(loaded, 16)
            sp.wait_ge(parts_done, 5)
            for n in range(3):
                for j in range(J):
                    sp.dma_start(bias3[n:n + 1, j, :], row_parts[:, n, :]).then_inc(parts_moved, 16)

            def load(b, q):
                after(sp, s["adj_psum"], b - 1)
                sp.dma_start(adj[:, q, :, :], d["adj"][b].rearrange("(j p) m -> p j m", p=P)).then_inc(adj_loaded[q], 16)

            each(sp, load)

        @block.tensor
        def _(pe):
            pe.wait_ge(loaded, 16 * 8)
            pe.wait_ge(parts_moved, 16 * 3 * J)

            def front(b, q):
                pe.wait_ge(s["xn_ready"], b + 1)
                after(pe, s["lin_ready"], b)
                for j in range(J):
                    last = pe.transpose(p_xT[:, j * P:(j + 1) * P], xn[:, q, j, :], ident[:, :])
                last.then_inc(s["xT_psum"], 1)
                pe.wait_ge(adj_loaded[q], adj_count(b, q))
                after(pe, s["ah_ready"], b)
                for m in range(J):
                    for j in range(J):
                        last = pe.transpose(p_adj[:, m * N + j * P:m * N + (j + 1) * P],
                                            adj[:, q, j, m * P:(m + 1) * P], ident[:, :])
                last.then_inc(s["adj_psum"], 1)
                pe.wait_ge(s["xT_ready"], b + 1)
                for n in range(2):
                    last = pe.matmul(p_qk[:, n, :], w[:, 1 + n, :], xT[:, q, :], start=True, stop=True)
                last.then_inc(s["qk_psum"], 1)
                pe.matmul(p_xT[:, N:2 * N], c["ones3"][:, :], bias3[:, :, :], start=True, stop=False,
                          skip_group_check=True)
                for j in range(J):
                    last = pe.matmul(p_xT[:, N + j * D:N + (j + 1) * D], xT[:, q, j * P:(j + 1) * P], w[:, 0, :],
                                     start=False, stop=True, skip_group_check=True)
                last.then_inc(s["lin_psum"], 1)
                pe.wait_ge(s["qk_ready"], b + 1)
                after(pe, s["att_ready"], b)
                for j in range(J):
                    for h in range(H):
                        r = slice(h * HD, (h + 1) * HD)
                        last = pe.matmul(p_s[:, h, j * N:(j + 1) * N], qkT[r, q, 1, j * P:(j + 1) * P],
                                         qkT[r, q, 0, :], start=True, stop=True, tile_position=(h * HD, 0))
                last.then_inc(s["s_psum"], 1)

            def back(b, q):
                pe.wait_ge(s["ah_ready"], b + 1)
                after(pe, s["y_ready"], b)
                for j in range(J):
                    for h in range(H):
                        for m in range(J):
                            last = pe.matmul(p_y[:, N + j * H + h:N + j * H + h + 1],
                                             ah[:, q, h, m * N + j * P:m * N + (j + 1) * P], c["ones"][:, 0:1],
                                             start=m == 0, stop=m == J - 1, skip_group_check=True)
                last.then_inc(s["degree_psum"], 1)
                pe.wait_ge(s["lin_dis_ready"], b + 1)
                for j in range(J):
                    for h in range(H):
                        for m in range(J):
                            last = pe.matmul(p_y[:, j * D + h * HD:j * D + (h + 1) * HD],
                                             ah[:, q, h, m * N + j * P:m * N + (j + 1) * P],
                                             lin_dis[:, q, m, h * HD:(h + 1) * HD],
                                             start=m == 0, stop=m == J - 1, skip_group_check=True)
                last.then_inc(s["y_psum"], 1)

            skewed(pe, front, back)

        @block.scalar
        def _(act):
            ln_act(act)

            def front(b, q):
                act.wait_ge(s["xT_psum"], b + 1)
                act.activation(xT[:, q, :], p_xT[:, 0:N], ACT.Copy).then_inc(s["xT_ready"], 1)
                act.wait_ge(s["qk_psum"], b + 1)
                after(act, s["lin_ready"], b)
                act.activation(relu_qk[:, :, :], p_qk[:, :, :], ACT.Relu, scale=0.99).then_inc(s["relu_ready"], 1)
                act.wait_ge(s["lin_psum"], b + 1)
                act.activation(relu_x[:, :, :], p_xT[:, N:2 * N].rearrange("p (j d) -> p j d", j=J), ACT.Relu,
                               scale=0.99).then_inc(s["relu_ready"], 1)
                act.wait_ge(s["s_psum"], b + 1)
                act.activation(att[:, q, :, :], p_s[:, :, :], ACT.Sigmoid, scale=HD ** -0.5).then_inc(s["att_ready"], 1)

            def back(b, q):
                pass

            skewed(act, front, back)

        @block.vector
        def _(dve):
            ln_dve(dve)
            dve.wait_ge(loaded, 16 * 8)
            split_rows(dve, row[:, :], row_work[:, :], [row_parts[:, n, :] for n in range(3)], parts_done)

            def front(b, q):
                after(dve, s["xT_psum"], b)
                for j in range(J):
                    t = b * J + j
                    last = dve.tensor_scalar(xn[:, q, j, :], x[:, t, :], c["rstd"][:, bass.ds(t, 1)],
                                             c["shift"][:, bass.ds(t, 1)], ALU.mult, ALU.add)
                last.then_inc(s["xn_ready"], 1)
                dve.wait_ge(s["relu_ready"], b * 2 + 1)
                dve.scalar_tensor_tensor(qkT[:, q, :, :], p_qk[:, :, :], 0.01, relu_qk[:, :, :], ALU.mult, ALU.add)\
                   .then_inc(s["qk_ready"], 1)
                dve.wait_ge(s["relu_ready"], b * 2 + 2)
                dve.scalar_tensor_tensor(lin[:, q, :, :], p_xT[:, N:2 * N].rearrange("p (j d) -> p j d", j=J), 0.01,
                                         relu_x[:, :, :], ALU.mult, ALU.add).then_inc(s["lin_ready"], 1)

            def weigh(b, q):
                dve.wait_ge(s["att_ready"], b + 1)
                dve.wait_ge(s["adj_psum"], b + 1)
                dve.tensor_tensor(ah[:, q, :, :], att[:, q, :, :],
                                  p_adj[:, :].rearrange("p (o n) -> p o n", o=1).broadcast_to([P, H, J * N]), ALU.mult)\
                   .then_inc(s["ah_ready"], 1)

            def back(b, q):
                dve.wait_ge(s["degree_psum"], b + 1)
                after(dve, s["root_ready"], b)
                dve.tensor_scalar(degree[:, :], p_y[:, N:N + J * H], 1.2e-38, None, ALU.max)
                after(dve, s["dis_ready"], b)
                dve.tensor_scalar(linked[:, :], p_y[:, N:N + J * H], 0.0, None, ALU.is_gt).then_inc(s["degree_ready"], 1)
                dve.wait_ge(s["y_psum"], b + 1)
                dve.tensor_tensor(heads(y[:, :, :]), heads(p_y[:, 0:N].rearrange("p (j d) -> p j d", j=J)),
                                  per_head(dis[:, q, :]), ALU.mult).then_inc(s["y_ready"], 1)
                dve.wait_ge(norm_ready, 1)
                dve.wait_ge(s["y_ready"], b + 1)
                for j in range(J):
                    last = dve.bn_stats(y6[:, j, :], y[:, j, :])
                last.then_inc(s["y_bn"], 1)
                dve.wait_ge(norm_ready, 1)
                dve.wait_ge(s["y_bn"], b + 1)
                for j in range(J):
                    last = dve.bn_aggr(y_stats[:, j, :], y6[:, j, :])
                last.then_inc(s["y_aggr"], 1)
                dve.wait_ge(s["y_aggr"], b + 1)
                dve.tensor_scalar(y_var[:, :], y_stats[:, :, 1], LN_EPS, None, ALU.add).then_inc(s["y_var_ready"], 1)
                dve.wait_ge(s["y_rstd_ready"], b + 1)
                after(dve, s["yg_ready"], b)
                for j in range(J):
                    last = dve.tensor_scalar(yn[:, j, :], y[:, j, :], y_stats[:, j, 0:1], y_rstd[:, j:j + 1],
                                             ALU.subtract, ALU.mult)
                last.then_inc(s["yn_ready"], 1)

            def close(b, q):
                dve.wait_ge(s["yg_ready"], b + 1)
                dve.wait_ge(s["off_ready"], b + 1)
                dve.tensor_tensor(x[:, bass.ds(b * J, J), :], yg[:, :, :], x_off[:, :, :], ALU.add)\
                   .then_inc(s["x_ready"], 1)
                dve.wait_ge(norm_ready, 1)
                dve.wait_ge(s["x_ready"], b + 1)
                for j in range(J):
                    last = dve.bn_stats(bn6[:, j, :], x[:, b * J + j, :])
                last.then_inc(s["x_bn"], 1)
                dve.wait_ge(norm_ready, 1)
                dve.wait_ge(s["x_bn"], b + 1)
                for j in range(J):
                    last = dve.bn_aggr(mean_var[:, j, :], bn6[:, j, :])
                last.then_inc(s["x_aggr"], 1)
                dve.wait_ge(s["x_aggr"], b + 1)
                keep_stats(dve, c, b, mean_var[:, :, :]).then_inc(s["x_kept"], 1)

            def front_all(b, q):
                front(b, q)
                weigh(b, q)

            def back_all(b, q):
                back(b, q)
                close(b, q)

            skewed(dve, front_all, back_all)
            dve.wait_ge(s["x_kept"], B)

        @block.gpsimd
        def _(pool):
            pool.wait_ge(loaded, 16 * 8)

            def front(b, q):
                pass

            def back(b, q):
                after(pool, s["x_ready"], b)
                pool.tensor_tensor(x_off[:, :, :], x[:, bass.ds(b * J, J), :], offset[:, :, :], ALU.add)\
                    .then_inc(s["off_ready"], 1)
                pool.wait_ge(s["degree_ready"], b + 1)
                pool.tensor_tensor(root[:, :], degree[:, :], minus_half[:, 0:J * H], ALU.pow).then_inc(s["root_ready"], 1)
                pool.wait_ge(s["root_ready"], b + 1)
                pool.tensor_tensor(dis[:, q, :], root[:, :], linked[:, :], ALU.mult).then_inc(s["dis_ready"], 1)
                pool.wait_ge(s["dis_ready"], b + 1)
                pool.wait_ge(s["lin_ready"], b + 1)
                pool.tensor_tensor(heads(lin_dis[:, q, :, :]), heads(lin[:, q, :, :]), per_head(dis[:, q, :]), ALU.mult)\
                    .then_inc(s["lin_dis_ready"], 1)
                pool.wait_ge(s["y_var_ready"], b + 1)
                pool.tensor_tensor(y_rstd[:, :], y_var[:, :], minus_half[:, 0:J], ALU.pow).then_inc(s["y_rstd_ready"], 1)
                pool.wait_ge(s["yn_ready"], b + 1)
                pool.tensor_tensor(yg[:, :, :], yn[:, :, :], gain[:, :, :], ALU.mult).then_inc(s["yg_ready"], 1)

            skewed(pool, front, back)


def stage_expert_attention(nc, d, c, out):
    L = E * P
    ROUNDS = 3
    G = J * H
    PG = 2 * G
    MASKED = -1.0e30
    with ExitStack() as ctx:
        def sb(n, s, t=F32):
            return ctx.enter_context(nc.sbuf_tensor("e_" + n, s, t))

        def ps(n, s, t=F32):
            return ctx.enter_context(nc.psum_tensor("e_" + n, s, t))

        sem = ctx.enter_context(stage_semaphores(nc, "e_"))
        x, ident = c["x"], c["ident"]
        w_hl, b_hl = sb("w_hl", [P, D]), sb("b_hl", [P, 1])
        w_q, w_kv = sb("w_q", [P, E, D]), sb("w_kv", [P, 2, D])
        w_gate = sb("w_gate", [P, E, H * E])
        w_fc, b_fc1 = sb("w_fc", [P, 2, D]), sb("b_fc1", [P, 1])
        w_fgate = sb("w_fgate", [P, H])
        row, row_work = sb("row", [1, H * E + D]), sb("row_work", [1, H * E + D])
        row_parts, bias3 = sb("row_parts", [1, 3, H * E + D], BF16), sb("bias3", [3, H * E + D], BF16)
        norms = sb("norms", [P, 4, HD])
        ident16, below, above = (sb(n, [P, P], BF16) for n in ("ident16", "below", "above"))
        pick = sb("pick", [P, E, P], BF16)
        resid, residT = sb("resid", [P, J, D]), sb("residT", [P, N])

        xn, xT, sxT = sb("xn", [P, 2, J, D]), sb("xT", [P, N]), sb("sxT", [P, 2, N])
        qT, kT, v = sb("qT", [P, E, N]), sb("kT", [P, N]), sb("v", [P, J, D])
        top = sb("top", [P, J, H, E])
        top2 = sb("top2", [P, J, H, HD], BF16)
        topT = sb("topT", [P, J * P], BF16)
        wT = sb("wT", [P, ROUNDS, H, L])
        nonzero = sb("nonzero", [P, J, P])
        over, keep = sb("over", [P, J, E, P]), sb("keep", [P, J, E, P])
        outT = sb("outT", [P, J, E, P])
        g_top, g_low, g_exp, g_sum, g_over, g_w = (sb("g_top", [P, G]), sb("g_low", [P, G, E]), sb("g_exp", [P, G, E]),
                                                   sb("g_sum", [P, G]), sb("g_over", [P, G]), sb("g_w", [P, G, E]))
        prod = sb("prod", [P, J, E, D])
        mixed = sb("mixed", [P, J, D])
        u = sb("u", [P, 2, J, D])
        n_sum, n_mean, n_mid, n_sq, n_ss, n_var, n_rstd, n_unit, n_gain = (
            sb("n_sum", [P, PG]), sb("n_mean", [P, PG]), sb("n_mid", [P, PG, HD]), sb("n_sq", [P, PG, HD]),
            sb("n_ss", [P, PG]), sb("n_var", [P, PG]), sb("n_rstd", [P, PG]), sb("n_unit", [P, PG, HD]),
            sb("n_gain", [P, PG, HD]))
        fx, fout = sb("fx", [P, PG, HD]), sb("fout", [P, PG, HD])
        fxT, fc1, fc1n, foT = sb("fxT", [P, 2 * N]), sb("fc1", [P, 2 * N]), sb("fc1n", [P, 2 * N]), sb("foT", [P, 2 * N])
        fc2 = sb("fc2", [P, PG, HD])
        f_top, f_low, f_exp, f_sum, f_over, f_w = (sb("f_top", [P, 2 * J]), sb("f_low", [P, 2 * J, H]),
                                                   sb("f_exp", [P, 2 * J, H]), sb("f_sum", [P, 2 * J]),
                                                   sb("f_over", [P, 2 * J]), sb("f_w", [P, PG]))
        gated = sb("gated", [P, PG, HD])

        p_a = ps("p_a", [P, H, L])
        p_v = ps("p_v", [P, J, E * P])
        p_in = ps("p_in", [P, 512])
        p_kv = ps("p_kv", [P, 512])

        loaded, built, parts_done, parts_moved = sem("loaded"), sem("built"), sem("parts_done"), sem("parts_moved")
        zeroed, masks = sem("zeroed"), sem("masks")
        resid_in, resid_out, resid_ready = sem("resid_in"), sem("resid_out"), sem("resid_ready")
        names = ("xn_ready xT_psum xT_ready sx_psum sx_ready q_psum q_ready kv_psum kv_ready s_psum top_ready top2_half "
                 "top2_ready topT_psum topT_ready t_psum sums_psum values_psum over_ready "
                 "nonzero_ready keep_ready out_ready gate_psum tok_psum g_top g_low g_exp g_sum g_over g_w prod_ready "
                 "mixed_ready u_ready").split()
        s = {n: sem(n) for n in names}
        weighed = [[sem(f"weighed{q}{n}") for n in range(ROUNDS)] for q in range(2)]
        norm_names = "sum mean mid sq ss var rstd unit gain".split()
        ns = {n: sem("n_" + n + "_done") for n in norm_names}
        tail_names = ("fx_ready fxT_psum fxT_ready fc1_psum fc1_ready fc1n_ready fc2_psum fc2_kept u2_ready fout_ready "
                      "foT_psum foT_ready f_psum f_top f_low f_exp f_sum f_over f_w gated_ready x_ready").split()
        t = {n: sem(n) for n in tail_names}
        stored = sem("stored")
        ln_act, ln_dve, norm_ready = outer_norm(nc, ctx, sem, c["x_stats"], c["rstd"], c["shift"], "e_ln")
        block = ctx.enter_context(nc.Block())

        def spread(a, width):
            return a.rearrange("p (g o) -> p g o", o=1).broadcast_to([P, a.shape[1], width])

        def pairs(eng, front, attend, tail):
            with eng.Fori(1, B // 2 + 1) as k:
                for q in range(2):
                    front(k * 2 - 2 + q, q)
                    attend(k * 2 - 2 + q, q, k)
                tail(k - 1)

        @block.sync
        def _(sp):
            sp.wait_ge(zeroed, 4)
            sp.dma_start(w_hl[:, :], d["exp_hl"]).then_inc(loaded, 16)
            sp.dma_start(b_hl[:, :], d["exp_hl_b"]).then_inc(loaded, 16)
            sp.dma_start(b_fc1[:, :], d["exp_fc1_b"]).then_inc(loaded, 16)
            sp.dma_start(w_fgate[:, :], d["exp_fgate"]).then_inc(loaded, 16)
            sp.dma_start(row[:, :], d["exp_rows"]).then_inc(loaded, 16)
            sp.dma_start(norms[:, :, :], d["exp_norms"]).then_inc(loaded, 16)
            for h in range(H):
                r = slice(h * HD, (h + 1) * HD)
                sp.dma_start(w_q[r, :, r], d["exp_q"][h]).then_inc(loaded, 16)
                sp.dma_start(w_kv[r, :, r], d["exp_kv"][h]).then_inc(loaded, 16)
                sp.dma_start(w_gate[r, :, h * E:(h + 1) * E], d["exp_gate"][h]).then_inc(loaded, 16)
                sp.dma_start(w_fc[r, :, r], d["exp_fc"]).then_inc(loaded, 16)
            sp.wait_ge(parts_done, 5)
            for n in range(3):
                sp.dma_start(bias3[n:n + 1, :], row_parts[:, n, :]).then_inc(parts_moved, 16)
            with sp.Fori(0, B // 2) as i:
                sp.wait_ge(t["x_ready"], i + 1)
                sp.dma_start(out[bass.ds(i * 2, 2)].rearrange("b (j p) d -> p b j d", p=P),
                             x[:, bass.ds(i * 2 * J, 2 * J), :].rearrange("p (b j) d -> p b j d", j=J))\
                  .then_inc(stored, 16)
            sp.wait_ge(stored, 16 * (B // 2))

        LOADED = 16 * (6 + 4 * H)
        MASKS = 6 + 2 * H

        @block.tensor
        def _(pe):
            pe.wait_ge(loaded, LOADED)
            pe.wait_ge(parts_moved, 16 * 3)
            pe.wait_ge(masks, MASKS)
            pe.wait_ge(built, 1)

            for n in range(H):
                pe.wait_ge(resid_in, 3 * n + 1)
                for j in range(J):
                    last = pe.transpose(p_in[:, j * P:(j + 1) * P], xn[:, n % 2, j, :], ident[:, :])
                last.then_inc(resid_out, 1)
                pe.wait_ge(resid_in, 3 * n + 2)
                pe.matmul(p_in[:, N:2 * N], w_hl[:, :], xT[:, :], start=True, stop=True).then_inc(resid_out, 1)
            pe.wait_ge(resid_in, 3 * H)
            for j in range(J):
                last = pe.transpose(p_in[:, j * P:(j + 1) * P], residT[:, j * P:(j + 1) * P], ident[:, :])
            last.then_inc(resid_out, 1)
            pe.wait_ge(resid_ready, 1)

            def front(b, q):
                pe.wait_ge(s["xn_ready"], b + 1)
                for j in range(J):
                    last = pe.transpose(p_in[:, j * P:(j + 1) * P], xn[:, q, j, :], ident[:, :])
                last.then_inc(s["xT_psum"], 1)
                pe.wait_ge(s["xT_ready"], b + 1)
                pe.matmul(p_in[:, N:2 * N], w_hl[:, :], xT[:, :], start=True, stop=True).then_inc(s["sx_psum"], 1)
                pe.wait_ge(s["sx_ready"], b + 1)
                for e in range(E):
                    last = pe.matmul(p_a[:, e // 2, (e % 2) * N:(e % 2 + 1) * N], w_q[:, e, :], sxT[:, q, :],
                                     start=True, stop=True)
                last.then_inc(s["q_psum"], 1)
                pe.matmul(p_kv[:, 0:N], w_kv[:, 0, :], sxT[:, q, :], start=True, stop=True)
                for j in range(J):
                    last = pe.matmul(p_kv[:, N + j * D:N + (j + 1) * D], sxT[:, q, j * P:(j + 1) * P], w_kv[:, 1, :],
                                     start=True, stop=True)
                last.then_inc(s["kv_psum"], 1)
                pe.wait_ge(s["q_ready"], b + 1)
                pe.wait_ge(s["kv_ready"], b + 1)
                for n, (to, first, count) in enumerate(((0, 0, 4), (1, 0, 2), (1, 2, 2))):
                    if n:
                        pe.wait_ge(s["top_ready"], b * ROUNDS + n)
                    cols = P * (to + 1)
                    for e in range(count):
                        for h in range(H):
                            r = slice(h * HD, (h + 1) * HD)
                            pe.matmul(p_a[:, h, e * cols:(e + 1) * cols], qT[r, first + e, to * P:(to + 1) * P],
                                      kT[r, 0:cols], start=e == 0, stop=False, tile_position=(h * HD, 0),
                                      skip_group_check=True)
                    for h in range(H):
                        view = p_a[:, h, :].rearrange("p (e c) -> p e c", e=count)
                        last = pe.matmul(view[:, :, cols - P:cols], ident16[:, :],
                                         below[:, :].rearrange("p (o c) -> p o c", o=1).broadcast_to([P, count, P]),
                                         start=False, stop=True, skip_group_check=True)
                    last.then_inc(s["s_psum"], 1)
                pe.wait_ge(s["top2_ready"], b + 1)
                for j in range(J):
                    last = pe.transpose(p_in[:, j * (P // 2):(j + 1) * (P // 2)].bitcast(BF16),
                                        top2[:, j, :, :].rearrange("p h c -> p (h c)"), ident16[:, :])
                last.then_inc(s["topT_psum"], 1)

            def attend(b, q, k):
                pe.wait_ge(s["topT_ready"], b + 1)
                for n, (frm, to) in enumerate(((0, 0), (0, 1), (1, 1))):
                    diagonal = frm == to
                    if n:
                        pe.wait_ge(weighed[q][n - 1], k)
                    else:
                        pe.wait_ge(s["top_ready"], b * ROUNDS + ROUNDS)
                    if diagonal:
                        for h in range(H):
                            pe.matmul(p_a[:, h, :].rearrange("p (e c) -> p e c", e=E), ident16[:, :],
                                      above[:, :].rearrange("p (o c) -> p o c", o=1).broadcast_to([P, E, P]),
                                      start=True, stop=False, skip_group_check=True)
                    for e in range(E):
                        for h in range(H):
                            r = slice(h * HD, (h + 1) * HD)
                            pe.matmul(p_a[:, h, e * P:(e + 1) * P], pick[r, e, :], topT[r, to * P:(to + 1) * P],
                                      start=e == 0 and not diagonal, stop=False, tile_position=(h * HD, 0), skip_group_check=True)
                    for h in range(H):
                        r = slice(h * HD, (h + 1) * HD)
                        last = pe.matmul(p_a[:, h, :], kT[r, frm * P:(frm + 1) * P], qT[r, :, to * P:(to + 1) * P],
                                         start=False, stop=True, tile_position=(h * HD, 0), skip_group_check=True)
                    last.then_inc(s["t_psum"], 1)
                pe.wait_ge(weighed[q][ROUNDS - 1], k)
                for lhs, dst, done in ((None, p_a, s["sums_psum"]), (v, p_v, s["values_psum"])):
                    for to, rounds in ((0, (0,)), (1, (1, 2))):
                        for n in rounds:
                            for h in range(H):
                                cols = slice(h * HD, (h + 1) * HD)
                                stat = c["ones"][:, 0:HD] if lhs is None else v[:, n // 2, cols]
                                last = pe.matmul(dst[cols, to, :], stat, wT[:, n, h, :], start=n == rounds[0],
                                                 stop=n == rounds[-1], tile_position=(0, h * HD), skip_group_check=True)
                    last.then_inc(done, 1)
                pe.wait_ge(s["out_ready"], b + 1)
                for j in range(J):
                    part = p_in[:, j * H * E:(j + 1) * H * E]
                    pe.matmul(part, c["ones3"][:, :], bias3[:, 0:H * E], start=True, stop=False, skip_group_check=True)
                    for e in range(E):
                        last = pe.matmul(part, outT[:, j, e, :], w_gate[:, e, :], start=False, stop=e == E - 1,
                                         skip_group_check=True)
                last.then_inc(s["gate_psum"], 1)
                for j in range(J):
                    for e in range(E):
                        last = pe.transpose(p_a[:, 2 + j, e * P:(e + 1) * P], outT[:, j, e, :], ident[:, :])
                last.then_inc(s["tok_psum"], 1)
                pe.wait_ge(s["g_low"], b + 1)
                pe.wait_ge(s["prod_ready"], b * J + J)

            def tail(i):
                pe.wait_ge(t["fx_ready"], i + 1)
                for a in range(2 * J):
                    last = pe.transpose(p_in[:, a * P:(a + 1) * P], fx[:, a * H:(a + 1) * H, :].rearrange("p h c -> p (h c)"),
                                        ident[:, :])
                last.then_inc(t["fxT_psum"], 1)
                pe.wait_ge(t["fxT_ready"], i + 1)
                pe.matmul(p_kv[:, :], w_fc[:, 0, :], fxT[:, :], start=True, stop=True).then_inc(t["fc1_psum"], 1)
                pe.wait_ge(t["fc1n_ready"], i + 1)
                for a in range(2 * J):
                    part = p_kv[:, a * D:(a + 1) * D]
                    pe.matmul(part, c["ones3"][:, :], bias3[:, H * E:], start=True, stop=False, skip_group_check=True)
                    last = pe.matmul(part, fc1n[:, a * P:(a + 1) * P], w_fc[:, 1, :], start=False, stop=True,
                                     skip_group_check=True)
                last.then_inc(t["fc2_psum"], 1)
                pe.wait_ge(t["fout_ready"], i + 1)
                for a in range(2 * J):
                    last = pe.transpose(p_in[:, a * P:(a + 1) * P],
                                        fout[:, a * H:(a + 1) * H, :].rearrange("p h c -> p (h c)"), ident[:, :])
                last.then_inc(t["foT_psum"], 1)
                pe.wait_ge(t["foT_ready"], i + 1)
                for a in range(2 * J):
                    last = pe.matmul(p_kv[:, a * H:(a + 1) * H], foT[:, a * P:(a + 1) * P], w_fgate[:, :], start=True,
                                     stop=True)
                last.then_inc(t["f_psum"], 1)
                pe.wait_ge(t["f_low"], i + 1)

            pairs(pe, front, attend, tail)

        @block.scalar
        def _(act):
            ln_act(act)
            act.wait_ge(loaded, LOADED)
            for n in range(H):
                r = slice(n * HD, (n + 1) * HD)
                act.wait_ge(resid_out, 2 * n + 1)
                act.activation(xT[:, :], p_in[:, 0:N], ACT.Copy).then_inc(resid_in, 1)
                act.wait_ge(resid_out, 2 * n + 2)
                act.activation(residT[r, :], p_in[r, N:2 * N], ACT.Identity, bias=b_hl[r, :]).then_inc(resid_in, 1)
            act.wait_ge(resid_out, 2 * H + 1)
            act.activation(resid[:, :, :].rearrange("p j d -> p (j d)"), p_in[:, 0:N], ACT.Copy).then_inc(resid_ready, 1)

            def front(b, q):
                act.wait_ge(s["xT_psum"], b + 1)
                act.activation(xT[:, :], p_in[:, 0:N], ACT.Copy).then_inc(s["xT_ready"], 1)
                act.wait_ge(s["sx_psum"], b + 1)
                act.activation(sxT[:, q, :], p_in[:, N:2 * N], ACT.Identity, bias=b_hl[:, 0:1]).then_inc(s["sx_ready"], 1)
                act.wait_ge(s["q_psum"], b + 1)
                act.activation(qT[:, :, :].rearrange("p e n -> p (e n)"), p_a[:, 0:2, :].rearrange("p a n -> p (a n)"), ACT.Copy)\
                   .then_inc(s["q_ready"], 1)
                act.wait_ge(s["kv_psum"], b + 1)
                act.activation(kT[:, :], p_kv[:, 0:N], ACT.Copy)
                act.activation(v[:, :, :].rearrange("p j d -> p (j d)"), p_kv[:, N:2 * N], ACT.Copy).then_inc(s["kv_ready"], 1)
                act.wait_ge(s["topT_psum"], b + 1)
                act.activation(topT[:, :], p_in[:, 0:P].bitcast(BF16), ACT.Copy).then_inc(s["topT_ready"], 1)

            def attend(b, q, k):
                for n in range(ROUNDS):
                    act.wait_ge(s["t_psum"], b * ROUNDS + n + 1)
                    act.activation(wT[:, n, :, :], p_a[:, :, :], ACT.Exp, scale=HD ** 0.5).then_inc(weighed[q][n], 1)
                act.wait_ge(s["g_low"], b + 1)
                act.activation(g_exp[:, :, :], g_low[:, :, :], ACT.Exp).then_inc(s["g_exp"], 1)

            def square(i, n):
                act.wait_ge(ns["mid"], i * 2 + n)
                act.activation(n_sq[:, :, :], n_mid[:, :, :], ACT.Square).then_inc(ns["sq"], 1)

            def tail(i):
                square(i, 1)
                act.wait_ge(t["fxT_psum"], i + 1)
                act.activation(fxT[:, :], p_in[:, :], ACT.Copy).then_inc(t["fxT_ready"], 1)
                act.wait_ge(t["fc1_psum"], i + 1)
                act.activation(fc1[:, :], p_kv[:, :], ACT.Relu, bias=b_fc1[:, 0:1]).then_inc(t["fc1_ready"], 1)
                square(i, 2)
                act.wait_ge(t["foT_psum"], i + 1)
                act.activation(foT[:, :], p_in[:, :], ACT.Copy).then_inc(t["foT_ready"], 1)
                act.wait_ge(t["f_low"], i + 1)
                act.activation(f_exp[:, :, :], f_low[:, :, :], ACT.Exp).then_inc(t["f_exp"], 1)

            pairs(act, front, attend, tail)

        @block.vector
        def _(dve):
            ln_dve(dve)
            dve.wait_ge(loaded, LOADED)
            split_rows(dve, row[:, :], row_work[:, :], [row_parts[:, n, :] for n in range(3)], parts_done)
            dve.wait_ge(norm_ready, 1)
            dve.wait_ge(masks, MASKS)
            dve.tensor_copy(ident16[:, :], ident[:, :]).then_inc(built, 1)

            def normalise(q, b):
                for j in range(J):
                    a = b * J + j
                    last = dve.tensor_scalar(xn[:, q, j, :], x[:, a, :], c["rstd"][:, bass.ds(a, 1)],
                                             c["shift"][:, bass.ds(a, 1)], ALU.mult, ALU.add)
                return last

            for n in range(H):
                if n >= 2:
                    dve.wait_ge(resid_out, 2 * (n - 2) + 1)
                if n:
                    dve.wait_ge(resid_in, 3 * n)
                normalise(n % 2, n).then_inc(resid_in, 1)
            dve.wait_ge(resid_ready, 1)

            def front(b, q):
                normalise(q, b).then_inc(s["xn_ready"], 1)
                for n, (to, first, count) in enumerate(((0, 0, 4), (1, 0, 2), (1, 2, 2))):
                    dve.wait_ge(s["s_psum"], b * ROUNDS + n + 1)
                    dve.tensor_reduce(top[:, to, :, first:first + count],
                                      p_a[:, :, :].rearrange("p h (e c) -> p h e c", e=count), AX.X, ALU.max)\
                       .then_inc(s["top_ready"], 1)
                dve.wait_ge(s["top_ready"], b * ROUNDS + ROUNDS)
                high, low = [top2[:, :, :, n:2 * E:2].rearrange("p j h e -> p (j h) e") for n in range(2)]
                all_top = top[:, :, :, :].rearrange("p j h e -> p (j h) e")
                dve.tensor_copy(high, all_top).then_inc(s["top2_half"], 1)
                dve.wait_ge(s["top2_half"], b + 1)
                dve.tensor_tensor(low, all_top, high, ALU.subtract).then_inc(s["top2_ready"], 1)

            def attend(b, q, k):
                dve.wait_ge(s["sx_ready"], b + 1)
                dve.tensor_scalar(nonzero[:, :, :].rearrange("p j c -> p (j c)"), sxT[:, q, :], 0.0, None, ALU.not_equal)\
                   .then_inc(s["nonzero_ready"], 1)
                dve.wait_ge(s["sums_psum"], b + 1)
                dve.reciprocal(over[:, :, :, :].rearrange("p j e c -> p j (e c)"), p_a[:, 0:J, :]).then_inc(s["over_ready"], 1)
                dve.wait_ge(s["values_psum"], b + 1)
                dve.wait_ge(s["keep_ready"], b * J + J)
                dve.tensor_tensor(outT[:, :, :, :].rearrange("p j e c -> p j (e c)"), p_v[:, :, :],
                                  keep[:, :, :, :].rearrange("p j e c -> p j (e c)"), ALU.mult).then_inc(s["out_ready"], 1)
                gate = p_in[:, 0:G * E].rearrange("p (g e) -> p g e", e=E)
                dve.wait_ge(s["gate_psum"], b + 1)
                dve.tensor_reduce(g_top[:, :], gate, AX.X, ALU.max).then_inc(s["g_top"], 1)
                dve.wait_ge(s["g_top"], b + 1)
                dve.tensor_tensor(g_low[:, :, :], gate, spread(g_top[:, :], E), ALU.subtract).then_inc(s["g_low"], 1)
                dve.wait_ge(s["g_exp"], b + 1)
                dve.tensor_reduce(g_sum[:, :], g_exp[:, :, :], AX.X, ALU.add).then_inc(s["g_sum"], 1)
                dve.wait_ge(s["g_sum"], b + 1)
                dve.reciprocal(g_over[:, :], g_sum[:, :]).then_inc(s["g_over"], 1)
                dve.wait_ge(s["g_over"], b + 1)
                dve.tensor_tensor(g_w[:, :, :], g_exp[:, :, :], spread(g_over[:, :], E), ALU.mult).then_inc(s["g_w"], 1)
                dve.wait_ge(s["tok_psum"], b + 1)
                dve.wait_ge(s["g_w"], b + 1)
                for j in range(J):
                    for e in range(E):
                        last = dve.tensor_tensor(prod[:, j, e, :].rearrange("p (h c) -> p h c", h=H),
                                                 p_a[:, 2 + j, e * P:(e + 1) * P].rearrange("p (h c) -> p h c", h=H),
                                                 g_w[:, j * H:(j + 1) * H, e:e + 1].broadcast_to([P, H, HD]), ALU.mult)
                    last.then_inc(s["prod_ready"], 1)
                dve.wait_ge(s["prod_ready"], b * J + J)
                dve.tensor_reduce(mixed[:, :, :], prod[:, :, :, :].rearrange("p j e c -> p j c e"), AX.X, ALU.add)\
                   .then_inc(s["mixed_ready"], 1)
                dve.wait_ge(s["mixed_ready"], b + 1)
                dve.tensor_tensor(u[:, q, :, :], mixed[:, :, :], resid[:, :, :], ALU.add).then_inc(s["u_ready"], 1)

            def norm(i, n, src, ready, count):
                k = i * 2 + n
                dve.wait_ge(ready, count)
                dve.tensor_reduce(n_sum[:, :], src, AX.X, ALU.add).then_inc(ns["sum"], 1)
                dve.wait_ge(ns["sum"], k)
                dve.tensor_scalar(n_mean[:, :], n_sum[:, :], 1.0 / HD, None, ALU.mult).then_inc(ns["mean"], 1)
                dve.wait_ge(ns["mean"], k)
                dve.tensor_tensor(n_mid[:, :, :], src, spread(n_mean[:, :], HD), ALU.subtract).then_inc(ns["mid"], 1)
                dve.wait_ge(ns["sq"], k)
                dve.tensor_reduce(n_ss[:, :], n_sq[:, :, :], AX.X, ALU.add).then_inc(ns["ss"], 1)
                dve.wait_ge(ns["ss"], k)
                dve.tensor_scalar(n_var[:, :], n_ss[:, :], 1.0 / HD, NORM_EPS, ALU.mult, ALU.add).then_inc(ns["var"], 1)
                dve.wait_ge(ns["rstd"], k)
                dve.tensor_tensor(n_unit[:, :, :], n_mid[:, :, :], spread(n_rstd[:, :], HD), ALU.mult).then_inc(ns["unit"], 1)

            def tail(i):
                groups = u[:, :, :, :].rearrange("p q j (h c) -> p (q j h) c", h=H)
                norm(i, 1, groups, s["u_ready"], i * 2 + 2)
                dve.wait_ge(t["fc1_ready"], i + 1)
                dve.scalar_tensor_tensor(fc1n[:, :], fxT[:, :], 0.0, fc1[:, :], ALU.not_equal, ALU.mult)\
                   .then_inc(t["fc1n_ready"], 1)
                dve.wait_ge(t["fc2_psum"], i + 1)
                flat = "p g c -> p (g c)"
                dve.scalar_tensor_tensor(fc2[:, :, :].rearrange(flat), fx[:, :, :].rearrange(flat), 0.0, p_kv[:, :],
                                         ALU.not_equal, ALU.mult).then_inc(t["fc2_kept"], 1)
                dve.wait_ge(t["fc2_kept"], i + 1)
                dve.tensor_tensor(groups, fc2[:, :, :], fx[:, :, :], ALU.add).then_inc(t["u2_ready"], 1)
                norm(i, 2, groups, t["u2_ready"], i + 1)
                logits = p_kv[:, 0:2 * J * H].rearrange("p (a h) -> p a h", h=H)
                dve.wait_ge(t["f_psum"], i + 1)
                dve.tensor_reduce(f_top[:, :], logits, AX.X, ALU.max).then_inc(t["f_top"], 1)
                dve.wait_ge(t["f_top"], i + 1)
                dve.tensor_tensor(f_low[:, :, :], logits, spread(f_top[:, :], H), ALU.subtract).then_inc(t["f_low"], 1)
                dve.wait_ge(t["f_exp"], i + 1)
                dve.tensor_reduce(f_sum[:, :], f_exp[:, :, :], AX.X, ALU.add).then_inc(t["f_sum"], 1)
                dve.wait_ge(t["f_sum"], i + 1)
                dve.reciprocal(f_over[:, :], f_sum[:, :]).then_inc(t["f_over"], 1)
                dve.wait_ge(t["f_over"], i + 1)
                dve.tensor_tensor(f_w[:, :].rearrange("p (a h) -> p a h", h=H), f_exp[:, :, :], spread(f_over[:, :], H),
                                  ALU.mult).then_inc(t["f_w"], 1)
                dve.wait_ge(t["f_w"], i + 1)
                dve.tensor_tensor(gated[:, :, :], fout[:, :, :], spread(f_w[:, :], HD), ALU.mult).then_inc(t["gated_ready"], 1)
                dve.wait_ge(t["x_ready"], i + 1)

            pairs(dve, front, attend, tail)

        @block.gpsimd
        def _(pool):
            for a in (w_q, w_kv, w_gate, w_fc):
                pool.memset(a[:, :, :], 0.0).then_inc(zeroed, 1)
            pool.memset(below[:, :], 0.0).then_inc(masks, 1)
            pool.memset(above[:, :], 0.0).then_inc(masks, 1)
            pool.memset(top2[:, :, :, :], 0.0).then_inc(masks, 1)
            pool.memset(pick[:, :, :], 0.0).then_inc(masks, 1)
            pool.wait_ge(masks, 4)
            pool.affine_select(out=below[:, :], in_=below[:, :], compare_op=ALU.is_ge, fill=MASKED, base=0,
                               pattern=[[-1, P]], channel_multiplier=1).then_inc(masks, 1)
            pool.affine_select(out=above[:, :], in_=above[:, :], compare_op=ALU.is_ge, fill=MASKED, base=0,
                               pattern=[[1, P]], channel_multiplier=-1).then_inc(masks, 1)
            for k in range(2 * H):
                h, n = divmod(k, 2)
                pool.wait_ge(masks, 6 + k)
                pool.affine_select(out=pick[:, :, :], in_=pick[:, :, :], compare_op=ALU.not_equal, fill=-1.0,
                                   base=-n - h * HD, pattern=[[-2, E], [0, P]], channel_multiplier=1).then_inc(masks, 1)
            pool.wait_ge(resid_ready, 1)
            pool.wait_ge(loaded, LOADED)

            def front(b, q):
                pass

            def attend(b, q, k):
                pool.wait_ge(s["nonzero_ready"], b + 1)
                pool.wait_ge(s["over_ready"], b + 1)
                for j in range(J):
                    pool.tensor_tensor(keep[:, j, :, :], over[:, j, :, :],
                                       nonzero[:, j:j + 1, :].broadcast_to([P, E, P]), ALU.mult).then_inc(s["keep_ready"], 1)

            def close_norm(i, n, dst, done):
                k = i * 2 + n
                pool.wait_ge(ns["var"], k)
                pool.tensor_tensor(n_rstd[:, :], n_var[:, :], c["minus_half"][:, 0:PG], ALU.pow).then_inc(ns["rstd"], 1)
                pool.wait_ge(ns["unit"], k)
                gain = norms[:, 2 * n - 2:2 * n - 1, :].broadcast_to([P, PG, HD])
                offset = norms[:, 2 * n - 1:2 * n, :].broadcast_to([P, PG, HD])
                pool.tensor_tensor(n_gain[:, :, :], n_unit[:, :, :], gain, ALU.mult).then_inc(ns["gain"], 1)
                pool.wait_ge(ns["gain"], k)
                pool.tensor_tensor(dst, n_gain[:, :, :], offset, ALU.add).then_inc(done, 1)

            def tail(i):
                close_norm(i, 1, fx[:, :, :], t["fx_ready"])
                close_norm(i, 2, fout[:, :, :], t["fout_ready"])
                pool.wait_ge(t["gated_ready"], i + 1)
                xi = x[:, bass.ds(i * 2 * J, 2 * J), :]
                pool.tensor_tensor(xi, xi, gated[:, :, :].rearrange("p (a h) c -> p a (h c)", h=H), ALU.add)\
                    .then_inc(t["x_ready"], 1)

            pairs(pool, front, attend, tail)


STAGES = [stage_gated_conv, stage_recurrent, stage_graph_attention]
LAST = stage_expert_attention


def more(inputs, row, col, wide):
    import numpy as _np

    return {
        "ffn_w": inputs["L0_ffn_W"].T, "ffn_b": row("L0_ffn_b"),
        "ffn_ln_w": col("L0_ffn_ln_w"), "ffn_ln_b": col("L0_ffn_ln_b"),
        "att_lin": inputs["L1_gnn_W_lin"], "att_q": inputs["L1_gnn_W_q"], "att_k": inputs["L1_gnn_W_k"],
        "att_b": row("L1_gnn_b_lin"), "att_g": wide("L1_gnn_ln_g"), "att_o": wide("L1_gnn_ln_b"),
        "exp_hl": inputs["L1_ffn_hl_w"].reshape(D, D).T, "exp_hl_b": col("L1_ffn_hl_b"),
        "exp_q": inputs["L1_ffn_wq"].transpose(0, 3, 1, 2),
        "exp_kv": _np.stack([inputs["L1_ffn_wk"], inputs["L1_ffn_wv"]]).transpose(1, 3, 0, 2),
        "exp_gate": inputs["L1_ffn_gate_w"].reshape(H, E, E, HD).transpose(0, 3, 2, 1),
        "exp_rows": _np.concatenate([row("L1_ffn_gate_b")] + [row("L1_ffn_fc2_b")] * H, axis=1),
        "exp_norms": _np.broadcast_to(_np.stack([inputs[f"L1_ffn_{n}"] for n in ("ln_g", "ln_b", "fnorm_g", "fnorm_b")]),
                                      (P, 4, HD)),
        "exp_fc": _np.stack([inputs["L1_ffn_fc1_w"], inputs["L1_ffn_fc2_w"]]).transpose(2, 0, 1),
        "exp_fc1_b": _np.concatenate([col("L1_ffn_fc1_b")] * H),
        "exp_fgate": inputs["L1_ffn_fgate_w"].T,
    }


def program(nc, d, out):
    with ExitStack() as ctx:
        def sb(n, s, t=F32):
            return ctx.enter_context(nc.sbuf_tensor(n, s, t))

        c = {
            "x": sb("x", [P, TILES, D]), "ident": sb("ident", [P, P]), "ones": sb("ones", [P, P]),
            "ones3": sb("ones3", [3, P], BF16), "minus_half": sb("minus_half", [P, 16]),
            "x_stats": sb("x_stats", [P, TILES, 2]), "rstd": sb("rstd", [P, TILES]), "shift": sb("shift", [P, TILES]),
        }
        stage_setup(nc, d, c)
        for stage in STAGES:
            stage(nc, d, c)
        LAST(nc, d, c, out)


def kernel(**inputs):
    import numpy as _np
    import concourse.bacc as _bacc
    from concourse import mybir as _mybir
    from concourse.bass_utils import run_bass_kernel_spmd as _run

    def row(name):
        return inputs[name].reshape(1, -1)

    def col(name):
        return inputs[name].reshape(-1, 1)

    def wide(name):
        return _np.broadcast_to(inputs[name].reshape(1, -1), (P, inputs[name].size))

    data = {
        "x": inputs["x"], "adj": inputs["adj"],
        "conv1": inputs["L0_gnn_conv1_w"][:, :, 0].T, "conv2": inputs["L0_gnn_conv2_w"].transpose(1, 2, 0),
        "wmsg": inputs["L0_gnn_w_msg"].T, "wih": inputs["L0_gnn_w_ih"].T, "whh": inputs["L0_gnn_w_hh"].T,
        "wse": inputs["L0_gnn_w_se"].T, "bse": col("L0_gnn_b_se"),
        "bih": row("L0_gnn_b_ih"), "bhh": row("L0_gnn_b_hh"), "bmsg": row("L0_gnn_b_msg"),
    }
    for n in ("bn1", "bn2"):
        for v in "gbmv":
            data[f"{n}_{v}"] = col(f"L0_gnn_{n}_{v}")
    data |= more(inputs, row, col, wide)
    nc = _bacc.Bacc("TRN2", target_bir_lowering=False, num_devices=1)
    arrays, d = {}, {}
    for name, a in data.items():
        a = _np.ascontiguousarray(a)
        arrays[f"in_{name}"] = a
        d[name] = nc.dram_tensor(f"in_{name}", a.shape, _mybir.dt.from_np(a.dtype), kind="ExternalInput").ap()
    out = nc.dram_tensor("out_0", (B, N, D), F32, kind="ExternalOutput").ap()
    program(nc, d, out)
    return _run(nc, [arrays], core_ids=[0]).results[0]["out_0"]
```

```python
from contextlib import ExitStack, contextmanager

import concourse.bass as bass
from concourse import mybir

ALU = mybir.AluOpType
ACT = mybir.ActivationFunctionType
AX = mybir.AxisListType
F32 = mybir.dt.float32
BF16 = mybir.dt.bfloat16
F32R = mybir.dt.float32r

P = 128
B = 32
N = 256
D = 128
J = N // P
TILES = B * J
TAPS = 17
PAD = TAPS // 2
SE = 3
STEPS = 30
H = 4
HD = D // H
E = 4
LN_EPS = 1e-5
NORM_EPS = 1e-8


@contextmanager
def stage_semaphores(nc, prefix):
    made = []

    def sem(name):
        made.append(nc.alloc_semaphore(name=prefix + name))
        return made[-1]

    yield sem
    nc.clear_and_free_semaphores(made)
    nc.all_engine_barrier()


def outer_norm(nc, ctx, sem, x_stats, rstd, shift, name):
    std = ctx.enter_context(nc.sbuf_tensor(f"{name}_std", [P, TILES], F32))
    eps = ctx.enter_context(nc.sbuf_tensor(f"{name}_eps", [P, 1], F32))
    eps_set, std_done, rstd_done, norm_ready = (
        sem(f"ln_{n}") for n in ("eps_set", "std_done", "rstd_done", "ready"))

    def on_scalar(act):
        act.wait_ge(eps_set, 1)
        act.activation(std[:, :], x_stats[:, :, 1], ACT.Sqrt, bias=eps[:, 0:1]).then_inc(std_done, 1)

    def on_vector(dve):
        dve.memset(eps[:, :], LN_EPS).then_inc(eps_set, 1)
        dve.wait_ge(std_done, 1)
        dve.reciprocal(rstd[:, :], std[:, :]).then_inc(rstd_done, 1)
        dve.wait_ge(rstd_done, 1)
        dve.scalar_tensor_tensor(shift[:, :], x_stats[:, :, 0], -1.0, rstd[:, :], ALU.mult, ALU.mult)\
           .then_inc(norm_ready, 1)

    return on_scalar, on_vector, norm_ready


def after(eng, sem, count):
    if not (isinstance(count, int) and count < 1):
        eng.wait_ge(sem, count)


def keep_stats(dve, c, b, mean_var):
    return dve.tensor_scalar(c["x_stats"][:, bass.ds(b * J, J), :], mean_var, 1.0, None, ALU.mult)


def stage_setup(nc, d, c):
    CHUNKS = 4
    PER = B // CHUNKS
    with ExitStack() as ctx:
        def sb(n, s, t=F32):
            return ctx.enter_context(nc.sbuf_tensor(n, s, t))

        sem = ctx.enter_context(stage_semaphores(nc, "setup_"))
        x_loaded = [sem(f"x_loaded{k}") for k in range(CHUNKS)]
        ident_zeroed, ident_done, ones_done = sem("ident_zeroed"), sem("ident_done"), sem("ones_done")
        stats_half, stats_done = sem("stats_half"), sem("stats_done")
        stats_kept = sem("stats_kept")
        bn6, mean_var = sb("setup_bn6", [P, J, 6]), sb("setup_mean_var", [P, J, 2])
        block = ctx.enter_context(nc.Block())

        @block.sync
        def _(sp):
            for k in range(CHUNKS):
                sp.dma_start(c["x"][:, k * PER * J:(k + 1) * PER * J, :].rearrange("p (b j) d -> p b j d", j=J),
                             d["x"][k * PER:(k + 1) * PER].rearrange("b (j p) d -> p b j d", p=P))\
                  .then_inc(x_loaded[k], 16)

        @block.gpsimd
        def _(pool):
            pool.memset(c["ident"][:, :], 0.0).then_inc(ident_zeroed, 1)
            pool.wait_ge(ident_zeroed, 1)
            pool.affine_select(out=c["ident"][:, :], in_=c["ident"][:, :], compare_op=ALU.not_equal, fill=1.0,
                               base=0, pattern=[[-1, P]], channel_multiplier=1).then_inc(ident_done, 1)
            pool.wait_ge(ident_done, 1)

        @block.vector
        def _(dve):
            dve.memset(c["ones"][:, :], 1.0).then_inc(ones_done, 1)
            dve.memset(c["ones3"][:, :], 1.0).then_inc(ones_done, 1)
            dve.memset(c["minus_half"][:, :], -0.5).then_inc(ones_done, 1)
            dve.wait_ge(ones_done, 3)
            dve.sem_inc(stats_kept, 1)
            for k in range(CHUNKS):
                dve.wait_ge(x_loaded[k], 16)
                with dve.Fori(k * PER + 1, (k + 1) * PER + 1) as n:
                    b = n - 1
                    dve.wait_ge(ones_done, 3)
                    dve.wait_ge(stats_kept, n)
                    for j in range(J):
                        last = dve.bn_stats(bn6[:, j, :], c["x"][:, b * J + j, :])
                    last.then_inc(stats_half, 1)
                    dve.wait_ge(ones_done, 3)
                    dve.wait_ge(stats_half, n)
                    for j in range(J):
                        last = dve.bn_aggr(mean_var[:, j, :], bn6[:, j, :])
                    last.then_inc(stats_done, 1)
                    dve.wait_ge(stats_done, n)
                    keep_stats(dve, c, b, mean_var[:, :, :]).then_inc(stats_kept, 1)
            dve.wait_ge(stats_kept, B + 1)


def split_rows(dve, row, work, parts, done):
    dve.tensor_copy(parts[0], row).then_inc(done, 1)
    dve.wait_ge(done, 1)
    dve.tensor_tensor(work, row, parts[0], ALU.subtract).then_inc(done, 1)
    dve.wait_ge(done, 2)
    dve.tensor_copy(parts[1], work).then_inc(done, 1)
    dve.wait_ge(done, 3)
    dve.tensor_tensor(work, work, parts[1], ALU.subtract).then_inc(done, 1)
    dve.wait_ge(done, 4)
    dve.tensor_copy(parts[2], work).then_inc(done, 1)


def each(eng, batch):
    batch(0, 0)
    batch(1, 1)
    with eng.Fori(1, B // 2) as i:
        for q in range(2):
            batch(i * 2 + q, q)


def adj_count(b, q):
    return 16 * (b // 2 + 1) if isinstance(b, int) else (b - q) * 8 + 16


def stage_gated_conv(nc, d, c):
    G = 4 * D
    with ExitStack() as ctx:
        def sb(n, s, t=F32):
            return ctx.enter_context(nc.sbuf_tensor("g_" + n, s, t))

        def ps(n, s):
            return ctx.enter_context(nc.psum_tensor("g_" + n, s, F32))

        sem = ctx.enter_context(stage_semaphores(nc, "g_"))
        x, ident = c["x"], c["ident"]
        w1, w2 = sb("w1", [P, D]), sb("w2", [P, TAPS, D])
        wmsg, wih, whh, wse = sb("wmsg", [P, D]), sb("wih", [P, 2, 3 * D]), sb("whh", [P, 3 * D]), sb("wse", [P, SE])
        bse = sb("bse", [SE, 1])
        bn = sb("bn", [P, 2, 4])
        bn_work = sb("bn_work", [P, 2, 2])
        bn_scale, bn_shift = sb("bn_scale", [P, 2, 1]), sb("bn_shift", [P, 2, 1])
        eps = sb("eps", [P, 1])
        row = sb("row", [1, G + D])
        hidden_row = sb("hidden_row", [1, 3 * D])
        row_work = sb("row_work", [1, G + D])
        row_parts = sb("row_parts", [1, 3, G + D], BF16)
        bias3 = sb("bias3", [3, G + D], BF16)
        mhalf3, neg3 = sb("mhalf3", [SE, P]), sb("neg3", [SE, 1])

        xn = sb("xn", [P, 2, J, D])
        xT = sb("xT", [P, 2, N])
        h1 = sb("h1", [P, 2, N + 2 * PAD])
        sT, s2T = sb("sT", [SE, 2, N]), sb("s2T", [SE, 2, N])
        nsq = sb("nsq", [P, 2, J])
        msg = sb("msg", [P, 2, J, D])
        adj = sb("adj", [P, 2, J, N])
        expo = sb("expo", [P, 2, J, N])
        aT = sb("aT", [P, 2, J, N])
        pre = sb("pre", [P, 2, N])
        convT = sb("convT", [P, 2, N])
        nmpT = sb("nmpT", [P, 2, N])
        rz = sb("rz", [P, 2, J, 2 * D])
        cand, cand2, nn = sb("cand", [P, 2, J, D]), sb("cand2", [P, 2, J, D]), sb("nn", [P, 2, J, D])
        diff, mix, upd = sb("diff", [P, 2, J, D]), sb("mix", [P, 2, J, D]), sb("upd", [P, 2, J, D])
        bn6, mean_var = sb("bn6", [P, 2, J, 6]), sb("mean_var", [P, J, 2])

        p_xT = ps("p_xT", [P, 512])
        p_h1 = ps("p_h1", [P, 512])
        p_adj = ps("p_adj", [P, 512])
        p_dist = ps("p_dist", [P, 512])
        p_conv = ps("p_conv", [P, 512])
        p_nmp = ps("p_nmp", [P, 512])
        p_gate = ps("p_gate", [P, J, 512])

        small_loaded, hidden_loaded, w_loaded = sem("small_loaded"), sem("hidden_loaded"), sem("w_loaded")
        parts_done, parts_moved, row_ready = sem("parts_done"), sem("parts_moved"), sem("row_ready")
        eps_set, bn_std, bn_ready, bn_steps, consts_set = (sem("eps_set"), sem("bn_std"), sem("bn_ready"),
                                                           sem("bn_steps"), sem("consts_set"))
        adj_loaded = [sem("adj_loaded0"), sem("adj_loaded1")]
        names = ("xn_ready xT_psum xT_ready h1_psum h1_ready sT_psum sT_ready nsq_psum nsq_ready adj_psum "
                 "dist_psum expo_ready aT_ready msg_psum msg_ready conv_psum pre_ready conv_ready nmp_psum "
                 "nmp_ready gates_psum rz_ready cand_half cand_ready nn_ready diff_ready mix_ready "
                 "upd_ready x_ready stats_half stats_done stats_kept").split()
        s = {n: sem(n) for n in names}
        ln_act, ln_dve, norm_ready = outer_norm(nc, ctx, sem, c["x_stats"], c["rstd"], c["shift"], "g_ln")
        block = ctx.enter_context(nc.Block())

        @block.sync
        def _(sp):
            for dst, src in ((w1[:, :], d["conv1"]), (wmsg[:, :], d["wmsg"]),
                             (w2[:, :, :], d["conv2"]), (wih[:, :, :], d["wih"].rearrange("(a p) n -> p a n", p=P)),
                             (whh[:, :], d["whh"]), (wse[:, :], d["wse"]), (bse[:, :], d["bse"])):
                sp.dma_start(dst, src).then_inc(w_loaded, 16)
            def batch(b, q):
                after(sp, s["adj_psum"], b - 1)
                sp.dma_start(adj[:, q, :, :], d["adj"][b].rearrange("(j p) m -> p j m", p=P))\
                  .then_inc(adj_loaded[q], 16)

            each(sp, batch)

        @block.gpsimd
        def _(pool):
            for n, src in enumerate(("bn1_g", "bn1_b", "bn1_m", "bn1_v")):
                pool.dma_start(bn[:, 0, n:n + 1], d[src]).then_inc(small_loaded, 16)
            for n, src in enumerate(("bn2_g", "bn2_b", "bn2_m", "bn2_v")):
                pool.dma_start(bn[:, 1, n:n + 1], d[src]).then_inc(small_loaded, 16)
            pool.dma_start(row[:, 0:3 * D], d["bih"]).then_inc(hidden_loaded, 16)
            pool.dma_start(row[:, 3 * D:G], d["bhh"][:, 2 * D:3 * D]).then_inc(hidden_loaded, 16)
            pool.dma_start(row[:, G:G + D], d["bmsg"]).then_inc(hidden_loaded, 16)
            pool.dma_start(hidden_row[:, :], d["bhh"]).then_inc(hidden_loaded, 16)
            pool.memset(h1[:, :, 0:PAD], 0.0).then_inc(consts_set, 1)
            pool.memset(h1[:, :, PAD + N:], 0.0).then_inc(consts_set, 1)
            pool.memset(mhalf3[:, :], -0.5).then_inc(consts_set, 1)
            pool.memset(neg3[:, :], -1.0).then_inc(consts_set, 1)
            pool.wait_ge(parts_done, 5)
            for n in range(3):
                pool.dma_start(bias3[n:n + 1, :], row_parts[:, n, :]).then_inc(parts_moved, 16)
            def batch(b, q):
                pool.wait_ge(s["nn_ready"], b + 1)
                after(pool, s["mix_ready"], b)
                pool.tensor_tensor(diff[:, q, :, :], xn[:, q, :, :], nn[:, q, :, :], ALU.subtract)\
                    .then_inc(s["diff_ready"], 1)
                pool.wait_ge(s["upd_ready"], b + 1)
                pool.tensor_tensor(x[:, bass.ds(b * J, J), :], x[:, bass.ds(b * J, J), :], upd[:, q, :, :],
                                   ALU.add).then_inc(s["x_ready"], 1)

            each(pool, batch)

        @block.scalar
        def _(act):
            ln_act(act)
            act.wait_ge(eps_set, 1)
            act.wait_ge(small_loaded, 16 * 8)
            act.activation(bn_work[:, :, 0:1], bn[:, :, 3:4], ACT.Sqrt, bias=eps[:, 0:1]).then_inc(bn_std, 1)
            act.wait_ge(bn_ready, 1)
            act.wait_ge(consts_set, 4)
            act.wait_ge(w_loaded, 16 * 7)
            def batch(b, q):
                act.wait_ge(s["xT_psum"], b + 1)
                act.activation(xT[:, q, :], p_xT[:, 0:N], ACT.Copy).then_inc(s["xT_ready"], 1)
                act.wait_ge(s["sT_psum"], b + 1)
                act.activation(sT[:, q, :], p_h1[0:SE, N:2 * N], ACT.Identity, bias=bse[:, 0:1]).then_inc(s["sT_ready"], 1)
                act.activation(s2T[:, q, :], p_h1[0:SE, N:2 * N], ACT.Square, bias=bse[:, 0:1]).then_inc(s["sT_ready"], 1)
                act.activation(h1[:, q, PAD:PAD + N], p_h1[:, 0:N], ACT.Relu, bias=bn_shift[:, 0, :],
                               scale=bn_scale[:, 0, :]).then_inc(s["h1_ready"], 1)
                act.wait_ge(s["msg_psum"], b + 1)
                act.activation(msg[:, q, :, :], p_xT[:, N:2 * N].rearrange("p (j d) -> p j d", j=J), ACT.Relu)\
                   .then_inc(s["msg_ready"], 1)
                act.wait_ge(s["nsq_psum"], b + 1)
                act.activation(nsq[:, q, :], p_nmp[:, N:N + J], ACT.Copy).then_inc(s["nsq_ready"], 1)
                act.wait_ge(s["dist_psum"], b + 1)
                act.wait_ge(s["nsq_ready"], b + 1)
                for j in range(J):
                    act.activation(expo[:, q, j, :], p_dist[:, j * N:(j + 1) * N], ACT.Exp, scale=2.0,
                                   bias=nsq[:, q, j:j + 1]).then_inc(s["expo_ready"], 1)
                act.wait_ge(s["pre_ready"], b + 1)
                act.activation(convT[:, q, :], pre[:, q, :], ACT.Relu, bias=bn_shift[:, 1, :]).then_inc(s["conv_ready"], 1)
                act.wait_ge(s["nmp_psum"], b + 1)
                act.activation(nmpT[:, q, :], p_nmp[:, 0:N], ACT.Copy).then_inc(s["nmp_ready"], 1)
                act.wait_ge(s["gates_psum"], b + 1)
                act.activation(rz[:, q, :, :], p_gate[:, :, 0:2 * D], ACT.Tanh, scale=0.5).then_inc(s["rz_ready"], 1)
                act.wait_ge(s["cand_ready"], b + 1)
                act.activation(nn[:, q, :, :], cand2[:, q, :, :], ACT.Tanh).then_inc(s["nn_ready"], 1)

            each(act, batch)

        @block.vector
        def _(dve):
            dve.memset(eps[:, :], LN_EPS).then_inc(eps_set, 1)
            ln_dve(dve)
            dve.wait_ge(bn_std, 1)
            dve.reciprocal(bn_work[:, :, 1:2], bn_work[:, :, 0:1]).then_inc(bn_steps, 1)
            dve.wait_ge(bn_steps, 1)
            dve.tensor_tensor(bn_scale[:, :, :], bn[:, :, 0:1], bn_work[:, :, 1:2], ALU.mult).then_inc(bn_steps, 1)
            dve.wait_ge(bn_steps, 2)
            dve.tensor_tensor(bn_work[:, :, 0:1], bn[:, :, 2:3], bn_scale[:, :, :], ALU.mult).then_inc(bn_steps, 1)
            dve.wait_ge(bn_steps, 3)
            dve.tensor_tensor(bn_shift[:, :, :], bn[:, :, 1:2], bn_work[:, :, 0:1], ALU.subtract).then_inc(bn_ready, 1)
            dve.wait_ge(hidden_loaded, 16 * 4)
            dve.tensor_tensor(row[:, 0:2 * D], row[:, 0:2 * D], hidden_row[:, 0:2 * D], ALU.add).then_inc(row_ready, 1)
            dve.wait_ge(row_ready, 1)
            split_rows(dve, row[:, :], row_work[:, :], [row_parts[:, n, :] for n in range(3)], parts_done)
            dve.wait_ge(norm_ready, 1)
            dve.wait_ge(bn_ready, 1)
            def batch(b, q):
                after(dve, s["diff_ready"], b)
                for j in range(J):
                    t = b * J + j
                    dve.tensor_scalar(xn[:, q, j, :], x[:, t, :], c["rstd"][:, bass.ds(t, 1)],
                                      c["shift"][:, bass.ds(t, 1)], ALU.mult, ALU.add).then_inc(s["xn_ready"], 1)
                dve.wait_ge(s["adj_psum"], b + 1)
                dve.wait_ge(s["expo_ready"], (b + 1) * J)
                dve.tensor_tensor(aT[:, q, :, :], expo[:, q, :, :], p_adj[:, :].rearrange("p (j n) -> p j n", j=J),
                                  ALU.mult).then_inc(s["aT_ready"], 1)
                dve.wait_ge(s["conv_psum"], b + 1)
                dve.scalar_tensor_tensor(pre[:, q, :], p_conv[:, 0:N], bn_scale[:, 1, :], xT[:, q, :],
                                         ALU.mult, ALU.add).then_inc(s["pre_ready"], 1)
                dve.wait_ge(s["rz_ready"], b + 1)
                dve.scalar_tensor_tensor(cand[:, q, :, :], rz[:, q, :, 0:D], 1.0, p_gate[:, :, 3 * D:G],
                                         ALU.add, ALU.mult).then_inc(s["cand_half"], 1)
                dve.wait_ge(s["cand_half"], b + 1)
                dve.scalar_tensor_tensor(cand2[:, q, :, :], cand[:, q, :, :], 0.5, p_gate[:, :, 2 * D:3 * D],
                                         ALU.mult, ALU.add).then_inc(s["cand_ready"], 1)
                dve.wait_ge(s["diff_ready"], b + 1)
                dve.scalar_tensor_tensor(mix[:, q, :, :], rz[:, q, :, D:2 * D], 1.0, diff[:, q, :, :],
                                         ALU.add, ALU.mult).then_inc(s["mix_ready"], 1)
                after(dve, s["stats_kept"], b)
                dve.wait_ge(s["mix_ready"], b + 1)
                dve.scalar_tensor_tensor(upd[:, q, :, :], mix[:, q, :, :], 0.5, nn[:, q, :, :],
                                         ALU.mult, ALU.add).then_inc(s["upd_ready"], 1)
                dve.wait_ge(norm_ready, 1)
                dve.wait_ge(s["x_ready"], b + 1)
                for j in range(J):
                    last = dve.bn_stats(bn6[:, q, j, :], x[:, b * J + j, :])
                last.then_inc(s["stats_half"], 1)
                dve.wait_ge(norm_ready, 1)
                dve.wait_ge(s["stats_half"], b + 1)
                for j in range(J):
                    dve.bn_aggr(mean_var[:, j, :], bn6[:, q, j, :]).then_inc(s["stats_done"], 1)
                dve.wait_ge(s["stats_done"], (b + 1) * J)
                keep_stats(dve, c, b, mean_var[:, :, :]).then_inc(s["stats_kept"], 1)

            each(dve, batch)
            dve.wait_ge(s["stats_kept"], B)

        @block.tensor
        def _(pe):
            pe.wait_ge(w_loaded, 16 * 7)
            pe.wait_ge(consts_set, 4)
            pe.wait_ge(parts_moved, 16 * 3)
            def batch(b, q):
                after(pe, s["msg_ready"], b)
                pe.wait_ge(s["xn_ready"], (b + 1) * J)
                for j in range(J):
                    last = pe.transpose(p_xT[:, j * P:(j + 1) * P], xn[:, q, j, :], ident[:, :])
                last.then_inc(s["xT_psum"], 1)
                after(pe, s["aT_ready"], b)
                pe.wait_ge(adj_loaded[q], adj_count(b, q))
                for m in range(J):
                    for j in range(J):
                        last = pe.transpose(p_adj[:, m * N + j * P:m * N + (j + 1) * P],
                                            adj[:, q, j, m * P:(m + 1) * P], ident[:, :])
                last.then_inc(s["adj_psum"], 1)
                after(pe, s["h1_ready"], b)
                pe.wait_ge(s["xT_ready"], b + 1)
                pe.matmul(p_h1[:, 0:N], w1[:, :], xT[:, q, :], start=True, stop=True)
                pe.matmul(p_h1[0:SE, N:2 * N], wse[:, :], xT[:, q, :], start=True, stop=True,
                          skip_group_check=True).then_inc(s["sT_psum"], 1)
                for j in range(J):
                    part = p_xT[:, N + j * D:N + (j + 1) * D]
                    pe.matmul(part, c["ones3"][0:3, :], bias3[:, G:G + D], start=True, stop=False,
                              skip_group_check=True)
                    last = pe.matmul(part, xT[:, q, j * P:(j + 1) * P], wmsg[:, :], start=False, stop=True,
                                     skip_group_check=True)
                last.then_inc(s["msg_psum"], 1)
                after(pe, s["nmp_ready"], b)
                pe.wait_ge(s["sT_ready"], (b + 1) * 2)
                for j in range(J):
                    last = pe.matmul(p_nmp[:, N + j:N + j + 1], s2T[:, q, j * P:(j + 1) * P], neg3[:, :],
                                     start=True, stop=True)
                last.then_inc(s["nsq_psum"], 1)
                after(pe, s["expo_ready"], b * J)
                for j in range(J):
                    part = p_dist[:, j * N:(j + 1) * N]
                    pe.matmul(part, sT[:, q, j * P:(j + 1) * P], sT[:, q, :], start=True, stop=False)
                    last = pe.matmul(part, mhalf3[:, :], s2T[:, q, :], start=False, stop=True)
                last.then_inc(s["dist_psum"], 1)
                pe.wait_ge(s["h1_ready"], b + 1)
                after(pe, s["pre_ready"], b)
                for k in range(TAPS):
                    last = pe.matmul(p_conv[:, 0:N], w2[:, k, :], h1[:, q, k:k + N], start=k == 0, stop=k == TAPS - 1)
                last.then_inc(s["conv_psum"], 1)
                pe.wait_ge(s["nsq_ready"], b + 1)
                pe.wait_ge(s["msg_ready"], b + 1)
                pe.wait_ge(s["aT_ready"], b + 1)
                for m in range(J):
                    last = pe.matmul(p_nmp[:, 0:N], msg[:, q, m, :], aT[:, q, m, :], start=m == 0, stop=m == J - 1)
                last.then_inc(s["nmp_psum"], 1)
                after(pe, s["cand_ready"], b)
                for j in range(J):
                    pe.matmul(p_gate[:, j, :], c["ones3"][0:3, :], bias3[:, 0:G], start=True, stop=False,
                              skip_group_check=True)
                    xTj = xT[:, q, j * P:(j + 1) * P]
                    pe.matmul(p_gate[:, j, 0:2 * D], xTj, whh[:, 0:2 * D], start=False, stop=False,
                              skip_group_check=True)
                    pe.matmul(p_gate[:, j, 3 * D:G], xTj, whh[:, 2 * D:3 * D], start=False, stop=True,
                              skip_group_check=True)
                pe.wait_ge(s["conv_ready"], b + 1)
                for j in range(J):
                    pe.matmul(p_gate[:, j, 0:3 * D], convT[:, q, j * P:(j + 1) * P], wih[:, 0, :], start=False,
                              stop=False, skip_group_check=True)
                pe.wait_ge(s["nmp_ready"], b + 1)
                for j in range(J):
                    last = pe.matmul(p_gate[:, j, 0:3 * D], nmpT[:, q, j * P:(j + 1) * P], wih[:, 1, :],
                                     start=False, stop=True, skip_group_check=True)
                last.then_inc(s["gates_psum"], 1)

            each(pe, batch)


def stage_recurrent(nc, d, c):
    TG = 8
    GROUPS = TILES // TG
    HALF = TG // 2
    with ExitStack() as ctx:
        def sb(n, s, t=F32):
            return ctx.enter_context(nc.sbuf_tensor("r_" + n, s, t))

        sem = ctx.enter_context(stage_semaphores(nc, "r_"))
        x, ident = c["x"], c["ident"]
        w, w_gain, w_mid = sb("w", [P, D]), sb("w_gain", [P, D]), sb("w_mid", [P, D])
        ln_w, ln_b = sb("ln_w", [P, 1]), sb("ln_b", [P, 1])
        row, row_work = sb("row", [1, D]), sb("row_work", [1, D])
        row_parts, bias3 = sb("row_parts", [1, 3, D], BF16), sb("bias3", [3, HALF, D], BF16)
        h = sb("h", [P, GROUPS, TG, D])
        hT = sb("hT", [P, 2, TG, D])
        bn6 = sb("bn6", [P, 2, TG, 6])
        gap, ss, gap2 = sb("gap", [P, TG]), sb("ss", [P, TG]), sb("gap2", [P, TG])
        spread = sb("spread", [P, GROUPS, TG])
        scale = sb("scale", [P, GROUPS, TG])
        mean_var = sb("mean_var", [P, 2, TG, 2])
        p_hT = ctx.enter_context(nc.psum_tensor("r_p_hT", [P, 2, TG, D], F32))
        p_z = ctx.enter_context(nc.psum_tensor("r_p_z", [P, 2, TG, D], F32))

        loaded, mean_psum, bias_psum, w_steps, bias_row = (sem("loaded"), sem("mean_psum"), sem("bias_psum"),
                                                          sem("w_steps"), sem("bias_row"))
        parts_done, parts_moved = sem("parts_done"), sem("parts_moved")
        h_start = sem("h_start")
        scale_done, scaled, turned, copied, product = (sem("scale_done"), sem("scaled"), sem("turned"),
                                                       sem("copied"), sem("product"))
        tanh_done, mixed, silu_done, bn_done, gap_done, gap2_done, spread_done = (
            sem("tanh_done"), sem("mixed"), sem("silu_done"), sem("bn_done"), sem("gap_done"), sem("gap2_done"),
            sem("spread_done"))
        x_done, x_bn, x_aggr, x_kept = sem("x_done"), sem("x_bn"), sem("x_aggr"), sem("x_kept")
        ln_act, ln_dve, norm_ready = outer_norm(nc, ctx, sem, c["x_stats"], c["rstd"], c["shift"], "r_ln")
        CREDIT = 2
        block = ctx.enter_context(nc.Block())

        def front(step, g):
            return (step - 1) * GROUPS + g

        def back(step, g):
            return step * GROUPS + g

        @block.sync
        def _(sp):
            sp.dma_start(w[:, :], d["ffn_w"]).then_inc(loaded, 16)
            sp.dma_start(ln_w[:, :], d["ffn_ln_w"]).then_inc(loaded, 16)
            sp.dma_start(ln_b[:, :], d["ffn_ln_b"]).then_inc(loaded, 16)
            sp.dma_start(row[:, :], d["ffn_b"]).then_inc(loaded, 16)
            sp.wait_ge(parts_done, 5)
            for n in range(3):
                for t in range(HALF):
                    sp.dma_start(bias3[n:n + 1, t, :], row_parts[:, n, :]).then_inc(parts_moved, 16)

        @block.gpsimd
        def _(pool):
            def rescale(step, g):
                n = front(step, g) + 1
                pool.wait_ge(spread_done, n)
                pool.tensor_tensor(scale[:, g, :], spread[:, g, :], c["minus_half"][:, 0:TG], ALU.pow)\
                    .then_inc(scale_done, 1)
                pool.wait_ge(norm_ready, 1)
                pool.wait_ge(scale_done, n)
                for t in range(TG):
                    last = pool.tensor_scalar(h[:, g, t, :], h[:, g, t, :], scale[:, g, t:t + 1], float(D) ** 0.5,
                                              ALU.mult, ALU.mult)
                last.then_inc(scaled, 1)

            with pool.Fori(1, STEPS) as step:
                for g in range(GROUPS):
                    rescale(step, g)
            for g in range(GROUPS):
                rescale(STEPS, g)

        @block.tensor
        def _(pe):
            pe.wait_ge(w_steps, 1)
            pe.matmul(p_z[:, 0, 0, :], c["ones"][:, :], w_gain[:, :], start=True, stop=True).then_inc(mean_psum, 1)
            pe.matmul(p_hT[0:1, 0, 0, :], ln_b[:, :], w[:, :], start=True, stop=True).then_inc(bias_psum, 1)
            pe.sem_inc(product, CREDIT)
            pe.wait_ge(w_steps, 3)
            pe.wait_ge(bias_row, 1)
            pe.wait_ge(parts_moved, 16 * 3 * HALF)

            def turn(step, g):
                pe.wait_ge(scaled, front(step, g) + 1)
                pe.wait_ge(copied, front(step, g) + 1)
                for t in range(TG):
                    last = pe.transpose(p_hT[:, g % 2, t, :], h[:, g, t, :], ident[:, :])
                last.then_inc(turned, 1)

            def multiply(step, g):
                pe.wait_ge(copied, front(step, g) + 1 + CREDIT)
                pe.wait_ge(mixed, back(step, g) - 2 + 1)
                for a in range(0, TG, HALF):
                    pe.matmul(p_z[:, g % 2, a:a + HALF, :], c["ones3"][:, :], bias3[:, :, :], start=True, stop=False,
                              skip_group_check=True)
                    for t in range(a, a + HALF):
                        last = pe.matmul(p_z[:, g % 2, t, :], hT[:, g % 2, t, :], w[:, :], start=False, stop=True,
                                         skip_group_check=True)
                last.then_inc(product, 1)

            def all_groups(step):
                for g in range(GROUPS + 1):
                    if g < GROUPS:
                        turn(step, g)
                    if g >= 1:
                        multiply(step, g - 1)

            with pe.Fori(1, STEPS) as step:
                all_groups(step)
            all_groups(STEPS)

        @block.scalar
        def _(act):
            ln_act(act)
            act.sem_inc(copied, CREDIT)

            def copy_turned(step, g):
                act.wait_ge(turned, front(step, g) + 1)
                act.wait_ge(product, front(step, g) + 1)
                act.activation(hT[:, g % 2, :, :], p_hT[:, g % 2, :, :], ACT.Copy).then_inc(copied, 1)

            def tanh(step, g, src):
                act.activation(h[:, g, :, :], src, ACT.Tanh).then_inc(tanh_done, 1)

            def silu(step, g):
                act.wait_ge(mixed, back(step, g) + 1)
                act.activation(h[:, g, :, :], h[:, g, :, :], ACT.Silu).then_inc(silu_done, 1)

            for g in range(GROUPS + 1):
                if g < GROUPS:
                    act.wait_ge(h_start, g + 1)
                    act.activation(hT[:, g % 2, :, :], h[:, g, :, :], ACT.Tanh).then_inc(tanh_done, 1)
                if g >= 1:
                    silu(0, g - 1)
            with act.Fori(1, STEPS) as step:
                for g in range(GROUPS + 2):
                    if g < GROUPS:
                        copy_turned(step, g)
                    if 1 <= g <= GROUPS:
                        act.wait_ge(product, front(step, g - 1) + 1 + CREDIT)
                        tanh(step, g - 1, p_z[:, (g - 1) % 2, :, :])
                    if g >= 2:
                        silu(step, g - 2)
            for g in range(GROUPS):
                copy_turned(STEPS, g)

        @block.vector
        def _(dve):
            ln_dve(dve)
            dve.wait_ge(loaded, 16 * 4)
            dve.tensor_scalar(w_gain[:, :], w[:, :], ln_w[:, 0:1], None, ALU.mult).then_inc(w_steps, 1)
            dve.wait_ge(bias_psum, 1)
            dve.tensor_tensor(row[:, :], row[:, :], p_hT[0:1, 0, 0, :], ALU.add).then_inc(bias_row, 1)
            dve.wait_ge(mean_psum, 1)
            dve.tensor_scalar(w_mid[:, :], p_z[:, 0, 0, :], 1.0 / D, None, ALU.mult).then_inc(w_steps, 1)
            dve.wait_ge(w_steps, 2)
            dve.tensor_tensor(w[:, :], w_gain[:, :], w_mid[:, :], ALU.subtract).then_inc(w_steps, 1)
            dve.wait_ge(bias_row, 1)
            split_rows(dve, row[:, :], row_work[:, :], [row_parts[:, n, :] for n in range(3)], parts_done)
            dve.wait_ge(norm_ready, 1)

            def start(g):
                for t in range(TG):
                    a = g * TG + t
                    last = dve.tensor_scalar(h[:, g, t, :], x[:, a, :], c["rstd"][:, a:a + 1], c["shift"][:, a:a + 1],
                                             ALU.mult, ALU.add)
                last.then_inc(h_start, 1)

            def mix(step, g):
                dve.wait_ge(tanh_done, back(step, g) + 1)
                dve.scalar_tensor_tensor(h[:, g, :, :], h[:, g, :, :], 0.01, p_z[:, g % 2, :, :], ALU.mult, ALU.add)\
                   .then_inc(mixed, 1)

            def stats(step, g):
                n = back(step, g)
                dve.wait_ge(silu_done, n + 1)
                for t in range(TG):
                    last = dve.bn_stats(bn6[:, g % 2, t, :], h[:, g, t, :])
                last.then_inc(bn_done, 1)
                dve.wait_ge(bn_done, n + 1)
                dve.tensor_tensor(gap[:, :], bn6[:, g % 2, :, 1], bn6[:, g % 2, :, 4], ALU.subtract)
                dve.tensor_tensor(ss[:, :], bn6[:, g % 2, :, 2], bn6[:, g % 2, :, 5], ALU.add).then_inc(gap_done, 1)
                dve.wait_ge(gap_done, n + 1)
                dve.scalar_tensor_tensor(gap2[:, :], gap[:, :], D / 4.0, gap[:, :], ALU.mult, ALU.mult).then_inc(gap2_done, 1)
                dve.wait_ge(gap2_done, n + 1)
                dve.scalar_tensor_tensor(spread[:, g, :], gap2[:, :], D * LN_EPS, ss[:, :], ALU.add, ALU.add)\
                   .then_inc(spread_done, 1)

            for g in range(GROUPS + 2):
                if g < GROUPS:
                    start(g)
                if 1 <= g <= GROUPS:
                    dve.wait_ge(tanh_done, g)
                    dve.scalar_tensor_tensor(h[:, g - 1, :, :], hT[:, (g - 1) % 2, :, :], 0.01, h[:, g - 1, :, :],
                                             ALU.mult, ALU.add).then_inc(mixed, 1)
                if g >= 2:
                    stats(0, g - 2)
            with dve.Fori(1, STEPS) as step:
                for g in range(1, GROUPS + 2):
                    if g <= GROUPS:
                        mix(step, g - 1)
                    if g >= 2:
                        stats(step, g - 2)
            for g in range(GROUPS):
                dve.wait_ge(product, front(STEPS, g) + 1 + CREDIT)
                xg = x[:, g * TG:(g + 1) * TG, :]
                dve.tensor_tensor(xg, xg, p_z[:, g % 2, :, :], ALU.add).then_inc(mixed, 1)
                dve.wait_ge(mixed, back(STEPS, g) + 1)
                for t in range(TG):
                    last = dve.bn_stats(bn6[:, g % 2, t, :], x[:, g * TG + t, :])
                last.then_inc(x_bn, 1)
                dve.wait_ge(x_bn, g + 1)
                for t in range(TG):
                    last = dve.bn_aggr(c["x_stats"][:, g * TG + t, :], bn6[:, g % 2, t, :])
            last.then_inc(x_kept, 1)
            dve.wait_ge(x_kept, 1)


def skewed(eng, front, back):
    front(0, 0)
    front(1, 1)
    back(0, 0)
    with eng.Fori(1, B // 2) as i:
        for q in range(2):
            front(i * 2 + q, q)
            back(i * 2 + q - 1, 1 - q)
    back(B - 1, 1)


def stage_graph_attention(nc, d, c):
    with ExitStack() as ctx:
        def sb(n, s, t=F32):
            return ctx.enter_context(nc.sbuf_tensor("a_" + n, s, t))

        def ps(n, s):
            return ctx.enter_context(nc.psum_tensor("a_" + n, s, F32))

        sem = ctx.enter_context(stage_semaphores(nc, "a_"))
        x, ident = c["x"], c["ident"]
        w = sb("w", [P, 3, D])
        row, row_work = sb("row", [1, D]), sb("row_work", [1, D])
        row_parts, bias3 = sb("row_parts", [1, 3, D], BF16), sb("bias3", [3, J, D], BF16)
        gain, offset = sb("gain", [P, J, D]), sb("offset", [P, J, D])
        minus_half = c["minus_half"]
        xn = sb("xn", [P, 2, J, D])
        xT = sb("xT", [P, 2, N])
        adj = sb("adj", [P, 2, J, N])
        relu_qk, relu_x = sb("relu_qk", [P, 2, N]), sb("relu_x", [P, J, D])
        qkT = sb("qkT", [P, 2, 2, N])
        lin = sb("lin", [P, 2, J, D])
        att = sb("att", [P, 2, H, J * N])
        ah = sb("ah", [P, 2, H, J * N])
        degree, linked, root, dis = (sb("degree", [P, J * H]), sb("linked", [P, J * H]), sb("root", [P, J * H]),
                                     sb("dis", [P, 2, J * H]))
        lin_dis = sb("lin_dis", [P, 2, J, D])
        y, yn, yg, x_off = sb("y", [P, J, D]), sb("yn", [P, J, D]), sb("yg", [P, J, D]), sb("x_off", [P, J, D])
        y6, y_stats, y_var, y_rstd = sb("y6", [P, J, 6]), sb("y_stats", [P, J, 2]), sb("y_var", [P, J]), sb("y_rstd", [P, J])
        bn6, mean_var = sb("bn6", [P, J, 6]), sb("mean_var", [P, J, 2])

        p_xT = ps("p_xT", [P, 512])
        p_qk = ps("p_qk", [P, 2, N])
        p_adj = ps("p_adj", [P, J * N])
        p_s = ps("p_s", [P, H, J * N])
        p_y = ps("p_y", [P, 512])

        loaded, parts_done, parts_moved = sem("loaded"), sem("parts_done"), sem("parts_moved")
        adj_loaded = [sem("adj_loaded0"), sem("adj_loaded1")]
        names = ("xn_ready xT_psum xT_ready adj_psum qk_psum lin_psum relu_ready qk_ready lin_ready s_psum att_ready "
                 "ah_ready degree_psum degree_ready root_ready dis_ready lin_dis_ready y_psum y_ready y_bn y_aggr "
                 "y_var_ready y_rstd_ready yn_ready yg_ready off_ready x_ready x_bn x_aggr x_kept").split()
        s = {n: sem(n) for n in names}
        ln_act, ln_dve, norm_ready = outer_norm(nc, ctx, sem, c["x_stats"], c["rstd"], c["shift"], "a_ln")
        block = ctx.enter_context(nc.Block())

        def heads(t):
            return t.rearrange("p j (h e) -> p (j h) e", h=H)

        def per_head(t):
            return t.rearrange("p (g o) -> p g o", o=1).broadcast_to([P, J * H, HD])

        @block.sync
        def _(sp):
            for n, name in enumerate(("att_lin", "att_q", "att_k")):
                sp.dma_start(w[:, n, :], d[name]).then_inc(loaded, 16)
            sp.dma_start(row[:, :], d["att_b"]).then_inc(loaded, 16)
            for j in range(J):
                sp.dma_start(gain[:, j, :], d["att_g"]).then_inc(loaded, 16)
                sp.dma_start(offset[:, j, :], d["att_o"]).then_inc(loaded, 16)
            sp.wait_ge(parts_done, 5)
            for n in range(3):
                for j in range(J):
                    sp.dma_start(bias3[n:n + 1, j, :], row_parts[:, n, :]).then_inc(parts_moved, 16)

            def load(b, q):
                after(sp, s["adj_psum"], b - 1)
                sp.dma_start(adj[:, q, :, :], d["adj"][b].rearrange("(j p) m -> p j m", p=P)).then_inc(adj_loaded[q], 16)

            each(sp, load)

        @block.tensor
        def _(pe):
            pe.wait_ge(loaded, 16 * 8)
            pe.wait_ge(parts_moved, 16 * 3 * J)

            def front(b, q):
                pe.wait_ge(s["xn_ready"], b + 1)
                after(pe, s["lin_ready"], b)
                for j in range(J):
                    last = pe.transpose(p_xT[:, j * P:(j + 1) * P], xn[:, q, j, :], ident[:, :])
                last.then_inc(s["xT_psum"], 1)
                pe.wait_ge(adj_loaded[q], adj_count(b, q))
                after(pe, s["ah_ready"], b)
                for m in range(J):
                    for j in range(J):
                        last = pe.transpose(p_adj[:, m * N + j * P:m * N + (j + 1) * P],
                                            adj[:, q, j, m * P:(m + 1) * P], ident[:, :])
                last.then_inc(s["adj_psum"], 1)
                pe.wait_ge(s["xT_ready"], b + 1)
                for n in range(2):
                    last = pe.matmul(p_qk[:, n, :], w[:, 1 + n, :], xT[:, q, :], start=True, stop=True)
                last.then_inc(s["qk_psum"], 1)
                pe.matmul(p_xT[:, N:2 * N], c["ones3"][:, :], bias3[:, :, :], start=True, stop=False,
                          skip_group_check=True)
                for j in range(J):
                    last = pe.matmul(p_xT[:, N + j * D:N + (j + 1) * D], xT[:, q, j * P:(j + 1) * P], w[:, 0, :],
                                     start=False, stop=True, skip_group_check=True)
                last.then_inc(s["lin_psum"], 1)
                pe.wait_ge(s["qk_ready"], b + 1)
                after(pe, s["att_ready"], b)
                for j in range(J):
                    for h in range(H):
                        r = slice(h * HD, (h + 1) * HD)
                        last = pe.matmul(p_s[:, h, j * N:(j + 1) * N], qkT[r, q, 1, j * P:(j + 1) * P],
                                         qkT[r, q, 0, :], start=True, stop=True, tile_position=(h * HD, 0))
                last.then_inc(s["s_psum"], 1)

            def back(b, q):
                pe.wait_ge(s["ah_ready"], b + 1)
                after(pe, s["y_ready"], b)
                for j in range(J):
                    for h in range(H):
                        for m in range(J):
                            last = pe.matmul(p_y[:, N + j * H + h:N + j * H + h + 1],
                                             ah[:, q, h, m * N + j * P:m * N + (j + 1) * P], c["ones"][:, 0:1],
                                             start=m == 0, stop=m == J - 1, skip_group_check=True)
                last.then_inc(s["degree_psum"], 1)
                pe.wait_ge(s["lin_dis_ready"], b + 1)
                for j in range(J):
                    for h in range(H):
                        for m in range(J):
                            last = pe.matmul(p_y[:, j * D + h * HD:j * D + (h + 1) * HD],
                                             ah[:, q, h, m * N + j * P:m * N + (j + 1) * P],
                                             lin_dis[:, q, m, h * HD:(h + 1) * HD],
                                             start=m == 0, stop=m == J - 1, skip_group_check=True)
                last.then_inc(s["y_psum"], 1)

            skewed(pe, front, back)

        @block.scalar
        def _(act):
            ln_act(act)

            def front(b, q):
                act.wait_ge(s["xT_psum"], b + 1)
                act.activation(xT[:, q, :], p_xT[:, 0:N], ACT.Copy).then_inc(s["xT_ready"], 1)
                act.wait_ge(s["qk_psum"], b + 1)
                after(act, s["lin_ready"], b)
                act.activation(relu_qk[:, :, :], p_qk[:, :, :], ACT.Relu, scale=0.99).then_inc(s["relu_ready"], 1)
                act.wait_ge(s["lin_psum"], b + 1)
                act.activation(relu_x[:, :, :], p_xT[:, N:2 * N].rearrange("p (j d) -> p j d", j=J), ACT.Relu,
                               scale=0.99).then_inc(s["relu_ready"], 1)
                act.wait_ge(s["s_psum"], b + 1)
                act.activation(att[:, q, :, :], p_s[:, :, :], ACT.Sigmoid, scale=HD ** -0.5).then_inc(s["att_ready"], 1)

            def back(b, q):
                pass

            skewed(act, front, back)

        @block.vector
        def _(dve):
            ln_dve(dve)
            dve.wait_ge(loaded, 16 * 8)
            split_rows(dve, row[:, :], row_work[:, :], [row_parts[:, n, :] for n in range(3)], parts_done)

            def front(b, q):
                after(dve, s["xT_psum"], b)
                for j in range(J):
                    t = b * J + j
                    last = dve.tensor_scalar(xn[:, q, j, :], x[:, t, :], c["rstd"][:, bass.ds(t, 1)],
                                             c["shift"][:, bass.ds(t, 1)], ALU.mult, ALU.add)
                last.then_inc(s["xn_ready"], 1)
                dve.wait_ge(s["relu_ready"], b * 2 + 1)
                dve.scalar_tensor_tensor(qkT[:, q, :, :], p_qk[:, :, :], 0.01, relu_qk[:, :, :], ALU.mult, ALU.add)\
                   .then_inc(s["qk_ready"], 1)
                dve.wait_ge(s["relu_ready"], b * 2 + 2)
                dve.scalar_tensor_tensor(lin[:, q, :, :], p_xT[:, N:2 * N].rearrange("p (j d) -> p j d", j=J), 0.01,
                                         relu_x[:, :, :], ALU.mult, ALU.add).then_inc(s["lin_ready"], 1)

            def weigh(b, q):
                dve.wait_ge(s["att_ready"], b + 1)
                dve.wait_ge(s["adj_psum"], b + 1)
                dve.tensor_tensor(ah[:, q, :, :], att[:, q, :, :],
                                  p_adj[:, :].rearrange("p (o n) -> p o n", o=1).broadcast_to([P, H, J * N]), ALU.mult)\
                   .then_inc(s["ah_ready"], 1)

            def back(b, q):
                dve.wait_ge(s["degree_psum"], b + 1)
                after(dve, s["root_ready"], b)
                dve.tensor_scalar(degree[:, :], p_y[:, N:N + J * H], 1.2e-38, None, ALU.max)
                after(dve, s["dis_ready"], b)
                dve.tensor_scalar(linked[:, :], p_y[:, N:N + J * H], 0.0, None, ALU.is_gt).then_inc(s["degree_ready"], 1)
                dve.wait_ge(s["y_psum"], b + 1)
                dve.tensor_tensor(heads(y[:, :, :]), heads(p_y[:, 0:N].rearrange("p (j d) -> p j d", j=J)),
                                  per_head(dis[:, q, :]), ALU.mult).then_inc(s["y_ready"], 1)
                dve.wait_ge(norm_ready, 1)
                dve.wait_ge(s["y_ready"], b + 1)
                for j in range(J):
                    last = dve.bn_stats(y6[:, j, :], y[:, j, :])
                last.then_inc(s["y_bn"], 1)
                dve.wait_ge(norm_ready, 1)
                dve.wait_ge(s["y_bn"], b + 1)
                for j in range(J):
                    last = dve.bn_aggr(y_stats[:, j, :], y6[:, j, :])
                last.then_inc(s["y_aggr"], 1)
                dve.wait_ge(s["y_aggr"], b + 1)
                dve.tensor_scalar(y_var[:, :], y_stats[:, :, 1], LN_EPS, None, ALU.add).then_inc(s["y_var_ready"], 1)
                dve.wait_ge(s["y_rstd_ready"], b + 1)
                after(dve, s["yg_ready"], b)
                for j in range(J):
                    last = dve.tensor_scalar(yn[:, j, :], y[:, j, :], y_stats[:, j, 0:1], y_rstd[:, j:j + 1],
                                             ALU.subtract, ALU.mult)
                last.then_inc(s["yn_ready"], 1)

            def close(b, q):
                dve.wait_ge(s["yg_ready"], b + 1)
                dve.wait_ge(s["off_ready"], b + 1)
                dve.tensor_tensor(x[:, bass.ds(b * J, J), :], yg[:, :, :], x_off[:, :, :], ALU.add)\
                   .then_inc(s["x_ready"], 1)
                dve.wait_ge(norm_ready, 1)
                dve.wait_ge(s["x_ready"], b + 1)
                for j in range(J):
                    last = dve.bn_stats(bn6[:, j, :], x[:, b * J + j, :])
                last.then_inc(s["x_bn"], 1)
                dve.wait_ge(norm_ready, 1)
                dve.wait_ge(s["x_bn"], b + 1)
                for j in range(J):
                    last = dve.bn_aggr(mean_var[:, j, :], bn6[:, j, :])
                last.then_inc(s["x_aggr"], 1)
                dve.wait_ge(s["x_aggr"], b + 1)
                keep_stats(dve, c, b, mean_var[:, :, :]).then_inc(s["x_kept"], 1)

            def front_all(b, q):
                front(b, q)
                weigh(b, q)

            def back_all(b, q):
                back(b, q)
                close(b, q)

            skewed(dve, front_all, back_all)
            dve.wait_ge(s["x_kept"], B)

        @block.gpsimd
        def _(pool):
            pool.wait_ge(loaded, 16 * 8)

            def front(b, q):
                pass

            def back(b, q):
                after(pool, s["x_ready"], b)
                pool.tensor_tensor(x_off[:, :, :], x[:, bass.ds(b * J, J), :], offset[:, :, :], ALU.add)\
                    .then_inc(s["off_ready"], 1)
                pool.wait_ge(s["degree_ready"], b + 1)
                pool.tensor_tensor(root[:, :], degree[:, :], minus_half[:, 0:J * H], ALU.pow).then_inc(s["root_ready"], 1)
                pool.wait_ge(s["root_ready"], b + 1)
                pool.tensor_tensor(dis[:, q, :], root[:, :], linked[:, :], ALU.mult).then_inc(s["dis_ready"], 1)
                pool.wait_ge(s["dis_ready"], b + 1)
                pool.wait_ge(s["lin_ready"], b + 1)
                pool.tensor_tensor(heads(lin_dis[:, q, :, :]), heads(lin[:, q, :, :]), per_head(dis[:, q, :]), ALU.mult)\
                    .then_inc(s["lin_dis_ready"], 1)
                pool.wait_ge(s["y_var_ready"], b + 1)
                pool.tensor_tensor(y_rstd[:, :], y_var[:, :], minus_half[:, 0:J], ALU.pow).then_inc(s["y_rstd_ready"], 1)
                pool.wait_ge(s["yn_ready"], b + 1)
                pool.tensor_tensor(yg[:, :, :], yn[:, :, :], gain[:, :, :], ALU.mult).then_inc(s["yg_ready"], 1)

            skewed(pool, front, back)


def stage_expert_attention(nc, d, c, out):
    L = E * P
    ROUNDS = ((0, 0), (0, 1), (1, 1))
    TOP_ROUNDS = ((0, 0, 4), (1, 0, 2), (1, 2, 2))
    JOBS = len(ROUNDS) * H
    G = J * H
    PG = 2 * G
    MASKED = -1.0e30
    with ExitStack() as ctx:
        def sb(n, s, t=F32):
            return ctx.enter_context(nc.sbuf_tensor("e_" + n, s, t))

        def ps(n, s, t=F32):
            return ctx.enter_context(nc.psum_tensor("e_" + n, s, t))

        sem = ctx.enter_context(stage_semaphores(nc, "e_"))
        x, ident = c["x"], c["ident"]
        w_hl, b_hl = sb("w_hl", [P, D]), sb("b_hl", [P, 1])
        w_q, w_kv = sb("w_q", [P, E, D]), sb("w_kv", [P, 2, D])
        w_gate = sb("w_gate", [P, E, H * E])
        w_fc, b_fc1 = sb("w_fc", [P, 2, D]), sb("b_fc1", [P, 1])
        w_fgate = sb("w_fgate", [P, H])
        row, row_work = sb("row", [1, D]), sb("row_work", [1, D])
        b_gate, head_row = sb("b_gate", [P, J, H * E]), sb("head_row", [P, H])
        row_parts, bias3 = sb("row_parts", [1, 3, D], BF16), sb("bias3", [3, D], BF16)
        norms = sb("norms", [P, 4, HD])
        ident16, below, above = (sb(n, [P, P], BF16) for n in ("ident16", "below", "above"))
        pick = sb("pick", [P, H, E, P], BF16)
        resid, residT = sb("resid", [P, J, D]), sb("residT", [P, N])

        xn, xT, sxT = sb("xn", [P, 2, J, D]), sb("xT", [P, N]), sb("sxT", [P, 2, N])
        qT, kT, v = sb("qT", [P, 2, E, N]), sb("kT", [P, 2, H, N]), sb("v", [P, 2, J, D])
        q_round, k_round = sb("q_round", [P, E, N], F32R), sb("k_round", [P, H, N], F32R)
        top = sb("top", [P, J, H, E])
        top2 = sb("top2", [P, J, H, HD], BF16)
        topT = sb("topT", [P, J * P], BF16)
        wT = sb("wT", [P, len(ROUNDS), H, L])
        nonzero = sb("nonzero", [P, 2, J, P])
        sumsT = sb("sumsT", [P, J, E, P])
        outT = sb("outT", [P, J, E, P])
        z_over, z_norm, z_sum, logits = (sb("z_over", [P, J * E * H]), sb("z_norm", [P, J, E, H * E]),
                                         sb("z_sum", [P, J, H * E]), sb("logits", [P, J, H * E]))
        g_top, g_low, g_exp, g_sum, g_over, g_w, g_scaled = (sb("g_top", [P, G]), sb("g_low", [P, G, E]), sb("g_exp", [P, G, E]),
                                                   sb("g_sum", [P, G]), sb("g_over", [P, G]), sb("g_w", [P, G, E]),
                                                   sb("g_scaled", [P, G, E]))
        prod = sb("prod", [P, J, E, D])
        mixed = sb("mixed", [P, J, D])
        u = sb("u", [P, 2, J, D])
        n_sum, n_mean, n_mid, n_sq, n_ss, n_var, n_rstd, n_unit, n_gain = (
            sb("n_sum", [P, PG]), sb("n_mean", [P, PG]), sb("n_mid", [P, PG, HD]), sb("n_sq", [P, PG, HD]),
            sb("n_ss", [P, PG]), sb("n_var", [P, PG]), sb("n_rstd", [P, PG]), sb("n_unit", [P, PG, HD]),
            sb("n_gain", [P, PG, HD]))
        fx, fout = sb("fx", [P, PG, HD]), sb("fout", [P, PG, HD])
        fxT, fc1, fc1n, foT = sb("fxT", [P, 2 * N]), sb("fc1", [P, 2 * N]), sb("fc1n", [P, 2 * N]), sb("foT", [P, 2 * N])
        fc2, u2 = sb("fc2", [P, PG, HD]), sb("u2", [P, PG, HD])
        f_top, f_low, f_exp, f_sum, f_over, f_w = (sb("f_top", [P, 2 * J]), sb("f_low", [P, 2 * J, H]),
                                                   sb("f_exp", [P, 2 * J, H]), sb("f_sum", [P, 2 * J]),
                                                   sb("f_over", [P, 2 * J]), sb("f_w", [P, PG]))
        gated = sb("gated", [P, PG, HD])

        p_s = ps("p_s", [P, 2, L])
        p_t = ps("p_t", [P, 2, L])
        p_v = ps("p_v", [P, 2, L])
        p_in = ps("p_in", [P, 512])
        p_kv = ps("p_kv", [P, 512])

        loaded, built, parts_done, parts_moved = sem("loaded"), sem("built"), sem("parts_done"), sem("parts_moved")
        zeroed, masks = sem("zeroed"), sem("masks")
        resid_in, resid_out, resid_ready = sem("resid_in"), sem("resid_out"), sem("resid_ready")
        names = ("xn_ready xT_psum xT_ready sx_psum sx_ready nonzero_ready q_psum q_ready kv_psum kv_ready round_ready s_psum "
                 "top_ready top2_half top2_ready topT_psum topT_ready t_psum weighed values_psum sums_kept out_ready "
                 "gate_psum tok_psum z_over z_norm z_sum logits g_top g_low g_exp g_sum g_over g_w g_scaled prod_ready mixed_ready u_ready").split()
        s = {n: sem(n) for n in names}
        norm_names = "sum mean mid sq ss var rstd unit gain".split()
        ns = {n: sem("n_" + n + "_done") for n in norm_names}
        tail_names = ("fx_ready fxT_psum fxT_ready fc1_psum fc1_ready fc1n_ready fc2_psum fc2_kept u2_ready fout_ready "
                      "foT_psum foT_ready f_psum f_top f_low f_exp f_sum f_over f_w gated_ready x_ready").split()
        t = {n: sem(n) for n in tail_names}
        stored = sem("stored")
        ln_act, ln_dve, norm_ready = outer_norm(nc, ctx, sem, c["x_stats"], c["rstd"], c["shift"], "e_ln")
        block = ctx.enter_context(nc.Block())

        def spread(a, width):
            return a.rearrange("p (g o) -> p g o", o=1).broadcast_to([P, a.shape[1], width])

        def every(eng, prepare, turn_maxima, job, after_job, values, tail):
            def iteration(b, q, i, top, ahead):
                for n in range(JOBS):
                    job(b, q, n, top)
                    after_job(b, q, n)
                    if isinstance(i, int) and i < 1:
                        continue
                    tail(i - 1, q, n)
                if ahead:
                    prepare(b + 2, q, 0, i)
                values(b, q, 1, 0)
                if ahead:
                    prepare(b + 2, q, 1, i)
                values(b, q, 1, 1)
                if top:
                    turn_maxima(b + 1)
                if ahead:
                    prepare(b + 2, q, 2, i)

            for part in range(3):
                prepare(0, 0, part, 0)
            for n in range(JOBS):
                job(-1, 1, n, True)
            prepare(1, 1, 0, 0)
            prepare(1, 1, 1, 0)
            turn_maxima(0)
            prepare(1, 1, 2, 0)
            iteration(0, 0, 0, True, True)
            iteration(1, 1, 0, True, True)
            with eng.Fori(1, B // 2 - 1) as i:
                iteration(i * 2, 0, i, True, True)
                iteration(i * 2 + 1, 1, i, True, True)
            iteration(B - 2, 0, B // 2 - 1, True, False)
            iteration(B - 1, 1, B // 2 - 1, False, False)
            for q in range(2):
                for n in range(JOBS):
                    if not q:
                        after_job(B, q, n)
                    tail(B // 2 - 1, q, n)

        def first(b):
            return isinstance(b, int) and b < 1

        def over(b):
            return isinstance(b, int) and b >= B

        @block.sync
        def _(sp):
            sp.wait_ge(zeroed, 5)
            sp.dma_start(w_hl[:, :], d["exp_hl"]).then_inc(loaded, 16)
            sp.dma_start(b_hl[:, :], d["exp_hl_b"]).then_inc(loaded, 16)
            sp.dma_start(b_fc1[:, :], d["exp_fc1_b"]).then_inc(loaded, 16)
            sp.dma_start(w_fgate[:, :], d["exp_fgate"]).then_inc(loaded, 16)
            sp.dma_start(row[:, :], d["exp_fc2_b"]).then_inc(loaded, 16)
            for j in range(J):
                sp.dma_start(b_gate[:, j, :], d["exp_gate_b"]).then_inc(loaded, 16)
            sp.dma_start(norms[:, :, :], d["exp_norms"]).then_inc(loaded, 16)
            for h in range(H):
                r = slice(h * HD, (h + 1) * HD)
                sp.dma_start(w_q[r, :, r], d["exp_q"][h]).then_inc(loaded, 16)
                sp.dma_start(w_kv[r, :, r], d["exp_kv"][h]).then_inc(loaded, 16)
                sp.dma_start(w_gate[r, :, h * E:(h + 1) * E], d["exp_gate"][h]).then_inc(loaded, 16)
                sp.dma_start(w_fc[r, :, r], d["exp_fc"]).then_inc(loaded, 16)
            sp.wait_ge(parts_done, 5)
            for n in range(3):
                sp.dma_start(bias3[n:n + 1, :], row_parts[:, n, :]).then_inc(parts_moved, 16)
            with sp.Fori(0, B // 2) as i:
                sp.wait_ge(t["x_ready"], i + 1)
                sp.dma_start(out[bass.ds(i * 2, 2)].rearrange("b (j p) d -> p b j d", p=P),
                             x[:, bass.ds(i * 2 * J, 2 * J), :].rearrange("p (b j) d -> p b j d", j=J))\
                  .then_inc(stored, 16)
            sp.wait_ge(stored, 16 * (B // 2))

        LOADED = 16 * (6 + J + 4 * H)
        MASKS = 8 + 2 * H

        @block.tensor
        def _(pe):
            pe.wait_ge(loaded, LOADED)
            pe.wait_ge(parts_moved, 16 * 3)
            pe.wait_ge(masks, MASKS)
            pe.wait_ge(built, 1)

            for n in range(H):
                pe.wait_ge(resid_in, 3 * n + 1)
                for j in range(J):
                    last = pe.transpose(p_in[:, j * P:(j + 1) * P], xn[:, n % 2, j, :], ident[:, :])
                last.then_inc(resid_out, 1)
                pe.wait_ge(resid_in, 3 * n + 2)
                pe.matmul(p_in[:, N:2 * N], w_hl[:, :], xT[:, :], start=True, stop=True).then_inc(resid_out, 1)
            pe.wait_ge(resid_in, 3 * H)
            for j in range(J):
                last = pe.transpose(p_in[:, j * P:(j + 1) * P], residT[:, j * P:(j + 1) * P], ident[:, :])
            last.then_inc(resid_out, 1)
            pe.wait_ge(resid_ready, 1)

            def prepare(b, q, part, tails):
                if part == 0:
                    pe.wait_ge(s["xn_ready"], b + 1)
                    after(pe, t["foT_ready" if q else "fxT_ready"], tails)
                    for j in range(J):
                        last = pe.transpose(p_in[:, j * P:(j + 1) * P], xn[:, q, j, :], ident[:, :])
                    last.then_inc(s["xT_psum"], 1)
                elif part == 1:
                    pe.wait_ge(s["xT_ready"], b + 1)
                    pe.matmul(p_in[:, N:2 * N], w_hl[:, :], xT[:, :], start=True, stop=True).then_inc(s["sx_psum"], 1)
                else:
                    pe.wait_ge(s["sx_ready"], b + 1)
                    after(pe, s["kv_ready"], b)
                    if q:
                        after(pe, t["f_low"], tails)
                    pe.matmul(p_kv[:, 0:N], w_kv[:, 0, :], sxT[:, q, :], start=True, stop=True)
                    for j in range(J):
                        last = pe.matmul(p_kv[:, N + j * D:N + (j + 1) * D], sxT[:, q, j * P:(j + 1) * P], w_kv[:, 1, :],
                                         start=True, stop=True)
                    last.then_inc(s["kv_psum"], 1)
                    after(pe, s["top_ready"], b * JOBS)
                    for e in range(E):
                        last = pe.matmul(p_s[:, e // 2, (e % 2) * N:(e % 2 + 1) * N], w_q[:, e, :], sxT[:, q, :],
                                         start=True, stop=True)
                    last.then_inc(s["q_psum"], 1)

            def turn_maxima(b):
                if not (isinstance(b, int) and b >= B - 1):
                    pe.wait_ge(s["sx_ready"], b + 2)
                pe.wait_ge(s["top2_ready"], b + 1)
                for j in range(J):
                    last = pe.transpose(p_in[:, j * (P // 2):(j + 1) * (P // 2)].bitcast(BF16),
                                        top2[:, j, :, :].rearrange("p h c -> p (h c)"), ident16[:, :])
                last.then_inc(s["topT_psum"], 1)

            def job(b, q, n, top):
                h = n % H
                if not (isinstance(b, int) and b < 0):
                    frm, to = ROUNDS[n // H]
                    if n == 0:
                        pe.wait_ge(s["topT_ready"], b + 1)
                    after(pe, s["weighed"], b * JOBS + n - 1)
                    bank = p_t[:, n % 2, :]
                    if frm == to:
                        pe.matmul(bank.rearrange("p (e c) -> p e c", e=E), ident16[:, :],
                                  above[:, :].rearrange("p (o c) -> p o c", o=1).broadcast_to([P, E, P]),
                                  start=True, stop=False, skip_group_check=True)
                    for e in range(E):
                        pe.matmul(bank[:, e * P:(e + 1) * P], pick[:, h, e, :], topT[:, to * P:(to + 1) * P],
                                  start=e == 0 and frm != to, stop=False, skip_group_check=True)
                    pe.matmul(bank, kT[:, q, h, frm * P:(frm + 1) * P], qT[:, q, :, to * P:(to + 1) * P], start=False,
                              stop=True, skip_group_check=True).then_inc(s["t_psum"], 1)
                if top:
                    to, first, count = TOP_ROUNDS[n // H]
                    cols = P * (to + 1)
                    if n == 0:
                        pe.wait_ge(s["round_ready"], b + 2)
                    after(pe, s["top_ready"], (b + 1) * JOBS + n - 1)
                    bank = p_s[:, n % 2, :]
                    for e in range(count):
                        pe.matmul(bank[:, e * cols:(e + 1) * cols], q_round[:, first + e, to * P:(to + 1) * P],
                                  k_round[:, h, 0:cols], start=e == 0, stop=False, skip_group_check=True)
                    pe.matmul(bank.rearrange("p (e c) -> p e c", e=count)[:, :, cols - P:cols], ident16[:, :],
                              below[:, :].rearrange("p (o c) -> p o c", o=1).broadcast_to([P, count, P]),
                              start=False, stop=True, skip_group_check=True).then_inc(s["s_psum"], 1)

            def after_job(b, q, n):
                if n == 1 and not first(b):
                    pe.wait_ge(s["out_ready"], b * 2)
                    pe.wait_ge(s["sums_kept"], b * 2)
                    for j in range(J):
                        for e in range(E):
                            a = (j * E + e) * H * E
                            pe.matmul(p_in[:, a:a + H * E], outT[:, j, e, :], w_gate[:, e, :], start=True, stop=True)
                    for j in range(J):
                        for e in range(E):
                            a = J * E * H * E + (j * E + e) * H
                            last = pe.matmul(p_in[:, a:a + H], sumsT[:, j, e, :], head_row[:, :], start=True,
                                             stop=True)
                    last.then_inc(s["gate_psum"], 1)
                    for j in range(J):
                        for e in range(E):
                            last = pe.transpose(p_v[:, j, e * P:(e + 1) * P], outT[:, j, e, :], ident[:, :])
                    last.then_inc(s["tok_psum"], 1)
                if n == 6 and not over(b):
                    for part in range(2):
                        values(b, q, 0, part)

            def values(b, q, to, part):
                if part == 0:
                    rounds = (1, 2) if to else (0,)
                    pe.wait_ge(s["weighed"], b * JOBS + (JOBS if to else H))
                    if to:
                        pe.wait_ge(s["out_ready"], b * 2 + 1)
                        pe.wait_ge(s["sums_kept"], b * 2 + 1)
                    else:
                        after(pe, s["prod_ready"], b * J)
                else:
                    rounds = (1, 2) if to else (0,)
                for n in rounds:
                    for h in range(H):
                        cols = slice(h * HD, (h + 1) * HD)
                        stat = c["ones"][:, 0:HD] if part else v[:, q, n // 2, cols]
                        last = pe.matmul(p_v[cols, part, :], stat, wT[:, n, h, :], start=n == rounds[0],
                                         stop=n == rounds[-1], tile_position=(0, h * HD), skip_group_check=True)
                last.then_inc(s["values_psum"], 1)

            def tail(i, q, n):
                if (q, n) == (0, 10):
                    pe.wait_ge(s["g_low"], i * 2 + 2)
                    pe.wait_ge(t["fx_ready"], i + 1)
                    for a in range(2 * J):
                        last = pe.transpose(p_in[:, a * P:(a + 1) * P],
                                            fx[:, a * H:(a + 1) * H, :].rearrange("p h c -> p (h c)"), ident[:, :])
                    last.then_inc(t["fxT_psum"], 1)
                if (q, n) == (1, 0):
                    pe.wait_ge(t["fxT_ready"], i + 1)
                    pe.matmul(p_kv[:, :], w_fc[:, 0, :], fxT[:, :], start=True, stop=True).then_inc(t["fc1_psum"], 1)
                if (q, n) == (1, 2):
                    pe.wait_ge(t["fc1n_ready"], i + 1)
                    for a in range(2 * J):
                        part = p_kv[:, a * D:(a + 1) * D]
                        pe.matmul(part, c["ones3"][:, :], bias3[:, :], start=True, stop=False,
                                  skip_group_check=True)
                        last = pe.matmul(part, fc1n[:, a * P:(a + 1) * P], w_fc[:, 1, :], start=False, stop=True,
                                         skip_group_check=True)
                    last.then_inc(t["fc2_psum"], 1)
                if (q, n) == (1, 9):
                    pe.wait_ge(t["fout_ready"], i + 1)
                    for a in range(2 * J):
                        last = pe.transpose(p_in[:, a * P:(a + 1) * P],
                                            fout[:, a * H:(a + 1) * H, :].rearrange("p h c -> p (h c)"), ident[:, :])
                    last.then_inc(t["foT_psum"], 1)
                if (q, n) == (1, 10):
                    pe.wait_ge(t["foT_ready"], i + 1)
                    for a in range(2 * J):
                        last = pe.matmul(p_kv[:, a * H:(a + 1) * H], foT[:, a * P:(a + 1) * P], w_fgate[:, :],
                                         start=True, stop=True)
                    last.then_inc(t["f_psum"], 1)

            every(pe, prepare, turn_maxima, job, after_job, values, tail)

        @block.scalar
        def _(act):
            ln_act(act)
            act.wait_ge(loaded, LOADED)
            act.wait_ge(masks, MASKS)
            for n in range(H):
                r = slice(n * HD, (n + 1) * HD)
                act.wait_ge(resid_out, 2 * n + 1)
                act.activation(xT[:, :], p_in[:, 0:N], ACT.Copy).then_inc(resid_in, 1)
                act.wait_ge(resid_out, 2 * n + 2)
                act.activation(residT[r, :], p_in[r, N:2 * N], ACT.Identity, bias=b_hl[r, :]).then_inc(resid_in, 1)
            act.wait_ge(resid_out, 2 * H + 1)
            act.activation(resid[:, :, :].rearrange("p j d -> p (j d)"), p_in[:, 0:N], ACT.Copy).then_inc(resid_ready, 1)

            def prepare(b, q, part, tails):
                if part == 0:
                    act.wait_ge(s["xT_psum"], b + 1)
                    act.activation(xT[:, :], p_in[:, 0:N], ACT.Copy).then_inc(s["xT_ready"], 1)
                elif part == 1:
                    act.wait_ge(s["sx_psum"], b + 1)
                    act.activation(sxT[:, q, :], p_in[:, N:2 * N], ACT.Identity, bias=b_hl[:, 0:1])\
                       .then_inc(s["sx_ready"], 1)
                else:
                    act.wait_ge(s["kv_psum"], b + 1)
                    for h in range(H):
                        r = slice(h * HD, (h + 1) * HD)
                        act.activation(kT[r, q, h, :], p_kv[r, 0:N], ACT.Copy)
                    act.activation(v[:, q, :, :].rearrange("p j d -> p (j d)"), p_kv[:, N:2 * N], ACT.Copy)\
                       .then_inc(s["kv_ready"], 1)
                    act.wait_ge(s["q_psum"], b + 1)
                    act.activation(qT[:, q, :, :].rearrange("p e n -> p (e n)"),
                                   p_s[:, :, :].rearrange("p a n -> p (a n)"), ACT.Copy).then_inc(s["q_ready"], 1)

            def turn_maxima(b):
                act.wait_ge(s["topT_psum"], b + 1)
                act.activation(topT[:, :], p_in[:, 0:P].bitcast(BF16), ACT.Copy).then_inc(s["topT_ready"], 1)

            def job(b, q, n, top):
                if isinstance(b, int) and b < 0:
                    return
                if n == 0:
                    after(act, s["values_psum"], b * 4)
                act.wait_ge(s["t_psum"], b * JOBS + n + 1)
                act.activation(wT[:, n // H, n % H, :], p_t[:, n % 2, :], ACT.Exp, scale=HD ** 0.5)\
                   .then_inc(s["weighed"], 1)

            def keep_sums(b, to):
                act.wait_ge(s["values_psum"], b * 4 + to * 2 + 2)
                after(act, s["gate_psum"], b)
                act.activation(sumsT[:, to, :, :].rearrange("p e c -> p (e c)"), p_v[:, 1, :], ACT.Copy)\
                   .then_inc(s["sums_kept"], 1)

            def after_job(b, q, n):
                if n == 7 and not over(b):
                    keep_sums(b, 0)
                if n == 3 and not first(b):
                    act.wait_ge(s["g_low"], b)
                    act.activation(g_exp[:, :, :], g_low[:, :, :], ACT.Exp).then_inc(s["g_exp"], 1)

            def values(b, q, to, part):
                if part == 1:
                    keep_sums(b, to)

            def square(i, n):
                act.wait_ge(ns["mid"], i * 2 + n)
                act.activation(n_sq[:, :, :], n_mid[:, :, :], ACT.Square).then_inc(ns["sq"], 1)

            def tail(i, q, n):
                if (q, n) == (0, 6):
                    square(i, 1)
                if (q, n) == (0, 10):
                    act.wait_ge(t["fxT_psum"], i + 1)
                    act.activation(fxT[:, :], p_in[:, :], ACT.Copy).then_inc(t["fxT_ready"], 1)
                if (q, n) == (1, 0):
                    act.wait_ge(t["fc1_psum"], i + 1)
                    act.activation(fc1[:, :], p_kv[:, :], ACT.Relu, bias=b_fc1[:, 0:1]).then_inc(t["fc1_ready"], 1)
                if (q, n) == (1, 4):
                    square(i, 2)
                if (q, n) == (1, 9):
                    act.wait_ge(t["foT_psum"], i + 1)
                    act.activation(foT[:, :], p_in[:, :], ACT.Copy).then_inc(t["foT_ready"], 1)
                if (q, n) == (1, 11):
                    act.wait_ge(t["f_low"], i + 1)
                    act.activation(f_exp[:, :, :], f_low[:, :, :], ACT.Exp).then_inc(t["f_exp"], 1)

            every(act, prepare, turn_maxima, job, after_job, values, tail)

        @block.vector
        def _(dve):
            ln_dve(dve)
            dve.wait_ge(loaded, LOADED)
            split_rows(dve, row[:, :], row_work[:, :], [row_parts[:, n, :] for n in range(3)], parts_done)
            dve.wait_ge(norm_ready, 1)
            dve.wait_ge(masks, MASKS)
            dve.tensor_copy(ident16[:, :], ident[:, :]).then_inc(built, 1)

            def normalise(q, b):
                for j in range(J):
                    a = b * J + j
                    last = dve.tensor_scalar(xn[:, q, j, :], x[:, a, :], c["rstd"][:, bass.ds(a, 1)],
                                             c["shift"][:, bass.ds(a, 1)], ALU.mult, ALU.add)
                return last

            for n in range(H):
                if n >= 2:
                    dve.wait_ge(resid_out, 2 * (n - 2) + 1)
                if n:
                    dve.wait_ge(resid_in, 3 * n)
                normalise(n % 2, n).then_inc(resid_in, 1)
            dve.wait_ge(resid_ready, 1)

            def normalise_ahead(b, q):
                after(dve, s["xT_psum"], b - 1)
                normalise(q, b).then_inc(s["xn_ready"], 1)

            def prepare(b, q, part, tails):
                if part == 0 and isinstance(b, int) and b < 2:
                    normalise_ahead(b, q)
                elif part == 2:
                    dve.wait_ge(s["sx_ready"], b + 1)
                    dve.tensor_scalar(nonzero[:, q, :, :].rearrange("p j c -> p (j c)"), sxT[:, q, :], 0.0, None,
                                      ALU.not_equal).then_inc(s["nonzero_ready"], 1)
                    after(dve, s["s_psum"], b * JOBS)
                    dve.wait_ge(s["kv_ready"], b + 1)
                    dve.tensor_copy(k_round[:, :, :], kT[:, q, :, :])
                    dve.wait_ge(s["q_ready"], b + 1)
                    dve.tensor_copy(q_round[:, :, :], qT[:, q, :, :]).then_inc(s["round_ready"], 1)

            def turn_maxima(b):
                dve.wait_ge(s["top_ready"], (b + 1) * JOBS)
                high, low = [top2[:, :, :, n:2 * E:2].rearrange("p j h e -> p (j h) e") for n in range(2)]
                all_top = top[:, :, :, :].rearrange("p j h e -> p (j h) e")
                after(dve, s["topT_psum"], b)
                dve.tensor_copy(high, all_top).then_inc(s["top2_half"], 1)
                dve.wait_ge(s["top2_half"], b + 1)
                dve.tensor_tensor(low, all_top, high, ALU.subtract).then_inc(s["top2_ready"], 1)

            def job(b, q, n, top_too):
                if not top_too:
                    return
                to, first, count = TOP_ROUNDS[n // H]
                dve.wait_ge(s["s_psum"], (b + 1) * JOBS + n + 1)
                dve.tensor_reduce(top[:, to, n % H, first:first + count],
                                  p_s[:, n % 2, :].rearrange("p (e c) -> p e c", e=count), AX.X, ALU.max)\
                   .then_inc(s["top_ready"], 1)

            def outputs(b, q, to):
                dve.wait_ge(s["nonzero_ready"], b + 1)
                dve.wait_ge(s["values_psum"], b * 4 + to * 2 + 1)
                dve.tensor_tensor(outT[:, to, :, :], p_v[:, 0, :].rearrange("p (e c) -> p e c", e=E),
                                  nonzero[:, q, to:to + 1, :].broadcast_to([P, E, P]), ALU.mult)\
                   .then_inc(s["out_ready"], 1)

            def values(b, q, to, part):
                if part == 1:
                    outputs(b, q, to)

            def after_job(b, q, n):
                if n == 7 and not over(b):
                    outputs(b, q, 0)
                if n == 8 and not (isinstance(b, int) and b >= B - 2):
                    normalise_ahead(b + 2, q)
                if first(b):
                    return
                if n == 2:
                    dve.wait_ge(s["gate_psum"], b)
                    flat = J * E * H
                    dve.reciprocal(z_over[:, :], p_in[:, flat * E:flat * (E + 1)]).then_inc(s["z_over"], 1)
                    dve.wait_ge(s["z_over"], b)
                    dve.tensor_tensor(z_norm[:, :, :, :].rearrange("p j e (h g) -> p (j e h) g", h=H),
                                      p_in[:, 0:flat * E].rearrange("p (a g) -> p a g", g=E),
                                      spread(z_over[:, :], E), ALU.mult).then_inc(s["z_norm"], 1)
                    dve.wait_ge(s["z_norm"], b)
                    dve.tensor_reduce(z_sum[:, :, :], z_norm[:, :, :, :].rearrange("p j e a -> p j a e"), AX.X,
                                      ALU.add).then_inc(s["z_sum"], 1)
                    dve.wait_ge(s["z_sum"], b)
                    dve.tensor_tensor(logits[:, :, :], z_sum[:, :, :], b_gate[:, :, :], ALU.add)\
                       .then_inc(s["logits"], 1)
                    dve.wait_ge(s["logits"], b)
                    gate = logits[:, :, :].rearrange("p j (h g) -> p (j h) g", h=H)
                    dve.tensor_reduce(g_top[:, :], gate, AX.X, ALU.max).then_inc(s["g_top"], 1)
                    dve.wait_ge(s["g_top"], b)
                    dve.tensor_tensor(g_low[:, :, :], gate, spread(g_top[:, :], E), ALU.subtract).then_inc(s["g_low"], 1)
                if n == 4:
                    dve.wait_ge(s["g_exp"], b)
                    dve.tensor_reduce(g_sum[:, :], g_exp[:, :, :], AX.X, ALU.add).then_inc(s["g_sum"], 1)
                    dve.wait_ge(s["g_sum"], b)
                    dve.reciprocal(g_over[:, :], g_sum[:, :]).then_inc(s["g_over"], 1)
                    dve.wait_ge(s["g_over"], b)
                    dve.tensor_tensor(g_w[:, :, :], g_exp[:, :, :], spread(g_over[:, :], E), ALU.mult)\
                       .then_inc(s["g_w"], 1)
                    dve.wait_ge(s["g_w"], b)
                    for j in range(J):
                        last = dve.tensor_tensor(g_scaled[:, j * H:(j + 1) * H, :], g_w[:, j * H:(j + 1) * H, :],
                                                 z_over[:, j * E * H:(j + 1) * E * H].rearrange("p (e h) -> p h e", h=H),
                                                 ALU.mult)
                    last.then_inc(s["g_scaled"], 1)
                    dve.wait_ge(s["tok_psum"], b)
                    dve.wait_ge(s["g_scaled"], b)
                    for j in range(J):
                        for e in range(E):
                            last = dve.tensor_tensor(prod[:, j, e, :].rearrange("p (h c) -> p h c", h=H),
                                                     p_v[:, j, e * P:(e + 1) * P].rearrange("p (h c) -> p h c", h=H),
                                                     g_scaled[:, j * H:(j + 1) * H, e:e + 1].broadcast_to([P, H, HD]),
                                                     ALU.mult)
                        last.then_inc(s["prod_ready"], 1)
                if n == 5:
                    dve.wait_ge(s["prod_ready"], b * J)
                    dve.tensor_reduce(mixed[:, :, :], prod[:, :, :, :].rearrange("p j e c -> p j c e"), AX.X, ALU.add)\
                       .then_inc(s["mixed_ready"], 1)
                    dve.wait_ge(s["mixed_ready"], b)
                    dve.tensor_tensor(u[:, 1 - q, :, :], mixed[:, :, :], resid[:, :, :], ALU.add)\
                       .then_inc(s["u_ready"], 1)

            def norm(i, n, src, part):
                k = i * 2 + n
                if part == 0:
                    dve.tensor_reduce(n_sum[:, :], src, AX.X, ALU.add).then_inc(ns["sum"], 1)
                    dve.wait_ge(ns["sum"], k)
                    dve.tensor_scalar(n_mean[:, :], n_sum[:, :], 1.0 / HD, None, ALU.mult).then_inc(ns["mean"], 1)
                    dve.wait_ge(ns["mean"], k)
                    dve.tensor_tensor(n_mid[:, :, :], src, spread(n_mean[:, :], HD), ALU.subtract)\
                       .then_inc(ns["mid"], 1)
                if part == 1:
                    dve.wait_ge(ns["sq"], k)
                    dve.tensor_reduce(n_ss[:, :], n_sq[:, :, :], AX.X, ALU.add).then_inc(ns["ss"], 1)
                    dve.wait_ge(ns["ss"], k)
                    dve.tensor_scalar(n_var[:, :], n_ss[:, :], 1.0 / HD, NORM_EPS, ALU.mult, ALU.add)\
                       .then_inc(ns["var"], 1)
                if part == 2:
                    dve.wait_ge(ns["rstd"], k)
                    dve.tensor_tensor(n_unit[:, :, :], n_mid[:, :, :], spread(n_rstd[:, :], HD), ALU.mult)\
                       .then_inc(ns["unit"], 1)

            def tail(i, q, n):
                groups = u[:, :, :, :].rearrange("p q j (h c) -> p (q j h) c", h=H)
                flat = "p g c -> p (g c)"
                if (q, n) == (0, 5):
                    dve.wait_ge(s["u_ready"], i * 2 + 2)
                    norm(i, 1, groups, 0)
                if (q, n) == (0, 6):
                    norm(i, 1, groups, 1)
                if (q, n) == (0, 9):
                    norm(i, 1, groups, 2)
                if (q, n) == (1, 1):
                    dve.wait_ge(t["fc1_ready"], i + 1)
                    dve.scalar_tensor_tensor(fc1n[:, :], fxT[:, :], 0.0, fc1[:, :], ALU.not_equal, ALU.mult)\
                       .then_inc(t["fc1n_ready"], 1)
                if (q, n) == (1, 3):
                    dve.wait_ge(t["fc2_psum"], i + 1)
                    dve.scalar_tensor_tensor(fc2[:, :, :].rearrange(flat), fx[:, :, :].rearrange(flat), 0.0, p_kv[:, :],
                                             ALU.not_equal, ALU.mult).then_inc(t["fc2_kept"], 1)
                    dve.wait_ge(t["fc2_kept"], i + 1)
                    dve.tensor_tensor(u2[:, :, :], fc2[:, :, :], fx[:, :, :], ALU.add).then_inc(t["u2_ready"], 1)
                    dve.wait_ge(t["u2_ready"], i + 1)
                    norm(i, 2, u2[:, :, :], 0)
                if (q, n) == (1, 4):
                    norm(i, 2, u2[:, :, :], 1)
                if (q, n) == (1, 7):
                    norm(i, 2, u2[:, :, :], 2)
                if (q, n) == (1, 10):
                    logits = p_kv[:, 0:2 * J * H].rearrange("p (a h) -> p a h", h=H)
                    dve.wait_ge(t["f_psum"], i + 1)
                    dve.tensor_reduce(f_top[:, :], logits, AX.X, ALU.max).then_inc(t["f_top"], 1)
                    dve.wait_ge(t["f_top"], i + 1)
                    dve.tensor_tensor(f_low[:, :, :], logits, spread(f_top[:, :], H), ALU.subtract)\
                       .then_inc(t["f_low"], 1)
                if (q, n) == (1, 11):
                    dve.wait_ge(t["f_exp"], i + 1)
                    dve.tensor_reduce(f_sum[:, :], f_exp[:, :, :], AX.X, ALU.add).then_inc(t["f_sum"], 1)
                    dve.wait_ge(t["f_sum"], i + 1)
                    dve.reciprocal(f_over[:, :], f_sum[:, :]).then_inc(t["f_over"], 1)
                    dve.wait_ge(t["f_over"], i + 1)
                    dve.tensor_tensor(f_w[:, :].rearrange("p (a h) -> p a h", h=H), f_exp[:, :, :],
                                      spread(f_over[:, :], H), ALU.mult).then_inc(t["f_w"], 1)
                    dve.wait_ge(t["f_w"], i + 1)
                    dve.tensor_tensor(gated[:, :, :], fout[:, :, :], spread(f_w[:, :], HD), ALU.mult)\
                       .then_inc(t["gated_ready"], 1)

            every(dve, prepare, turn_maxima, job, after_job, values, tail)

        @block.gpsimd
        def _(pool):
            for a in (w_q, w_kv, w_gate, w_fc):
                pool.memset(a[:, :, :], 0.0).then_inc(zeroed, 1)
            pool.memset(head_row[:, :], 0.0).then_inc(zeroed, 1)
            pool.wait_ge(zeroed, 5)
            pool.memset(below[:, :], 0.0).then_inc(masks, 1)
            pool.memset(above[:, :], 0.0).then_inc(masks, 1)
            pool.memset(top2[:, :, :, :], 0.0).then_inc(masks, 1)
            pool.memset(pick[:, :, :, :], 0.0).then_inc(masks, 1)
            pool.memset(kT[:, :, :, :], 0.0).then_inc(masks, 1)
            pool.wait_ge(masks, 5)
            pool.affine_select(out=below[:, :], in_=below[:, :], compare_op=ALU.is_ge, fill=MASKED, base=0,
                               pattern=[[-1, P]], channel_multiplier=1).then_inc(masks, 1)
            pool.affine_select(out=above[:, :], in_=above[:, :], compare_op=ALU.is_ge, fill=MASKED, base=0,
                               pattern=[[1, P]], channel_multiplier=-1).then_inc(masks, 1)
            for k in range(2 * H):
                h, n = divmod(k, 2)
                pool.wait_ge(masks, 7 + k)
                pool.affine_select(out=pick[:, h, :, :], in_=pick[:, h, :, :], compare_op=ALU.not_equal, fill=-1.0,
                                   base=-n - h * HD, pattern=[[-2, E], [0, P]], channel_multiplier=1).then_inc(masks, 1)
            pool.affine_select(out=head_row[:, :], in_=head_row[:, :], compare_op=ALU.not_equal, fill=1.0, base=0,
                               pattern=[[-HD, H]], channel_multiplier=1).then_inc(masks, 1)
            pool.wait_ge(resid_ready, 1)
            pool.wait_ge(loaded, LOADED)

            def nothing(*_):
                pass

            def close_norm(i, n, dst, done):
                k = i * 2 + n
                pool.wait_ge(ns["var"], k)
                pool.tensor_tensor(n_rstd[:, :], n_var[:, :], c["minus_half"][:, 0:PG], ALU.pow).then_inc(ns["rstd"], 1)
                pool.wait_ge(ns["unit"], k)
                gain = norms[:, 2 * n - 2:2 * n - 1, :].broadcast_to([P, PG, HD])
                offset = norms[:, 2 * n - 1:2 * n, :].broadcast_to([P, PG, HD])
                pool.tensor_tensor(n_gain[:, :, :], n_unit[:, :, :], gain, ALU.mult).then_inc(ns["gain"], 1)
                pool.wait_ge(ns["gain"], k)
                pool.tensor_tensor(dst, n_gain[:, :, :], offset, ALU.add).then_inc(done, 1)

            def tail(i, q, n):
                if (q, n) == (0, 6):
                    close_norm(i, 1, fx[:, :, :], t["fx_ready"])
                if (q, n) == (1, 4):
                    close_norm(i, 2, fout[:, :, :], t["fout_ready"])
                if (q, n) == (1, 11):
                    pool.wait_ge(t["gated_ready"], i + 1)
                    xi = x[:, bass.ds(i * 2 * J, 2 * J), :]
                    pool.tensor_tensor(xi, xi, gated[:, :, :].rearrange("p (a h) c -> p a (h c)", h=H), ALU.add)\
                        .then_inc(t["x_ready"], 1)

            every(pool, nothing, nothing, nothing, nothing, nothing, tail)


STAGES = [stage_gated_conv, stage_recurrent, stage_graph_attention]
LAST = stage_expert_attention


def more(inputs, row, col, wide):
    import numpy as _np

    return {
        "ffn_w": inputs["L0_ffn_W"].T, "ffn_b": row("L0_ffn_b"),
        "ffn_ln_w": col("L0_ffn_ln_w"), "ffn_ln_b": col("L0_ffn_ln_b"),
        "att_lin": inputs["L1_gnn_W_lin"], "att_q": inputs["L1_gnn_W_q"], "att_k": inputs["L1_gnn_W_k"],
        "att_b": row("L1_gnn_b_lin"), "att_g": wide("L1_gnn_ln_g"), "att_o": wide("L1_gnn_ln_b"),
        "exp_hl": inputs["L1_ffn_hl_w"].reshape(D, D).T, "exp_hl_b": col("L1_ffn_hl_b"),
        "exp_q": inputs["L1_ffn_wq"].transpose(0, 3, 1, 2),
        "exp_kv": _np.stack([inputs["L1_ffn_wk"], inputs["L1_ffn_wv"]]).transpose(1, 3, 0, 2),
        "exp_gate": inputs["L1_ffn_gate_w"].reshape(H, E, E, HD).transpose(0, 3, 2, 1),
        "exp_gate_b": wide("L1_ffn_gate_b"), "exp_fc2_b": _np.concatenate([row("L1_ffn_fc2_b")] * H, axis=1),
        "exp_norms": _np.broadcast_to(_np.stack([inputs[f"L1_ffn_{n}"] for n in ("ln_g", "ln_b", "fnorm_g", "fnorm_b")]),
                                      (P, 4, HD)),
        "exp_fc": _np.stack([inputs["L1_ffn_fc1_w"], inputs["L1_ffn_fc2_w"]]).transpose(2, 0, 1),
        "exp_fc1_b": _np.concatenate([col("L1_ffn_fc1_b")] * H),
        "exp_fgate": inputs["L1_ffn_fgate_w"].T,
    }


def program(nc, d, out):
    with ExitStack() as ctx:
        def sb(n, s, t=F32):
            return ctx.enter_context(nc.sbuf_tensor(n, s, t))

        c = {
            "x": sb("x", [P, TILES, D]), "ident": sb("ident", [P, P]), "ones": sb("ones", [P, P]),
            "ones3": sb("ones3", [3, P], BF16), "minus_half": sb("minus_half", [P, 16]),
            "x_stats": sb("x_stats", [P, TILES, 2]), "rstd": sb("rstd", [P, TILES]), "shift": sb("shift", [P, TILES]),
        }
        stage_setup(nc, d, c)
        for stage in STAGES:
            stage(nc, d, c)
        LAST(nc, d, c, out)


def kernel(**inputs):
    import numpy as _np
    import concourse.bacc as _bacc
    from concourse import mybir as _mybir
    from concourse.bass_utils import run_bass_kernel_spmd as _run

    def row(name):
        return inputs[name].reshape(1, -1)

    def col(name):
        return inputs[name].reshape(-1, 1)

    def wide(name):
        return _np.broadcast_to(inputs[name].reshape(1, -1), (P, inputs[name].size))

    data = {
        "x": inputs["x"], "adj": inputs["adj"],
        "conv1": inputs["L0_gnn_conv1_w"][:, :, 0].T, "conv2": inputs["L0_gnn_conv2_w"].transpose(1, 2, 0),
        "wmsg": inputs["L0_gnn_w_msg"].T, "wih": inputs["L0_gnn_w_ih"].T, "whh": inputs["L0_gnn_w_hh"].T,
        "wse": inputs["L0_gnn_w_se"].T, "bse": col("L0_gnn_b_se"),
        "bih": row("L0_gnn_b_ih"), "bhh": row("L0_gnn_b_hh"), "bmsg": row("L0_gnn_b_msg"),
    }
    for n in ("bn1", "bn2"):
        for v in "gbmv":
            data[f"{n}_{v}"] = col(f"L0_gnn_{n}_{v}")
    data |= more(inputs, row, col, wide)
    nc = _bacc.Bacc("TRN2", target_bir_lowering=False, num_devices=1)
    arrays, d = {}, {}
    for name, a in data.items():
        a = _np.ascontiguousarray(a)
        arrays[f"in_{name}"] = a
        d[name] = nc.dram_tensor(f"in_{name}", a.shape, _mybir.dt.from_np(a.dtype), kind="ExternalInput").ap()
    out = nc.dram_tensor("out_0", (B, N, D), F32, kind="ExternalOutput").ap()
    program(nc, d, out)
    return _run(nc, [arrays], core_ids=[0]).results[0]["out_0"]
```

```python
from contextlib import ExitStack, contextmanager

import concourse.bass as bass
from concourse import mybir

ALU = mybir.AluOpType
ACT = mybir.ActivationFunctionType
AX = mybir.AxisListType
F32 = mybir.dt.float32
BF16 = mybir.dt.bfloat16
F32R = mybir.dt.float32r

P = 128
B = 32
N = 256
D = 128
J = N // P
TILES = B * J
TAPS = 17
PAD = TAPS // 2
SE = 3
STEPS = 30
H = 4
HD = D // H
E = 4
LN_EPS = 1e-5
NORM_EPS = 1e-8


@contextmanager
def stage_semaphores(nc, prefix):
    made = []

    def sem(name):
        made.append(nc.alloc_semaphore(name=prefix + name))
        return made[-1]

    yield sem
    nc.clear_and_free_semaphores(made)
    nc.all_engine_barrier()


def outer_norm(nc, ctx, sem, x_stats, rstd, shift, name):
    std = ctx.enter_context(nc.sbuf_tensor(f"{name}_std", [P, TILES], F32))
    eps = ctx.enter_context(nc.sbuf_tensor(f"{name}_eps", [P, 1], F32))
    eps_set, std_done, rstd_done, norm_ready = (
        sem(f"ln_{n}") for n in ("eps_set", "std_done", "rstd_done", "ready"))

    def on_scalar(act):
        act.wait_ge(eps_set, 1)
        act.activation(std[:, :], x_stats[:, :, 1], ACT.Sqrt, bias=eps[:, 0:1]).then_inc(std_done, 1)

    def on_vector(dve):
        dve.memset(eps[:, :], LN_EPS).then_inc(eps_set, 1)
        dve.wait_ge(std_done, 1)
        dve.reciprocal(rstd[:, :], std[:, :]).then_inc(rstd_done, 1)
        dve.wait_ge(rstd_done, 1)
        dve.scalar_tensor_tensor(shift[:, :], x_stats[:, :, 0], -1.0, rstd[:, :], ALU.mult, ALU.mult)\
           .then_inc(norm_ready, 1)

    return on_scalar, on_vector, norm_ready


def after(eng, sem, count):
    if not (isinstance(count, int) and count < 1):
        eng.wait_ge(sem, count)


def keep_stats(dve, c, b, mean_var):
    return dve.tensor_scalar(c["x_stats"][:, bass.ds(b * J, J), :], mean_var, 1.0, None, ALU.mult)


def stage_setup(nc, d, c):
    CHUNKS = 4
    PER = B // CHUNKS
    with ExitStack() as ctx:
        def sb(n, s, t=F32):
            return ctx.enter_context(nc.sbuf_tensor(n, s, t))

        sem = ctx.enter_context(stage_semaphores(nc, "setup_"))
        x_loaded = [sem(f"x_loaded{k}") for k in range(CHUNKS)]
        ident_zeroed, ident_done, ones_done = sem("ident_zeroed"), sem("ident_done"), sem("ones_done")
        stats_half, stats_kept = sem("stats_half"), sem("stats_kept")
        bn6 = sb("setup_bn6", [P, TILES, 6])
        block = ctx.enter_context(nc.Block())

        @block.sync
        def _(sp):
            for k in range(CHUNKS):
                sp.dma_start(c["x"][:, k * PER * J:(k + 1) * PER * J, :].rearrange("p (b j) d -> p b j d", j=J),
                             d["x"][k * PER:(k + 1) * PER].rearrange("b (j p) d -> p b j d", p=P))\
                  .then_inc(x_loaded[k], 16)

        @block.gpsimd
        def _(pool):
            pool.memset(c["ident"][:, :], 0.0).then_inc(ident_zeroed, 1)
            pool.wait_ge(ident_zeroed, 1)
            pool.affine_select(out=c["ident"][:, :], in_=c["ident"][:, :], compare_op=ALU.not_equal, fill=1.0,
                               base=0, pattern=[[-1, P]], channel_multiplier=1).then_inc(ident_done, 1)
            pool.wait_ge(ident_done, 1)

        @block.vector
        def _(dve):
            dve.memset(c["ones"][:, :], 1.0).then_inc(ones_done, 1)
            dve.memset(c["ones3"][:, :], 1.0).then_inc(ones_done, 1)
            dve.memset(c["minus_half"][:, :], -0.5).then_inc(ones_done, 1)
            dve.wait_ge(ones_done, 3)
            for k in range(CHUNKS):
                dve.wait_ge(x_loaded[k], 16)
                tiles = range(k * PER * J, (k + 1) * PER * J)
                for t in tiles:
                    last = dve.bn_stats(bn6[:, t, :], c["x"][:, t, :])
                last.then_inc(stats_half, 1)
                dve.wait_ge(stats_half, k + 1)
                for t in tiles:
                    last = dve.bn_aggr(c["x_stats"][:, t, :], bn6[:, t, :])
                last.then_inc(stats_kept, 1)
            dve.wait_ge(stats_kept, CHUNKS)


def split_rows(dve, row, work, parts, done):
    dve.tensor_copy(parts[0], row).then_inc(done, 1)
    dve.wait_ge(done, 1)
    dve.tensor_tensor(work, row, parts[0], ALU.subtract).then_inc(done, 1)
    dve.wait_ge(done, 2)
    dve.tensor_copy(parts[1], work).then_inc(done, 1)
    dve.wait_ge(done, 3)
    dve.tensor_tensor(work, work, parts[1], ALU.subtract).then_inc(done, 1)
    dve.wait_ge(done, 4)
    dve.tensor_copy(parts[2], work).then_inc(done, 1)


def each(eng, batch):
    batch(0, 0)
    batch(1, 1)
    with eng.Fori(1, B // 2) as i:
        for q in range(2):
            batch(i * 2 + q, q)


DEPTH = 4


def pipelined(eng, step):
    for n in range(DEPTH + 1):
        step(n, n % DEPTH)
    with eng.Fori(1, B // DEPTH - 1) as i:
        for r in range(1, DEPTH + 1):
            step(i * DEPTH + r, r % DEPTH)
    for n in range(B - DEPTH + 1, B + DEPTH - 1):
        step(n, n % DEPTH)


def inside(b):
    return not isinstance(b, int) or 0 <= b < B


def adj_reached(b, r):
    return 16 * (b // 2 + 1) if isinstance(b, int) else (b - r) * 8 + 16 * (r // 2 + 1)


def stage_gated_conv(nc, d, c):
    G = 4 * D
    with ExitStack() as ctx:
        def sb(n, s, t=F32):
            return ctx.enter_context(nc.sbuf_tensor("g_" + n, s, t))

        def ps(n, s):
            return ctx.enter_context(nc.psum_tensor("g_" + n, s, F32))

        sem = ctx.enter_context(stage_semaphores(nc, "g_"))
        x, ident = c["x"], c["ident"]
        w1, w2 = sb("w1", [P, D]), sb("w2", [P, TAPS, D])
        wmsg, wih, whh, wse = sb("wmsg", [P, D]), sb("wih", [P, 2, 3 * D]), sb("whh", [P, 3 * D]), sb("wse", [P, SE])
        bse = sb("bse", [SE, 1])
        bn = sb("bn", [P, 2, 4])
        bn_work = sb("bn_work", [P, 2, 2])
        bn_scale, bn_shift = sb("bn_scale", [P, 2, 1]), sb("bn_shift", [P, 2, 1])
        eps = sb("eps", [P, 1])
        row = sb("row", [1, G + D])
        hidden_row = sb("hidden_row", [1, 3 * D])
        row_work = sb("row_work", [1, G + D])
        row_parts = sb("row_parts", [1, 3, G + D], BF16)
        bias3 = sb("bias3", [3, G + D], BF16)
        mhalf3, neg3 = sb("mhalf3", [SE, P]), sb("neg3", [SE, 1])

        xn = sb("xn", [P, DEPTH, J, D])
        xT = sb("xT", [P, 2, N])
        h1 = sb("h1", [P, 2, N + 2 * PAD])
        sT, s2T = sb("sT", [SE, 2, N]), sb("s2T", [SE, 2, N])
        nsq = sb("nsq", [P, 2, J])
        msg = sb("msg", [P, 2, J, D])
        adj = sb("adj", [P, 2, J, N])
        expo = sb("expo", [P, 2, J, N])
        aT = sb("aT", [P, 2, J, N])
        pre = sb("pre", [P, 2, N])
        convT = sb("convT", [P, 2, N])
        nmpT = sb("nmpT", [P, 2, N])
        rz = sb("rz", [P, 2, J, 2 * D])
        cand, cand2, nn = sb("cand", [P, 2, J, D]), sb("cand2", [P, 2, J, D]), sb("nn", [P, 2, J, D])
        diff, mix, upd = sb("diff", [P, 2, J, D]), sb("mix", [P, 2, J, D]), sb("upd", [P, 2, J, D])
        bn6, mean_var = sb("bn6", [P, 2, J, 6]), sb("mean_var", [P, J, 2])

        p_xT = ps("p_xT", [P, 512])
        p_h1 = ps("p_h1", [P, 512])
        p_adj = ps("p_adj", [P, 512])
        p_dist = ps("p_dist", [P, 512])
        p_conv = ps("p_conv", [P, 512])
        p_nmp = ps("p_nmp", [P, 512])
        p_gate = ps("p_gate", [P, J, 512])

        small_loaded, hidden_loaded, w_loaded = sem("small_loaded"), sem("hidden_loaded"), sem("w_loaded")
        parts_done, parts_moved, row_ready = sem("parts_done"), sem("parts_moved"), sem("row_ready")
        eps_set, bn_std, bn_ready, bn_steps, consts_set = (sem("eps_set"), sem("bn_std"), sem("bn_ready"),
                                                           sem("bn_steps"), sem("consts_set"))
        adj_loaded = [sem("adj_loaded0"), sem("adj_loaded1")]
        names = ("xn_ready xT_psum xT_ready h1_ready sT_psum sT_ready nsq_psum nsq_ready adj_psum "
                 "dist_psum expo_ready aT_ready msg_psum msg_ready conv_psum pre_ready conv_ready nmp_psum "
                 "nmp_ready gates_psum rz_ready cand_half cand_ready nn_ready diff_ready mix_ready "
                 "upd_ready x_ready stats_half stats_done stats_kept").split()
        s = {n: sem(n) for n in names}
        ln_act, ln_dve, norm_ready = outer_norm(nc, ctx, sem, c["x_stats"], c["rstd"], c["shift"], "g_ln")
        block = ctx.enter_context(nc.Block())

        @block.sync
        def _(sp):
            for dst, src in ((w1[:, :], d["conv1"]), (wmsg[:, :], d["wmsg"]),
                             (w2[:, :, :], d["conv2"]), (wih[:, :, :], d["wih"].rearrange("(a p) n -> p a n", p=P)),
                             (whh[:, :], d["whh"]), (wse[:, :], d["wse"]), (bse[:, :], d["bse"])):
                sp.dma_start(dst, src).then_inc(w_loaded, 16)
            def batch(b, q):
                after(sp, s["adj_psum"], b - 1)
                sp.dma_start(adj[:, q, :, :], d["adj"][b].rearrange("(j p) m -> p j m", p=P))\
                  .then_inc(adj_loaded[q], 16)

            each(sp, batch)

        @block.gpsimd
        def _(pool):
            for n, src in enumerate(("bn1_g", "bn1_b", "bn1_m", "bn1_v")):
                pool.dma_start(bn[:, 0, n:n + 1], d[src]).then_inc(small_loaded, 16)
            for n, src in enumerate(("bn2_g", "bn2_b", "bn2_m", "bn2_v")):
                pool.dma_start(bn[:, 1, n:n + 1], d[src]).then_inc(small_loaded, 16)
            pool.dma_start(row[:, 0:3 * D], d["bih"]).then_inc(hidden_loaded, 16)
            pool.dma_start(row[:, 3 * D:G], d["bhh"][:, 2 * D:3 * D]).then_inc(hidden_loaded, 16)
            pool.dma_start(row[:, G:G + D], d["bmsg"]).then_inc(hidden_loaded, 16)
            pool.dma_start(hidden_row[:, :], d["bhh"]).then_inc(hidden_loaded, 16)
            pool.memset(h1[:, :, 0:PAD], 0.0).then_inc(consts_set, 1)
            pool.memset(h1[:, :, PAD + N:], 0.0).then_inc(consts_set, 1)
            pool.memset(mhalf3[:, :], -0.5).then_inc(consts_set, 1)
            pool.memset(neg3[:, :], -1.0).then_inc(consts_set, 1)
            pool.wait_ge(parts_done, 5)
            for n in range(3):
                pool.dma_start(bias3[n:n + 1, :], row_parts[:, n, :]).then_inc(parts_moved, 16)
            def step(n, r):
                b, q = n - 1, (r - 1) % 2
                if not inside(b):
                    return
                pool.wait_ge(s["nn_ready"], b + 1)
                after(pool, s["mix_ready"], b)
                pool.tensor_tensor(diff[:, q, :, :], xn[:, (r - 1) % DEPTH, :, :], nn[:, q, :, :], ALU.subtract)\
                    .then_inc(s["diff_ready"], 1)
                pool.wait_ge(s["upd_ready"], b + 1)
                pool.tensor_tensor(x[:, bass.ds(b * J, J), :], x[:, bass.ds(b * J, J), :], upd[:, q, :, :],
                                   ALU.add).then_inc(s["x_ready"], 1)

            pipelined(pool, step)

        @block.scalar
        def _(act):
            ln_act(act)
            act.wait_ge(eps_set, 1)
            act.wait_ge(small_loaded, 16 * 8)
            act.activation(bn_work[:, :, 0:1], bn[:, :, 3:4], ACT.Sqrt, bias=eps[:, 0:1]).then_inc(bn_std, 1)
            act.wait_ge(bn_ready, 1)
            act.wait_ge(consts_set, 4)
            act.wait_ge(w_loaded, 16 * 7)
            def bring_in(b, q):
                act.wait_ge(s["sT_psum"], b + 1)
                act.activation(sT[:, q, :], p_h1[0:SE, N:2 * N], ACT.Identity, bias=bse[:, 0:1]).then_inc(s["sT_ready"], 1)
                act.activation(s2T[:, q, :], p_h1[0:SE, N:2 * N], ACT.Square, bias=bse[:, 0:1]).then_inc(s["sT_ready"], 1)
                act.activation(h1[:, q, PAD:PAD + N], p_h1[:, 0:N], ACT.Relu, bias=bn_shift[:, 0, :],
                               scale=bn_scale[:, 0, :]).then_inc(s["h1_ready"], 1)
                act.wait_ge(s["msg_psum"], b + 1)
                act.activation(msg[:, q, :, :], p_xT[:, N:2 * N].rearrange("p (j d) -> p j d", j=J), ACT.Relu)\
                   .then_inc(s["msg_ready"], 1)

            def distances(b, q):
                act.wait_ge(s["nsq_psum"], b + 1)
                act.activation(nsq[:, q, :], p_nmp[:, N:N + J], ACT.Copy).then_inc(s["nsq_ready"], 1)
                act.wait_ge(s["dist_psum"], b + 1)
                act.wait_ge(s["nsq_ready"], b + 1)
                for j in range(J):
                    act.activation(expo[:, q, j, :], p_dist[:, j * N:(j + 1) * N], ACT.Exp, scale=2.0,
                                   bias=nsq[:, q, j:j + 1]).then_inc(s["expo_ready"], 1)

            def step(n, r):
                b, q = n - 1, (r - 1) % 2
                if inside(n):
                    act.wait_ge(s["xT_psum"], n + 1)
                    act.activation(xT[:, r % 2, :], p_xT[:, 0:N], ACT.Copy).then_inc(s["xT_ready"], 1)
                    bring_in(n, r % 2)
                if inside(b):
                    act.wait_ge(s["pre_ready"], b + 1)
                    act.activation(convT[:, q, :], pre[:, q, :], ACT.Relu, bias=bn_shift[:, 1, :]).then_inc(s["conv_ready"], 1)
                if inside(n):
                    distances(n, r % 2)
                if inside(b):
                    act.wait_ge(s["nmp_psum"], b + 1)
                    act.activation(nmpT[:, q, :], p_nmp[:, 0:N], ACT.Copy).then_inc(s["nmp_ready"], 1)
                    act.wait_ge(s["gates_psum"], b + 1)
                    act.activation(rz[:, q, :, :], p_gate[:, :, 0:2 * D], ACT.Tanh, scale=0.5).then_inc(s["rz_ready"], 1)
                    act.wait_ge(s["cand_ready"], b + 1)
                    act.activation(nn[:, q, :, :], cand2[:, q, :, :], ACT.Tanh).then_inc(s["nn_ready"], 1)

            pipelined(act, step)

        @block.vector
        def _(dve):
            dve.memset(eps[:, :], LN_EPS).then_inc(eps_set, 1)
            ln_dve(dve)
            dve.wait_ge(bn_std, 1)
            dve.reciprocal(bn_work[:, :, 1:2], bn_work[:, :, 0:1]).then_inc(bn_steps, 1)
            dve.wait_ge(bn_steps, 1)
            dve.tensor_tensor(bn_scale[:, :, :], bn[:, :, 0:1], bn_work[:, :, 1:2], ALU.mult).then_inc(bn_steps, 1)
            dve.wait_ge(bn_steps, 2)
            dve.tensor_tensor(bn_work[:, :, 0:1], bn[:, :, 2:3], bn_scale[:, :, :], ALU.mult).then_inc(bn_steps, 1)
            dve.wait_ge(bn_steps, 3)
            dve.tensor_tensor(bn_shift[:, :, :], bn[:, :, 1:2], bn_work[:, :, 0:1], ALU.subtract).then_inc(bn_ready, 1)
            dve.wait_ge(hidden_loaded, 16 * 4)
            dve.tensor_tensor(row[:, 0:2 * D], row[:, 0:2 * D], hidden_row[:, 0:2 * D], ALU.add).then_inc(row_ready, 1)
            dve.wait_ge(row_ready, 1)
            split_rows(dve, row[:, :], row_work[:, :], [row_parts[:, n, :] for n in range(3)], parts_done)
            dve.wait_ge(norm_ready, 1)
            dve.wait_ge(bn_ready, 1)
            def normalise(b, r):
                after(dve, s["diff_ready"], b - DEPTH + 1)
                for j in range(J):
                    t = b * J + j
                    dve.tensor_scalar(xn[:, r, j, :], x[:, t, :], c["rstd"][:, bass.ds(t, 1)],
                                      c["shift"][:, bass.ds(t, 1)], ALU.mult, ALU.add).then_inc(s["xn_ready"], 1)

            def close(b, q):
                dve.wait_ge(s["rz_ready"], b + 1)
                dve.scalar_tensor_tensor(cand[:, q, :, :], rz[:, q, :, 0:D], 1.0, p_gate[:, :, 3 * D:G],
                                         ALU.add, ALU.mult).then_inc(s["cand_half"], 1)
                dve.wait_ge(s["cand_half"], b + 1)
                dve.scalar_tensor_tensor(cand2[:, q, :, :], cand[:, q, :, :], 0.5, p_gate[:, :, 2 * D:3 * D],
                                         ALU.mult, ALU.add).then_inc(s["cand_ready"], 1)
                dve.wait_ge(s["diff_ready"], b + 1)
                dve.scalar_tensor_tensor(mix[:, q, :, :], rz[:, q, :, D:2 * D], 1.0, diff[:, q, :, :],
                                         ALU.add, ALU.mult).then_inc(s["mix_ready"], 1)
                after(dve, s["stats_kept"], b)
                dve.wait_ge(s["mix_ready"], b + 1)
                dve.scalar_tensor_tensor(upd[:, q, :, :], mix[:, q, :, :], 0.5, nn[:, q, :, :],
                                         ALU.mult, ALU.add).then_inc(s["upd_ready"], 1)
                dve.wait_ge(norm_ready, 1)
                dve.wait_ge(s["x_ready"], b + 1)
                for j in range(J):
                    last = dve.bn_stats(bn6[:, q, j, :], x[:, b * J + j, :])
                last.then_inc(s["stats_half"], 1)
                dve.wait_ge(norm_ready, 1)
                dve.wait_ge(s["stats_half"], b + 1)
                for j in range(J):
                    dve.bn_aggr(mean_var[:, j, :], bn6[:, q, j, :]).then_inc(s["stats_done"], 1)
                dve.wait_ge(s["stats_done"], (b + 1) * J)
                keep_stats(dve, c, b, mean_var[:, :, :]).then_inc(s["stats_kept"], 1)

            def step(n, r):
                b, q = n - 1, (r - 1) % 2
                if isinstance(n, int) and n == 0:
                    normalise(n, r)
                if inside(b):
                    dve.wait_ge(s["conv_psum"], b + 1)
                    dve.scalar_tensor_tensor(pre[:, q, :], p_conv[:, 0:N], bn_scale[:, 1, :], xT[:, q, :],
                                             ALU.mult, ALU.add).then_inc(s["pre_ready"], 1)
                if inside(n):
                    dve.wait_ge(s["adj_psum"], n + 1)
                    dve.wait_ge(s["expo_ready"], (n + 1) * J)
                    dve.tensor_tensor(aT[:, r % 2, :, :], expo[:, r % 2, :, :],
                                      p_adj[:, :].rearrange("p (j n) -> p j n", j=J), ALU.mult).then_inc(s["aT_ready"], 1)
                if inside(n + 1):
                    normalise(n + 1, (r + 1) % DEPTH)
                if inside(b):
                    close(b, q)

            pipelined(dve, step)
            dve.wait_ge(s["stats_kept"], B)

        @block.tensor
        def _(pe):
            pe.wait_ge(w_loaded, 16 * 7)
            pe.wait_ge(consts_set, 4)
            pe.wait_ge(parts_moved, 16 * 3)
            def turn(b, q, r):
                after(pe, s["msg_ready"], b)
                pe.wait_ge(s["xn_ready"], (b + 1) * J)
                for j in range(J):
                    last = pe.transpose(p_xT[:, j * P:(j + 1) * P], xn[:, r, j, :], ident[:, :])
                last.then_inc(s["xT_psum"], 1)
                after(pe, s["aT_ready"], b)
                pe.wait_ge(adj_loaded[q], adj_reached(b, r))
                for m in range(J):
                    for j in range(J):
                        last = pe.transpose(p_adj[:, m * N + j * P:m * N + (j + 1) * P],
                                            adj[:, q, j, m * P:(m + 1) * P], ident[:, :])
                last.then_inc(s["adj_psum"], 1)

            def convolve(b, q, taps):
                if taps[0] == 0:
                    pe.wait_ge(s["h1_ready"], b + 1)
                    after(pe, s["pre_ready"], b)
                for k in taps:
                    last = pe.matmul(p_conv[:, 0:N], w2[:, k, :], h1[:, q, k:k + N], start=k == 0, stop=k == TAPS - 1)
                if taps[-1] == TAPS - 1:
                    last.then_inc(s["conv_psum"], 1)

            def bring_in(b, q):
                after(pe, s["h1_ready"], b)
                pe.wait_ge(s["xT_ready"], b + 1)
                pe.matmul(p_h1[:, 0:N], w1[:, :], xT[:, q, :], start=True, stop=True)
                pe.matmul(p_h1[0:SE, N:2 * N], wse[:, :], xT[:, q, :], start=True, stop=True,
                          skip_group_check=True).then_inc(s["sT_psum"], 1)
                for j in range(J):
                    part = p_xT[:, N + j * D:N + (j + 1) * D]
                    pe.matmul(part, c["ones3"][0:3, :], bias3[:, G:G + D], start=True, stop=False,
                              skip_group_check=True)
                    last = pe.matmul(part, xT[:, q, j * P:(j + 1) * P], wmsg[:, :], start=False, stop=True,
                                     skip_group_check=True)
                last.then_inc(s["msg_psum"], 1)

            def distances(b, q):
                after(pe, s["nmp_ready"], b - 1)
                pe.wait_ge(s["sT_ready"], (b + 1) * 2)
                for j in range(J):
                    last = pe.matmul(p_nmp[:, N + j:N + j + 1], s2T[:, q, j * P:(j + 1) * P], neg3[:, :],
                                     start=True, stop=True)
                last.then_inc(s["nsq_psum"], 1)
                after(pe, s["expo_ready"], b * J)
                for j in range(J):
                    part = p_dist[:, j * N:(j + 1) * N]
                    pe.matmul(part, sT[:, q, j * P:(j + 1) * P], sT[:, q, :], start=True, stop=False)
                    last = pe.matmul(part, mhalf3[:, :], s2T[:, q, :], start=False, stop=True)
                last.then_inc(s["dist_psum"], 1)

            def gates(b, q):
                after(pe, s["nsq_ready"], min(b + 2, B) if isinstance(b, int) else b + 2)
                pe.wait_ge(s["msg_ready"], b + 1)
                pe.wait_ge(s["aT_ready"], b + 1)
                for m in range(J):
                    last = pe.matmul(p_nmp[:, 0:N], msg[:, q, m, :], aT[:, q, m, :], start=m == 0, stop=m == J - 1)
                last.then_inc(s["nmp_psum"], 1)
                after(pe, s["cand_ready"], b)
                for j in range(J):
                    pe.matmul(p_gate[:, j, :], c["ones3"][0:3, :], bias3[:, 0:G], start=True, stop=False,
                              skip_group_check=True)
                    xTj = xT[:, q, j * P:(j + 1) * P]
                    pe.matmul(p_gate[:, j, 0:2 * D], xTj, whh[:, 0:2 * D], start=False, stop=False,
                              skip_group_check=True)
                    pe.matmul(p_gate[:, j, 3 * D:G], xTj, whh[:, 2 * D:3 * D], start=False, stop=True,
                              skip_group_check=True)
                pe.wait_ge(s["conv_ready"], b + 1)
                for j in range(J):
                    pe.matmul(p_gate[:, j, 0:3 * D], convT[:, q, j * P:(j + 1) * P], wih[:, 0, :], start=False,
                              stop=False, skip_group_check=True)
                pe.wait_ge(s["nmp_ready"], b + 1)
                for j in range(J):
                    last = pe.matmul(p_gate[:, j, 0:3 * D], nmpT[:, q, j * P:(j + 1) * P], wih[:, 1, :],
                                     start=False, stop=True, skip_group_check=True)
                last.then_inc(s["gates_psum"], 1)

            def step(n, r):
                b, q = n - 1, (r - 1) % 2
                if inside(n):
                    turn(n, r % 2, r)
                if inside(b):
                    convolve(b, q, range(0, PAD))
                if inside(n):
                    bring_in(n, r % 2)
                if inside(b):
                    convolve(b, q, range(PAD, TAPS))
                if inside(n):
                    distances(n, r % 2)
                if inside(b):
                    gates(b, q)

            pipelined(pe, step)



def stage_recurrent(nc, d, c):
    SCALED_BY = {"pool": range(0, 5), "dve": range(5, 6), "act": range(6, 8)}
    TG = 8
    GROUPS = TILES // TG
    HALF = TG // 2
    with ExitStack() as ctx:
        def sb(n, s, t=F32):
            return ctx.enter_context(nc.sbuf_tensor("r_" + n, s, t))

        sem = ctx.enter_context(stage_semaphores(nc, "r_"))
        x, ident = c["x"], c["ident"]
        w, w_gain, w_mid = sb("w", [P, D]), sb("w_gain", [P, D]), sb("w_mid", [P, D])
        ln_w, ln_b = sb("ln_w", [P, 1]), sb("ln_b", [P, 1])
        row, row_work = sb("row", [1, D]), sb("row_work", [1, D])
        row_parts, bias3 = sb("row_parts", [1, 3, D], BF16), sb("bias3", [3, HALF, D], BF16)
        h = sb("h", [P, GROUPS, TG, D])
        hT = sb("hT", [P, 2, TG, D])
        bn6, x6 = sb("bn6", [P, 2, TG, 6]), sb("x6", [P, 2, TG, 6])
        gap, ss, gap2 = sb("gap", [P, TG]), sb("ss", [P, TG]), sb("gap2", [P, TG])
        spread = sb("spread", [P, GROUPS, TG])
        scale = sb("scale", [P, GROUPS, TG])
        mean_var = sb("mean_var", [P, 2, TG, 2])
        p_hT = ctx.enter_context(nc.psum_tensor("r_p_hT", [P, 2, TG, D], F32))
        p_z = ctx.enter_context(nc.psum_tensor("r_p_z", [P, 2, TG, D], F32))

        loaded, mean_psum, bias_psum, w_steps, bias_row = (sem("loaded"), sem("mean_psum"), sem("bias_psum"),
                                                          sem("w_steps"), sem("bias_row"))
        parts_done, parts_moved = sem("parts_done"), sem("parts_moved")
        h_start = sem("h_start")
        scale_done, turned, copied, product = sem("scale_done"), sem("turned"), sem("copied"), sem("product")
        scaled = {name: sem(f"scaled_{name}") for name in SCALED_BY}
        tanh_done, mixed, silu_done, bn_done, gap_done, gap2_done, spread_done = (
            sem("tanh_done"), sem("mixed"), sem("silu_done"), sem("bn_done"), sem("gap_done"), sem("gap2_done"),
            sem("spread_done"))
        x_done, x_bn, x_aggr, x_kept = sem("x_done"), sem("x_bn"), sem("x_aggr"), sem("x_kept")
        ln_act, ln_dve, norm_ready = outer_norm(nc, ctx, sem, c["x_stats"], c["rstd"], c["shift"], "r_ln")
        CREDIT = 2
        block = ctx.enter_context(nc.Block())

        LAST_TURN = STEPS * GROUPS + GROUPS - 1

        def has_front(n):
            return not isinstance(n, int) or GROUPS <= n <= LAST_TURN

        def has_back(n):
            return not isinstance(n, int) or GROUPS <= n < STEPS * GROUPS

        def turns(eng, turn):
            for g in range(GROUPS):
                turn(GROUPS + g, g)
            with eng.Fori(2, STEPS) as step:
                for g in range(GROUPS):
                    turn(step * GROUPS + g, g)
            for n in range(STEPS * GROUPS, LAST_TURN + 4):
                turn(n, n % GROUPS)

        @block.sync
        def _(sp):
            sp.dma_start(w[:, :], d["ffn_w"]).then_inc(loaded, 16)
            sp.dma_start(ln_w[:, :], d["ffn_ln_w"]).then_inc(loaded, 16)
            sp.dma_start(ln_b[:, :], d["ffn_ln_b"]).then_inc(loaded, 16)
            sp.dma_start(row[:, :], d["ffn_b"]).then_inc(loaded, 16)
            sp.wait_ge(parts_done, 5)
            for n in range(3):
                for t in range(HALF):
                    sp.dma_start(bias3[n:n + 1, t, :], row_parts[:, n, :]).then_inc(parts_moved, 16)

        @block.gpsimd
        def _(pool):
            def turn(n, g):
                if not has_front(n):
                    return
                pool.wait_ge(spread_done, n - GROUPS + 1)
                pool.tensor_tensor(scale[:, g, :], spread[:, g, :], c["minus_half"][:, 0:TG], ALU.pow)\
                    .then_inc(scale_done, 1)
                pool.wait_ge(norm_ready, 1)
                pool.wait_ge(scale_done, n - GROUPS + 1)
                for t in SCALED_BY["pool"]:
                    last = pool.tensor_scalar(h[:, g, t, :], h[:, g, t, :], scale[:, g, t:t + 1], 1.0, ALU.mult,
                                              ALU.mult)
                last.then_inc(scaled["pool"], 1)

            turns(pool, turn)

        @block.tensor
        def _(pe):
            pe.wait_ge(w_steps, 1)
            pe.matmul(p_z[:, 0, 0, :], c["ones"][:, :], w_gain[:, :], start=True, stop=True).then_inc(mean_psum, 1)
            pe.matmul(p_hT[0:1, 0, 0, :], ln_b[:, :], w[:, :], start=True, stop=True).then_inc(bias_psum, 1)
            pe.sem_inc(product, CREDIT)
            pe.wait_ge(w_steps, 3)
            pe.wait_ge(bias_row, 1)
            pe.wait_ge(parts_moved, 16 * 3 * HALF)

            def transpose(n, g):
                for part in SCALED_BY:
                    pe.wait_ge(scaled[part], n - GROUPS + 1)
                pe.wait_ge(copied, n - GROUPS + 1)
                for t in range(TG):
                    last = pe.transpose(p_hT[:, g % 2, t, :], h[:, g, t, :], ident[:, :])
                last.then_inc(turned, 1)

            def multiply(n, g):
                pe.wait_ge(copied, n - GROUPS + 1 + CREDIT)
                pe.wait_ge(mixed, n - 2 + 1)
                for a in range(0, TG, HALF):
                    pe.matmul(p_z[:, g % 2, a:a + HALF, :], c["ones3"][:, :], bias3[:, :, :], start=True, stop=False,
                              skip_group_check=True)
                    for t in range(a, a + HALF):
                        last = pe.matmul(p_z[:, g % 2, t, :], hT[:, g % 2, t, :], w[:, :], start=False, stop=True,
                                         skip_group_check=True)
                last.then_inc(product, 1)

            def turn(n, g):
                if has_front(n):
                    transpose(n, g)
                if has_front(n - 1):
                    multiply(n - 1, (g - 1) % GROUPS)

            turns(pe, turn)

        @block.scalar
        def _(act):
            ln_act(act)
            act.sem_inc(copied, CREDIT)

            def copy_turned(n, g):
                act.wait_ge(turned, n - GROUPS + 1)
                act.wait_ge(product, n - GROUPS + 1)
                act.activation(hT[:, g % 2, :, :], p_hT[:, g % 2, :, :], ACT.Copy).then_inc(copied, 1)

            def silu(n, g):
                act.wait_ge(mixed, n + 1)
                act.activation(h[:, g, :, :], h[:, g, :, :], ACT.Silu).then_inc(silu_done, 1)

            def rescale(n, g):
                act.wait_ge(scale_done, n - GROUPS + 1)
                for t in SCALED_BY["act"]:
                    last = act.activation(h[:, g, t, :], h[:, g, t, :], ACT.Copy, scale=scale[:, g, t:t + 1])
                last.then_inc(scaled["act"], 1)

            def turn(n, g):
                if has_front(n + 2):
                    rescale(n + 2, (g + 2) % GROUPS)
                if has_front(n):
                    copy_turned(n, g)
                if has_back(n - 1):
                    act.wait_ge(product, n - 1 - GROUPS + 1 + CREDIT)
                    act.activation(h[:, (g - 1) % GROUPS, :, :], p_z[:, (g - 1) % 2, :, :], ACT.Tanh)\
                       .then_inc(tanh_done, 1)
                if has_back(n - 2):
                    silu(n - 2, (g - 2) % GROUPS)

            for g in range(GROUPS + 1):
                if g < GROUPS:
                    act.wait_ge(h_start, g + 1)
                    act.activation(hT[:, g % 2, :, :], h[:, g, :, :], ACT.Tanh).then_inc(tanh_done, 1)
                if g >= 1:
                    silu(g - 1, g - 1)
            rescale(GROUPS, 0)
            rescale(GROUPS + 1, 1)
            turns(act, turn)

        @block.vector
        def _(dve):
            ln_dve(dve)
            dve.wait_ge(loaded, 16 * 4)
            dve.tensor_scalar(w_gain[:, :], w[:, :], ln_w[:, 0:1], float(D) ** 0.5, ALU.mult, ALU.mult).then_inc(w_steps, 1)
            dve.wait_ge(bias_psum, 1)
            dve.tensor_tensor(row[:, :], row[:, :], p_hT[0:1, 0, 0, :], ALU.add).then_inc(bias_row, 1)
            dve.wait_ge(mean_psum, 1)
            dve.tensor_scalar(w_mid[:, :], p_z[:, 0, 0, :], 1.0 / D, None, ALU.mult).then_inc(w_steps, 1)
            dve.wait_ge(w_steps, 2)
            dve.tensor_tensor(w[:, :], w_gain[:, :], w_mid[:, :], ALU.subtract).then_inc(w_steps, 1)
            dve.wait_ge(bias_row, 1)
            split_rows(dve, row[:, :], row_work[:, :], [row_parts[:, n, :] for n in range(3)], parts_done)
            dve.wait_ge(norm_ready, 1)

            def start(g):
                for t in range(TG):
                    a = g * TG + t
                    last = dve.tensor_scalar(h[:, g, t, :], x[:, a, :], c["rstd"][:, a:a + 1], c["shift"][:, a:a + 1],
                                             ALU.mult, ALU.add)
                last.then_inc(h_start, 1)

            def mix(n, g):
                dve.wait_ge(tanh_done, n + 1)
                dve.scalar_tensor_tensor(h[:, g, :, :], h[:, g, :, :], 0.01, p_z[:, g % 2, :, :], ALU.mult, ALU.add)\
                   .then_inc(mixed, 1)

            def stats(n, g, part):
                if part == 0:
                    dve.wait_ge(silu_done, n + 1)
                for t in range(part * HALF, part * HALF + HALF):
                    last = dve.bn_stats(bn6[:, g % 2, t, :], h[:, g, t, :])
                last.then_inc(bn_done, 1)

            def gaps(n, g):
                dve.wait_ge(bn_done, n * 2 + 2)
                after(dve, spread_done, n)
                dve.tensor_tensor(gap[:, :], bn6[:, g % 2, :, 1], bn6[:, g % 2, :, 4], ALU.subtract)
                dve.tensor_tensor(ss[:, :], bn6[:, g % 2, :, 2], bn6[:, g % 2, :, 5], ALU.add).then_inc(gap_done, 1)

            def square_gaps(n, g):
                dve.wait_ge(gap_done, n + 1)
                dve.scalar_tensor_tensor(gap2[:, :], gap[:, :], D / 4.0, gap[:, :], ALU.mult, ALU.mult).then_inc(gap2_done, 1)

            def spreads(n, g):
                dve.wait_ge(gap2_done, n + 1)
                dve.scalar_tensor_tensor(spread[:, g, :], gap2[:, :], D * LN_EPS, ss[:, :], ALU.add, ALU.add)\
                   .then_inc(spread_done, 1)

            def rescale(n, g):
                dve.wait_ge(scale_done, n - GROUPS + 1)
                for t in SCALED_BY["dve"]:
                    last = dve.tensor_scalar(h[:, g, t, :], h[:, g, t, :], scale[:, g, t:t + 1], 1.0, ALU.mult, ALU.mult)
                last.then_inc(scaled["dve"], 1)

            def add_to_x(n, g):
                dve.wait_ge(product, n - GROUPS + 1 + CREDIT)
                xg = x[:, g * TG:(g + 1) * TG, :]
                dve.tensor_tensor(xg, xg, p_z[:, g % 2, :, :], ALU.add).then_inc(mixed, 1)
                dve.wait_ge(mixed, n + 1)
                for t in range(TG):
                    last = dve.bn_stats(x6[:, g % 2, t, :], x[:, g * TG + t, :])
                last.then_inc(x_bn, 1)
                dve.wait_ge(x_bn, g + 1)
                for t in range(TG):
                    last = dve.bn_aggr(c["x_stats"][:, g * TG + t, :], x6[:, g % 2, t, :])
                last.then_inc(x_kept, 1)

            def turn(n, g):
                if has_front(n + 2):
                    rescale(n + 2, (g + 2) % GROUPS)
                if has_back(n - 1):
                    mix(n - 1, (g - 1) % GROUPS)
                if has_back(n - 3):
                    gaps(n - 3, (g - 3) % GROUPS)
                if has_back(n - 2):
                    stats(n - 2, (g - 2) % GROUPS, 0)
                if has_back(n - 3):
                    square_gaps(n - 3, (g - 3) % GROUPS)
                if has_back(n - 2):
                    stats(n - 2, (g - 2) % GROUPS, 1)
                if has_back(n - 3):
                    spreads(n - 3, (g - 3) % GROUPS)
                if isinstance(n, int) and STEPS * GROUPS <= n - 1 <= LAST_TURN:
                    add_to_x(n - 1, (g - 1) % GROUPS)

            for g in range(GROUPS + 2):
                if g < GROUPS:
                    start(g)
                if 1 <= g <= GROUPS:
                    dve.wait_ge(tanh_done, g)
                    dve.scalar_tensor_tensor(h[:, g - 1, :, :], hT[:, (g - 1) % 2, :, :], 0.01, h[:, g - 1, :, :],
                                             ALU.mult, ALU.add).then_inc(mixed, 1)
                if g >= 2:
                    for part in range(2):
                        stats(g - 2, g - 2, part)
                    gaps(g - 2, g - 2)
                    square_gaps(g - 2, g - 2)
                    spreads(g - 2, g - 2)
            rescale(GROUPS, 0)
            rescale(GROUPS + 1, 1)
            turns(dve, turn)
            dve.wait_ge(x_kept, GROUPS)



def stage_graph_attention(nc, d, c):
    with ExitStack() as ctx:
        def sb(n, s, t=F32):
            return ctx.enter_context(nc.sbuf_tensor("a_" + n, s, t))

        def ps(n, s):
            return ctx.enter_context(nc.psum_tensor("a_" + n, s, F32))

        sem = ctx.enter_context(stage_semaphores(nc, "a_"))
        x, ident = c["x"], c["ident"]
        w = sb("w", [P, 3, D])
        row, row_work = sb("row", [1, D]), sb("row_work", [1, D])
        row_parts, bias3 = sb("row_parts", [1, 3, D], BF16), sb("bias3", [3, J, D], BF16)
        gain, offset = sb("gain", [P, J, D]), sb("offset", [P, J, D])
        minus_half = c["minus_half"]
        xn = sb("xn", [P, 2, J, D])
        xT = sb("xT", [P, 2, N])
        adj = sb("adj", [P, 2, J, N])
        relu_qk, relu_x = sb("relu_qk", [P, 2, N]), sb("relu_x", [P, J, D])
        qT = sb("qT", [P, 2, N])
        kT = sb("kT", [P, 2, H, N])
        lin = sb("lin", [P, DEPTH, J, D])
        head_row = sb("head_row", [P, H])
        degT, yT = sb("degT", [P, N]), sb("yT", [P, N])
        att = sb("att", [P, 2, H, J * N])
        ah = sb("ah", [P, 2, H, J * N])
        degree_raw, degree, linked, root, dis = (sb("degree_raw", [P, J * H]), sb("degree", [P, J * H]), sb("linked", [P, J * H]), sb("root", [P, J * H]),
                                     sb("dis", [P, 2, J * H]))
        lin_dis = sb("lin_dis", [P, 2, J, D])
        y, yn, yg, x_off = sb("y", [P, J, D]), sb("yn", [P, J, D]), sb("yg", [P, J, D]), sb("x_off", [P, J, D])
        y6, y_stats, y_var, y_rstd = sb("y6", [P, J, 6]), sb("y_stats", [P, J, 2]), sb("y_var", [P, J]), sb("y_rstd", [P, J])
        bn6, mean_var = sb("bn6", [P, J, 6]), sb("mean_var", [P, J, 2])

        p_xT = ps("p_xT", [P, 512])
        p_qk = ps("p_qk", [P, 2, N])
        p_adj = ps("p_adj", [P, J * N])
        p_s = ps("p_s", [P, H, J * N])
        p_y = ps("p_y", [P, 512])

        loaded, parts_done, parts_moved = sem("loaded"), sem("parts_done"), sem("parts_moved")
        zeroed, head_row_done = sem("zeroed"), sem("head_row_done")
        adj_loaded = [sem("adj_loaded0"), sem("adj_loaded1")]
        names = ("xn_ready xT_psum xT_ready adj_psum qk_psum lin_psum relu_ready qk_ready lin_ready s_psum att_ready "
                 "ah_ready degT_psum degT_ready degree_kept yT_psum yT_ready degree_psum degree_ready root_ready dis_ready lin_dis_ready y_psum y_ready y_bn y_aggr "
                 "y_var_ready y_rstd_ready yn_ready yg_ready off_ready x_ready x_bn x_aggr x_kept").split()
        s = {n: sem(n) for n in names}
        ln_act, ln_dve, norm_ready = outer_norm(nc, ctx, sem, c["x_stats"], c["rstd"], c["shift"], "a_ln")
        block = ctx.enter_context(nc.Block())

        def least(n):
            return min(n, B) if isinstance(n, int) else n

        def heads(t):
            return t.rearrange("p j (h e) -> p (j h) e", h=H)

        def per_head(t):
            return t.rearrange("p (g o) -> p g o", o=1).broadcast_to([P, J * H, HD])

        @block.sync
        def _(sp):
            for n, name in enumerate(("att_lin", "att_q", "att_k")):
                sp.dma_start(w[:, n, :], d[name]).then_inc(loaded, 16)
            sp.dma_start(row[:, :], d["att_b"]).then_inc(loaded, 16)
            for j in range(J):
                sp.dma_start(gain[:, j, :], d["att_g"]).then_inc(loaded, 16)
                sp.dma_start(offset[:, j, :], d["att_o"]).then_inc(loaded, 16)
            sp.wait_ge(parts_done, 5)
            for n in range(3):
                for j in range(J):
                    sp.dma_start(bias3[n:n + 1, j, :], row_parts[:, n, :]).then_inc(parts_moved, 16)

            def load(b, q):
                after(sp, s["adj_psum"], b - 1)
                sp.dma_start(adj[:, q, :, :], d["adj"][b].rearrange("(j p) m -> p j m", p=P)).then_inc(adj_loaded[q], 16)

            each(sp, load)

        @block.tensor
        def _(pe):
            pe.wait_ge(loaded, 16 * 8)
            pe.wait_ge(parts_moved, 16 * 3 * J)

            pe.wait_ge(zeroed, 2)
            pe.wait_ge(head_row_done, 1)

            def turn_x(b, q):
                pe.wait_ge(s["xn_ready"], b + 1)
                after(pe, s["degree_kept"], b - 2)
                for j in range(J):
                    last = pe.transpose(p_xT[:, j * P:(j + 1) * P], xn[:, q, j, :], ident[:, :])
                last.then_inc(s["xT_psum"], 1)

            def project(b, q):
                pe.wait_ge(s["xT_ready"], b + 1)
                after(pe, s["qk_ready"], b)
                for n in range(2):
                    last = pe.matmul(p_qk[:, n, :], w[:, 1 + n, :], xT[:, q, :], start=True, stop=True)
                last.then_inc(s["qk_psum"], 1)
                pe.matmul(p_xT[:, N:2 * N], c["ones3"][:, :], bias3[:, :, :], start=True, stop=False,
                          skip_group_check=True)
                for j in range(J):
                    last = pe.matmul(p_xT[:, N + j * D:N + (j + 1) * D], xT[:, q, j * P:(j + 1) * P], w[:, 0, :],
                                     start=False, stop=True, skip_group_check=True)
                last.then_inc(s["lin_psum"], 1)

            def score(b, q, g):
                pe.wait_ge(s["qk_ready"], b + 1)
                after(pe, s["att_ready"], b * 2 - 1 + g)
                for h, j in ((2 * g, 0), (2 * g, 1), (2 * g + 1, 0), (2 * g + 1, 1)):
                    last = pe.matmul(p_s[:, h, j * N:(j + 1) * N], kT[:, q, h, j * P:(j + 1) * P], qT[:, q, :],
                                     start=True, stop=True)
                last.then_inc(s["s_psum"], 1)

            def turn_adj(b, q, r):
                pe.wait_ge(adj_loaded[q], adj_reached(b, r))
                after(pe, s["ah_ready"], b * 2)
                for m in range(J):
                    for j in range(J):
                        last = pe.transpose(p_adj[:, m * N + j * P:m * N + (j + 1) * P],
                                            adj[:, q, j, m * P:(m + 1) * P], ident[:, :])
                last.then_inc(s["adj_psum"], 1)

            def by_head(dst, b, q, stat):
                for m in range(J):
                    for h in range(H):
                        last = pe.matmul(dst[h * HD:(h + 1) * HD, :], stat(m, h), ah[:, q, h, m * N:(m + 1) * N],
                                         start=m == 0, stop=m == J - 1, tile_position=(0, h * HD),
                                         skip_group_check=True)
                return last

            def degree_rows(b, q):
                pe.wait_ge(s["ah_ready"], b * 2 + 2)
                after(pe, s["lin_ready"], least(b + 3))
                by_head(p_xT[:, 0:N], b, q, lambda m, h: c["ones"][:, 0:HD]).then_inc(s["degT_psum"], 1)

            def degrees(b, q):
                pe.wait_ge(s["degT_ready"], b + 1)
                for j in range(J):
                    last = pe.matmul(p_xT[:, N + j * H:N + (j + 1) * H], degT[:, j * P:(j + 1) * P], head_row[:, :],
                                     start=True, stop=True)
                last.then_inc(s["degree_psum"], 1)

            def result(b, q):
                pe.wait_ge(s["lin_dis_ready"], b + 1)
                after(pe, s["y_ready"], b)
                by_head(p_y[:, 0:N], b, q, lambda m, h: lin_dis[:, q, m, h * HD:(h + 1) * HD])\
                    .then_inc(s["yT_psum"], 1)

            def turn_result(b, q):
                pe.wait_ge(s["yT_ready"], b + 1)
                for j in range(J):
                    last = pe.transpose(p_y[:, N + j * P:N + (j + 1) * P], yT[:, j * P:(j + 1) * P], ident[:, :])
                last.then_inc(s["y_psum"], 1)

            def step(n, r):
                if inside(n):
                    turn_x(n, r % 2)
                    project(n, r % 2)
                if inside(n - 1):
                    turn_adj(n - 1, (r - 1) % 2, (r - 1) % DEPTH)
                    score(n - 1, (r - 1) % 2, 0)
                if inside(n - 3):
                    result(n - 3, (r - 3) % 2)
                if inside(n - 1):
                    score(n - 1, (r - 1) % 2, 1)
                if inside(n - 3):
                    turn_result(n - 3, (r - 3) % 2)
                if inside(n - 2):
                    degree_rows(n - 2, r % 2)
                    degrees(n - 2, r % 2)

            pipelined(pe, step)

        @block.scalar
        def _(act):
            ln_act(act)

            def sigmoid(b, q, g):
                act.wait_ge(s["s_psum"], b * 2 + g + 1)
                after(act, s["ah_ready"], b * 2 - 2)
                act.activation(att[:, q, 2 * g:2 * g + 2, :], p_s[:, 2 * g:2 * g + 2, :], ACT.Sigmoid,
                               scale=HD ** -0.5).then_inc(s["att_ready"], 1)

            def step(n, r):
                if inside(n):
                    act.wait_ge(s["xT_psum"], n + 1)
                    act.activation(xT[:, r % 2, :], p_xT[:, 0:N], ACT.Copy).then_inc(s["xT_ready"], 1)
                if inside(n):
                    act.wait_ge(s["qk_psum"], n + 1)
                    after(act, s["lin_ready"], n)
                    act.activation(relu_qk[:, :, :], p_qk[:, :, :], ACT.Relu, scale=0.99).then_inc(s["relu_ready"], 1)
                    act.wait_ge(s["lin_psum"], n + 1)
                    act.activation(relu_x[:, :, :], p_xT[:, N:2 * N].rearrange("p (j d) -> p j d", j=J), ACT.Relu,
                                   scale=0.99).then_inc(s["relu_ready"], 1)
                if inside(n - 1):
                    sigmoid(n - 1, (r - 1) % 2, 0)
                if inside(n - 3):
                    act.wait_ge(s["yT_psum"], n - 2)
                    act.activation(yT[:, :], p_y[:, 0:N], ACT.Copy).then_inc(s["yT_ready"], 1)
                if inside(n - 1):
                    sigmoid(n - 1, (r - 1) % 2, 1)
                if inside(n - 2):
                    act.wait_ge(s["degT_psum"], n - 1)
                    act.activation(degT[:, :], p_xT[:, 0:N], ACT.Copy).then_inc(s["degT_ready"], 1)
                    act.wait_ge(s["degree_psum"], n - 1)
                    after(act, s["degree_ready"], n - 2)
                    act.activation(degree_raw[:, :], p_xT[:, N:N + J * H], ACT.Copy).then_inc(s["degree_kept"], 1)

            pipelined(act, step)

        @block.vector
        def _(dve):
            ln_dve(dve)
            dve.wait_ge(loaded, 16 * 8)
            split_rows(dve, row[:, :], row_work[:, :], [row_parts[:, n, :] for n in range(3)], parts_done)

            def normalise(b, q):
                after(dve, s["xT_psum"], b - 1)
                for j in range(J):
                    t = b * J + j
                    last = dve.tensor_scalar(xn[:, q, j, :], x[:, t, :], c["rstd"][:, bass.ds(t, 1)],
                                             c["shift"][:, bass.ds(t, 1)], ALU.mult, ALU.add)
                last.then_inc(s["xn_ready"], 1)

            def projections(b, q, r):
                dve.wait_ge(s["relu_ready"], b * 2 + 1)
                dve.scalar_tensor_tensor(qT[:, q, :], p_qk[:, 0, :], 0.01, relu_qk[:, 0, :], ALU.mult, ALU.add)
                for h in range(H):
                    rows = slice(h * HD, (h + 1) * HD)
                    last = dve.scalar_tensor_tensor(kT[rows, q, h, :], p_qk[rows, 1, :], 0.01, relu_qk[rows, 1, :],
                                                    ALU.mult, ALU.add)
                last.then_inc(s["qk_ready"], 1)
                dve.wait_ge(s["relu_ready"], b * 2 + 2)
                dve.scalar_tensor_tensor(lin[:, r, :, :], p_xT[:, N:2 * N].rearrange("p (j d) -> p j d", j=J), 0.01,
                                         relu_x[:, :, :], ALU.mult, ALU.add).then_inc(s["lin_ready"], 1)

            def weigh(b, q, g):
                after(dve, s["yT_psum"], b - 1)
                dve.wait_ge(s["adj_psum"], b + 1)
                dve.wait_ge(s["att_ready"], b * 2 + g + 1)
                two = slice(2 * g, 2 * g + 2)
                dve.tensor_tensor(ah[:, q, two, :], att[:, q, two, :],
                                  p_adj[:, :].rearrange("p (o n) -> p o n", o=1).broadcast_to([P, 2, J * N]), ALU.mult)\
                   .then_inc(s["ah_ready"], 1)

            def degrees(b, q):
                dve.wait_ge(s["degree_kept"], b + 1)
                after(dve, s["root_ready"], b)
                dve.tensor_scalar(degree[:, :], degree_raw[:, :], 1.2e-38, None, ALU.max)
                after(dve, s["dis_ready"], b)
                dve.tensor_scalar(linked[:, :], degree_raw[:, :], 0.0, None, ALU.is_gt)\
                   .then_inc(s["degree_ready"], 1)

            def result(b, q):
                dve.wait_ge(s["y_psum"], b + 1)
                dve.tensor_tensor(heads(y[:, :, :]), heads(p_y[:, N:2 * N].rearrange("p (j d) -> p j d", j=J)),
                                  per_head(dis[:, q, :]), ALU.mult).then_inc(s["y_ready"], 1)
                dve.wait_ge(norm_ready, 1)
                dve.wait_ge(s["y_ready"], b + 1)
                for j in range(J):
                    last = dve.bn_stats(y6[:, j, :], y[:, j, :])
                last.then_inc(s["y_bn"], 1)
                dve.wait_ge(norm_ready, 1)
                dve.wait_ge(s["y_bn"], b + 1)
                for j in range(J):
                    last = dve.bn_aggr(y_stats[:, j, :], y6[:, j, :])
                last.then_inc(s["y_aggr"], 1)
                dve.wait_ge(s["y_aggr"], b + 1)
                dve.tensor_scalar(y_var[:, :], y_stats[:, :, 1], LN_EPS, None, ALU.add).then_inc(s["y_var_ready"], 1)

            def scale_result(b, q):
                dve.wait_ge(s["y_rstd_ready"], b + 1)
                after(dve, s["yg_ready"], b)
                for j in range(J):
                    last = dve.tensor_scalar(yn[:, j, :], y[:, j, :], y_stats[:, j, 0:1], y_rstd[:, j:j + 1],
                                             ALU.subtract, ALU.mult)
                last.then_inc(s["yn_ready"], 1)

            def close(b, q):
                dve.wait_ge(s["yg_ready"], b + 1)
                dve.wait_ge(s["off_ready"], b + 1)
                dve.tensor_tensor(x[:, bass.ds(b * J, J), :], yg[:, :, :], x_off[:, :, :], ALU.add)\
                   .then_inc(s["x_ready"], 1)
                dve.wait_ge(norm_ready, 1)
                dve.wait_ge(s["x_ready"], b + 1)
                for j in range(J):
                    last = dve.bn_stats(bn6[:, j, :], x[:, b * J + j, :])
                last.then_inc(s["x_bn"], 1)
                dve.wait_ge(norm_ready, 1)
                dve.wait_ge(s["x_bn"], b + 1)
                for j in range(J):
                    last = dve.bn_aggr(mean_var[:, j, :], bn6[:, j, :])
                last.then_inc(s["x_aggr"], 1)
                dve.wait_ge(s["x_aggr"], b + 1)
                keep_stats(dve, c, b, mean_var[:, :, :]).then_inc(s["x_kept"], 1)

            def step(n, r):
                if isinstance(n, int) and n == 0:
                    normalise(n, r % 2)
                if inside(n):
                    projections(n, r % 2, r)
                if inside(n + 1):
                    normalise(n + 1, (r + 1) % 2)
                if inside(n - 1):
                    weigh(n - 1, (r - 1) % 2, 0)
                if inside(n - 3):
                    result(n - 3, (r - 3) % 2)
                if inside(n - 1):
                    weigh(n - 1, (r - 1) % 2, 1)
                if inside(n - 3):
                    scale_result(n - 3, (r - 3) % 2)
                if inside(n - 2):
                    degrees(n - 2, r % 2)
                if inside(n - 3):
                    close(n - 3, (r - 3) % 2)

            dve.wait_ge(zeroed, 2)
            pipelined(dve, step)
            dve.wait_ge(s["x_kept"], B)

        @block.gpsimd
        def _(pool):
            pool.memset(kT[:, :, :, :], 0.0).then_inc(zeroed, 1)
            pool.memset(head_row[:, :], 0.0).then_inc(zeroed, 1)
            pool.wait_ge(zeroed, 2)
            pool.affine_select(out=head_row[:, :], in_=head_row[:, :], compare_op=ALU.not_equal, fill=1.0, base=0,
                               pattern=[[-HD, H]], channel_multiplier=1).then_inc(head_row_done, 1)
            pool.wait_ge(loaded, 16 * 8)

            def step(n, r):
                if inside(n - 3):
                    b = n - 3
                    after(pool, s["x_ready"], b)
                    pool.tensor_tensor(x_off[:, :, :], x[:, bass.ds(b * J, J), :], offset[:, :, :], ALU.add)\
                        .then_inc(s["off_ready"], 1)
                    pool.wait_ge(s["y_var_ready"], b + 1)
                    pool.tensor_tensor(y_rstd[:, :], y_var[:, :], minus_half[:, 0:J], ALU.pow).then_inc(s["y_rstd_ready"], 1)
                    pool.wait_ge(s["yn_ready"], b + 1)
                    pool.tensor_tensor(yg[:, :, :], yn[:, :, :], gain[:, :, :], ALU.mult).then_inc(s["yg_ready"], 1)
                if inside(n - 2):
                    b, q = n - 2, r % 2
                    pool.wait_ge(s["degree_ready"], b + 1)
                    pool.tensor_tensor(root[:, :], degree[:, :], minus_half[:, 0:J * H], ALU.pow).then_inc(s["root_ready"], 1)
                    after(pool, s["y_ready"], b - 1)
                    pool.wait_ge(s["root_ready"], b + 1)
                    pool.tensor_tensor(dis[:, q, :], root[:, :], linked[:, :], ALU.mult).then_inc(s["dis_ready"], 1)
                    pool.wait_ge(s["dis_ready"], b + 1)
                    pool.wait_ge(s["lin_ready"], b + 1)
                    after(pool, s["yT_psum"], b - 1)
                    pool.tensor_tensor(heads(lin_dis[:, q, :, :]), heads(lin[:, (r - 2) % DEPTH, :, :]),
                                       per_head(dis[:, q, :]), ALU.mult).then_inc(s["lin_dis_ready"], 1)

            pipelined(pool, step)


def stage_expert_attention(nc, d, c, out):
    L = E * P
    ROUNDS = ((0, 0), (0, 1), (1, 1))
    TOP_ROUNDS = ((0, 0, 4), (1, 0, 2), (1, 2, 2))
    JOBS = len(ROUNDS) * H
    G = J * H
    PG = 2 * G
    MASKED = -1.0e30
    with ExitStack() as ctx:
        def sb(n, s, t=F32):
            return ctx.enter_context(nc.sbuf_tensor("e_" + n, s, t))

        def ps(n, s, t=F32):
            return ctx.enter_context(nc.psum_tensor("e_" + n, s, t))

        sem = ctx.enter_context(stage_semaphores(nc, "e_"))
        x, ident = c["x"], c["ident"]
        w_hl, b_hl = sb("w_hl", [P, D]), sb("b_hl", [P, 1])
        w_q, w_kv = sb("w_q", [P, E, D]), sb("w_kv", [P, 2, D])
        w_gate = sb("w_gate", [P, E, H * E])
        w_fc, b_fc1 = sb("w_fc", [P, 2, D]), sb("b_fc1", [P, 1])
        w_fgate = sb("w_fgate", [P, H])
        row, row_work = sb("row", [1, D]), sb("row_work", [1, D])
        b_gate, head_row = sb("b_gate", [P, J, H * E]), sb("head_row", [P, H])
        row_parts, bias3 = sb("row_parts", [1, 3, D], BF16), sb("bias3", [3, D], BF16)
        norms = sb("norms", [P, 4, HD])
        ident16, below, above = (sb(n, [P, P], BF16) for n in ("ident16", "below", "above"))
        pick = sb("pick", [P, H, E, P], BF16)
        resid, residT = sb("resid", [P, J, D]), sb("residT", [P, N])

        xn, xT, sxT = sb("xn", [P, 2, J, D]), sb("xT", [P, N]), sb("sxT", [P, 2, N])
        qT, kT, v = sb("qT", [P, 2, E, N]), sb("kT", [P, 2, H, N]), sb("v", [P, 2, J, D])
        q_round, k_round = sb("q_round", [P, E, N], F32R), sb("k_round", [P, H, N], F32R)
        top = sb("top", [P, J, H, E])
        top2 = sb("top2", [P, J, H, HD], BF16)
        topT = sb("topT", [P, J * P], BF16)
        wT = sb("wT", [P, len(ROUNDS), H, L])
        nonzero = sb("nonzero", [P, 2, J, P])
        sumsT = sb("sumsT", [P, J, E, P])
        outT = sb("outT", [P, J, E, P])
        z_over, z_norm, z_sum, logits = (sb("z_over", [P, J * E * H]), sb("z_norm", [P, J, E, H * E]),
                                         sb("z_sum", [P, J, H * E]), sb("logits", [P, J, H * E]))
        g_top, g_low, g_exp, g_sum, g_over, g_w, g_scaled = (sb("g_top", [P, G]), sb("g_low", [P, G, E]), sb("g_exp", [P, G, E]),
                                                   sb("g_sum", [P, G]), sb("g_over", [P, G]), sb("g_w", [P, G, E]),
                                                   sb("g_scaled", [P, G, E]))
        prod = sb("prod", [P, J, E, D])
        mixed = sb("mixed", [P, J, D])
        u = sb("u", [P, 2, J, D])
        n_sum, n_mean, n_mid, n_sq, n_ss, n_var, n_rstd, n_unit, n_gain = (
            sb("n_sum", [P, PG]), sb("n_mean", [P, PG]), sb("n_mid", [P, PG, HD]), sb("n_sq", [P, PG, HD]),
            sb("n_ss", [P, PG]), sb("n_var", [P, PG]), sb("n_rstd", [P, PG]), sb("n_unit", [P, PG, HD]),
            sb("n_gain", [P, PG, HD]))
        fx, fout = sb("fx", [P, PG, HD]), sb("fout", [P, PG, HD])
        fxT, fc1, fc1n, foT = sb("fxT", [P, 2 * N]), sb("fc1", [P, 2 * N]), sb("fc1n", [P, 2 * N]), sb("foT", [P, 2 * N])
        fc2, u2 = sb("fc2", [P, PG, HD]), sb("u2", [P, PG, HD])
        f_top, f_low, f_exp, f_sum, f_over, f_w = (sb("f_top", [P, 2 * J]), sb("f_low", [P, 2 * J, H]),
                                                   sb("f_exp", [P, 2 * J, H]), sb("f_sum", [P, 2 * J]),
                                                   sb("f_over", [P, 2 * J]), sb("f_w", [P, PG]))
        gated = sb("gated", [P, PG, HD])

        p_s = ps("p_s", [P, 2, L])
        p_t = ps("p_t", [P, 2, L])
        p_v = ps("p_v", [P, 2, L])
        p_in = ps("p_in", [P, 512])
        p_kv = ps("p_kv", [P, 512])

        loaded, built, parts_done, parts_moved = sem("loaded"), sem("built"), sem("parts_done"), sem("parts_moved")
        zeroed, masks = sem("zeroed"), sem("masks")
        resid_in, resid_out, resid_ready = sem("resid_in"), sem("resid_out"), sem("resid_ready")
        names = ("xn_ready xT_psum xT_ready sx_psum sx_ready nonzero_ready q_psum q_ready kv_psum kv_ready round_ready s_psum "
                 "top_ready top2_half top2_ready topT_psum topT_ready t_psum weighed values_psum sums_kept out_ready "
                 "gate_psum tok_psum z_over z_norm z_sum logits g_top g_low g_exp g_sum g_over g_w g_scaled prod_ready mixed_ready u_ready").split()
        s = {n: sem(n) for n in names}
        norm_names = "sum mean mid sq ss var rstd unit gain".split()
        ns = {n: sem("n_" + n + "_done") for n in norm_names}
        tail_names = ("fx_ready fxT_psum fxT_ready fc1_psum fc1_ready fc1n_ready fc2_psum fc2_kept u2_ready fout_ready "
                      "foT_psum foT_ready f_psum f_top f_low f_exp f_sum f_over f_w gated_ready x_ready").split()
        t = {n: sem(n) for n in tail_names}
        stored = sem("stored")
        ln_act, ln_dve, norm_ready = outer_norm(nc, ctx, sem, c["x_stats"], c["rstd"], c["shift"], "e_ln")
        block = ctx.enter_context(nc.Block())

        def spread(a, width):
            return a.rearrange("p (g o) -> p g o", o=1).broadcast_to([P, a.shape[1], width])

        def every(eng, prepare, turn_maxima, job, after_job, values, tail):
            def iteration(b, q, i, top, ahead):
                tails = not (isinstance(i, int) and i < 1)
                for n in range(JOBS):
                    job(b, q, n, top)
                    after_job(b, q, n)
                    if tails:
                        tail(i - 1, q, n)
                if ahead:
                    prepare(b + 2, q, 0, i)
                values(b, q, 1, 0)
                if ahead:
                    prepare(b + 2, q, 1, i)
                values(b, q, 1, 1)
                if top:
                    turn_maxima(b + 1)
                if tails:
                    tail(i - 1, q, JOBS)
                if ahead:
                    prepare(b + 2, q, 2, i)
                if tails:
                    tail(i - 1, q, JOBS + 1)

            for part in range(3):
                prepare(0, 0, part, 0)
            for n in range(JOBS):
                job(-1, 1, n, True)
            prepare(1, 1, 0, 0)
            prepare(1, 1, 1, 0)
            turn_maxima(0)
            prepare(1, 1, 2, 0)
            iteration(0, 0, 0, True, True)
            iteration(1, 1, 0, True, True)
            with eng.Fori(1, B // 2 - 1) as i:
                iteration(i * 2, 0, i, True, True)
                iteration(i * 2 + 1, 1, i, True, True)
            iteration(B - 2, 0, B // 2 - 1, True, False)
            iteration(B - 1, 1, B // 2 - 1, False, False)
            for q in range(2):
                for n in range(JOBS + 2):
                    if not q:
                        after_job(B, q, n)
                    tail(B // 2 - 1, q, n)

        def first(b):
            return isinstance(b, int) and b < 1

        def over(b):
            return isinstance(b, int) and b >= B

        @block.sync
        def _(sp):
            sp.wait_ge(zeroed, 5)
            sp.dma_start(w_hl[:, :], d["exp_hl"]).then_inc(loaded, 16)
            sp.dma_start(b_hl[:, :], d["exp_hl_b"]).then_inc(loaded, 16)
            sp.dma_start(b_fc1[:, :], d["exp_fc1_b"]).then_inc(loaded, 16)
            sp.dma_start(w_fgate[:, :], d["exp_fgate"]).then_inc(loaded, 16)
            sp.dma_start(row[:, :], d["exp_fc2_b"]).then_inc(loaded, 16)
            for j in range(J):
                sp.dma_start(b_gate[:, j, :], d["exp_gate_b"]).then_inc(loaded, 16)
            sp.dma_start(norms[:, :, :], d["exp_norms"]).then_inc(loaded, 16)
            for h in range(H):
                r = slice(h * HD, (h + 1) * HD)
                sp.dma_start(w_q[r, :, r], d["exp_q"][h]).then_inc(loaded, 16)
                sp.dma_start(w_kv[r, :, r], d["exp_kv"][h]).then_inc(loaded, 16)
                sp.dma_start(w_gate[r, :, h * E:(h + 1) * E], d["exp_gate"][h]).then_inc(loaded, 16)
                sp.dma_start(w_fc[r, :, r], d["exp_fc"]).then_inc(loaded, 16)
            sp.wait_ge(parts_done, 5)
            for n in range(3):
                sp.dma_start(bias3[n:n + 1, :], row_parts[:, n, :]).then_inc(parts_moved, 16)
            with sp.Fori(0, B // 2) as i:
                sp.wait_ge(t["x_ready"], i + 1)
                sp.dma_start(out[bass.ds(i * 2, 2)].rearrange("b (j p) d -> p b j d", p=P),
                             x[:, bass.ds(i * 2 * J, 2 * J), :].rearrange("p (b j) d -> p b j d", j=J))\
                  .then_inc(stored, 16)
            sp.wait_ge(stored, 16 * (B // 2))

        LOADED = 16 * (6 + J + 4 * H)
        MASKS = 8 + 2 * H

        @block.tensor
        def _(pe):
            pe.wait_ge(loaded, LOADED)
            pe.wait_ge(parts_moved, 16 * 3)
            pe.wait_ge(masks, MASKS)
            pe.wait_ge(built, 1)

            for n in range(H):
                pe.wait_ge(resid_in, 3 * n + 1)
                for j in range(J):
                    last = pe.transpose(p_in[:, j * P:(j + 1) * P], xn[:, n % 2, j, :], ident[:, :])
                last.then_inc(resid_out, 1)
                pe.wait_ge(resid_in, 3 * n + 2)
                pe.matmul(p_in[:, N:2 * N], w_hl[:, :], xT[:, :], start=True, stop=True).then_inc(resid_out, 1)
            pe.wait_ge(resid_in, 3 * H)
            for j in range(J):
                last = pe.transpose(p_in[:, j * P:(j + 1) * P], residT[:, j * P:(j + 1) * P], ident[:, :])
            last.then_inc(resid_out, 1)
            pe.wait_ge(resid_ready, 1)

            def prepare(b, q, part, tails):
                if part == 0:
                    pe.wait_ge(s["xn_ready"], b + 1)
                    for j in range(J):
                        last = pe.transpose(p_in[:, j * P:(j + 1) * P], xn[:, q, j, :], ident[:, :])
                    last.then_inc(s["xT_psum"], 1)
                elif part == 1:
                    pe.wait_ge(s["xT_ready"], b + 1)
                    pe.matmul(p_in[:, N:2 * N], w_hl[:, :], xT[:, :], start=True, stop=True).then_inc(s["sx_psum"], 1)
                else:
                    pe.wait_ge(s["sx_ready"], b + 1)
                    after(pe, s["kv_ready"], b)
                    if q:
                        after(pe, t["foT_ready"], tails)
                    pe.matmul(p_kv[:, 0:N], w_kv[:, 0, :], sxT[:, q, :], start=True, stop=True)
                    for j in range(J):
                        last = pe.matmul(p_kv[:, N + j * D:N + (j + 1) * D], sxT[:, q, j * P:(j + 1) * P], w_kv[:, 1, :],
                                         start=True, stop=True)
                    last.then_inc(s["kv_psum"], 1)
                    after(pe, s["top_ready"], b * JOBS)
                    for e in range(E):
                        last = pe.matmul(p_s[:, e // 2, (e % 2) * N:(e % 2 + 1) * N], w_q[:, e, :], sxT[:, q, :],
                                         start=True, stop=True)
                    last.then_inc(s["q_psum"], 1)

            def turn_maxima(b):
                if not (isinstance(b, int) and b >= B - 1):
                    pe.wait_ge(s["sx_ready"], b + 2)
                pe.wait_ge(s["top2_ready"], b + 1)
                for j in range(J):
                    last = pe.transpose(p_in[:, j * (P // 2):(j + 1) * (P // 2)].bitcast(BF16),
                                        top2[:, j, :, :].rearrange("p h c -> p (h c)"), ident16[:, :])
                last.then_inc(s["topT_psum"], 1)

            def gate_parts(b):
                pe.wait_ge(s["out_ready"], b * 2)
                pe.wait_ge(s["sums_kept"], b * 2)
                for j in range(J):
                    for e in range(E):
                        a = (j * E + e) * H * E
                        pe.matmul(p_in[:, a:a + H * E], outT[:, j, e, :], w_gate[:, e, :], start=True, stop=True)

            def job(b, q, n, top):
                h = n % H
                if not (isinstance(b, int) and b < 0):
                    frm, to = ROUNDS[n // H]
                    if n == 0:
                        pe.wait_ge(s["topT_ready"], b + 1)
                    after(pe, s["weighed"], b * JOBS + n - 1)
                    bank = p_t[:, n % 2, :]
                    if frm == to:
                        pe.matmul(bank.rearrange("p (e c) -> p e c", e=E), ident16[:, :],
                                  above[:, :].rearrange("p (o c) -> p o c", o=1).broadcast_to([P, E, P]),
                                  start=True, stop=False, skip_group_check=True)
                    for e in range(E):
                        pe.matmul(bank[:, e * P:(e + 1) * P], pick[:, h, e, :], topT[:, to * P:(to + 1) * P],
                                  start=e == 0 and frm != to, stop=False, skip_group_check=True)
                    pe.matmul(bank, kT[:, q, h, frm * P:(frm + 1) * P], qT[:, q, :, to * P:(to + 1) * P], start=False,
                              stop=True, skip_group_check=True).then_inc(s["t_psum"], 1)
                if n == 0 and not first(b):
                    gate_parts(b)
                if top:
                    to, start, count = TOP_ROUNDS[n // H]
                    cols = P * (to + 1)
                    if n == 0:
                        pe.wait_ge(s["round_ready"], b + 2)
                    after(pe, s["top_ready"], (b + 1) * JOBS + n - 1)
                    bank = p_s[:, n % 2, :]
                    for e in range(count):
                        pe.matmul(bank[:, e * cols:(e + 1) * cols], q_round[:, start + e, to * P:(to + 1) * P],
                                  k_round[:, h, 0:cols], start=e == 0, stop=False, skip_group_check=True)
                    pe.matmul(bank.rearrange("p (e c) -> p e c", e=count)[:, :, cols - P:cols], ident16[:, :],
                              below[:, :].rearrange("p (o c) -> p o c", o=1).broadcast_to([P, count, P]),
                              start=False, stop=True, skip_group_check=True).then_inc(s["s_psum"], 1)

            def after_job(b, q, n):
                if n == 0 and over(b):
                    gate_parts(b)
                if n == 1 and not first(b):
                    for j in range(J):
                        for e in range(E):
                            a = J * E * H * E + (j * E + e) * H
                            last = pe.matmul(p_in[:, a:a + H], sumsT[:, j, e, :], head_row[:, :], start=True,
                                             stop=True)
                    last.then_inc(s["gate_psum"], 1)
                if n == 2 and not first(b):
                    for j in range(J):
                        for e in range(E):
                            last = pe.transpose(p_v[:, j, e * P:(e + 1) * P], outT[:, j, e, :], ident[:, :])
                    last.then_inc(s["tok_psum"], 1)
                if n == 6 and not over(b):
                    for part in range(2):
                        values(b, q, 0, part)

            def values(b, q, to, part):
                if part == 0:
                    rounds = (1, 2) if to else (0,)
                    pe.wait_ge(s["weighed"], b * JOBS + (JOBS if to else H))
                    if to:
                        pe.wait_ge(s["out_ready"], b * 2 + 1)
                        pe.wait_ge(s["sums_kept"], b * 2 + 1)
                    else:
                        after(pe, s["prod_ready"], b * J)
                else:
                    rounds = (1, 2) if to else (0,)
                for n in rounds:
                    for h in range(H):
                        cols = slice(h * HD, (h + 1) * HD)
                        stat = c["ones"][:, 0:HD] if part else v[:, q, n // 2, cols]
                        last = pe.matmul(p_v[cols, part, :], stat, wT[:, n, h, :], start=n == rounds[0],
                                         stop=n == rounds[-1], tile_position=(0, h * HD), skip_group_check=True)
                last.then_inc(s["values_psum"], 1)

            def tail(i, q, n):
                turned = p_kv[:, :]
                if (q, n) == (1, 1):
                    pe.wait_ge(t["fx_ready"], i + 1)
                    for a in range(2 * J):
                        last = pe.transpose(turned[:, a * P:(a + 1) * P],
                                            fx[:, a * H:(a + 1) * H, :].rearrange("p h c -> p (h c)"), ident[:, :])
                    last.then_inc(t["fxT_psum"], 1)
                if (q, n) == (1, 2):
                    pe.wait_ge(t["fxT_ready"], i + 1)
                    pe.matmul(p_kv[:, :], w_fc[:, 0, :], fxT[:, :], start=True, stop=True).then_inc(t["fc1_psum"], 1)
                if (q, n) == (1, 4):
                    pe.wait_ge(t["fc1n_ready"], i + 1)
                    for a in range(2 * J):
                        part = p_kv[:, a * D:(a + 1) * D]
                        pe.matmul(part, c["ones3"][:, :], bias3[:, :], start=True, stop=False, skip_group_check=True)
                        last = pe.matmul(part, fc1n[:, a * P:(a + 1) * P], w_fc[:, 1, :], start=False, stop=True,
                                         skip_group_check=True)
                    last.then_inc(t["fc2_psum"], 1)
                if (q, n) == (1, 11):
                    pe.wait_ge(t["fout_ready"], i + 1)
                    for a in range(2 * J):
                        last = pe.transpose(turned[:, a * P:(a + 1) * P],
                                            fout[:, a * H:(a + 1) * H, :].rearrange("p h c -> p (h c)"), ident[:, :])
                    last.then_inc(t["foT_psum"], 1)
                if (q, n) == (1, JOBS):
                    pe.wait_ge(t["foT_ready"], i + 1)
                    for a in range(2 * J):
                        last = pe.matmul(p_t[:, 1, a * H:(a + 1) * H], foT[:, a * P:(a + 1) * P], w_fgate[:, :],
                                         start=True, stop=True)
                    last.then_inc(t["f_psum"], 1)
                if (q, n) == (1, JOBS + 1):
                    pe.wait_ge(t["f_low"], i + 1)

            every(pe, prepare, turn_maxima, job, after_job, values, tail)

        @block.scalar
        def _(act):
            ln_act(act)
            act.wait_ge(loaded, LOADED)
            act.wait_ge(masks, MASKS)
            for n in range(H):
                r = slice(n * HD, (n + 1) * HD)
                act.wait_ge(resid_out, 2 * n + 1)
                act.activation(xT[:, :], p_in[:, 0:N], ACT.Copy).then_inc(resid_in, 1)
                act.wait_ge(resid_out, 2 * n + 2)
                act.activation(residT[r, :], p_in[r, N:2 * N], ACT.Identity, bias=b_hl[r, :]).then_inc(resid_in, 1)
            act.wait_ge(resid_out, 2 * H + 1)
            act.activation(resid[:, :, :].rearrange("p j d -> p (j d)"), p_in[:, 0:N], ACT.Copy).then_inc(resid_ready, 1)

            def prepare(b, q, part, tails):
                if part == 0:
                    act.wait_ge(s["xT_psum"], b + 1)
                    act.activation(xT[:, :], p_in[:, 0:N], ACT.Copy).then_inc(s["xT_ready"], 1)
                elif part == 1:
                    act.wait_ge(s["sx_psum"], b + 1)
                    act.activation(sxT[:, q, :], p_in[:, N:2 * N], ACT.Identity, bias=b_hl[:, 0:1])\
                       .then_inc(s["sx_ready"], 1)
                else:
                    act.wait_ge(s["kv_psum"], b + 1)
                    for h in range(H):
                        r = slice(h * HD, (h + 1) * HD)
                        act.activation(kT[r, q, h, :], p_kv[r, 0:N], ACT.Copy)
                    act.activation(v[:, q, :, :].rearrange("p j d -> p (j d)"), p_kv[:, N:2 * N], ACT.Copy)\
                       .then_inc(s["kv_ready"], 1)
                    act.wait_ge(s["q_psum"], b + 1)
                    act.activation(qT[:, q, :, :].rearrange("p e n -> p (e n)"),
                                   p_s[:, :, :].rearrange("p a n -> p (a n)"), ACT.Copy).then_inc(s["q_ready"], 1)

            def turn_maxima(b):
                act.wait_ge(s["topT_psum"], b + 1)
                act.activation(topT[:, :], p_in[:, 0:P].bitcast(BF16), ACT.Copy).then_inc(s["topT_ready"], 1)

            def job(b, q, n, top):
                if isinstance(b, int) and b < 0:
                    return
                if n == 0:
                    after(act, s["values_psum"], b * 4)
                act.wait_ge(s["t_psum"], b * JOBS + n + 1)
                act.activation(wT[:, n // H, n % H, :], p_t[:, n % 2, :], ACT.Exp, scale=HD ** 0.5)\
                   .then_inc(s["weighed"], 1)

            def keep_sums(b, to):
                act.wait_ge(s["values_psum"], b * 4 + to * 2 + 2)
                after(act, s["gate_psum"], b)
                act.activation(sumsT[:, to, :, :].rearrange("p e c -> p (e c)"), p_v[:, 1, :], ACT.Copy)\
                   .then_inc(s["sums_kept"], 1)

            def after_job(b, q, n):
                if n == 7 and not over(b):
                    keep_sums(b, 0)
                if n == 3 and not first(b):
                    act.wait_ge(s["g_low"], b)
                    act.activation(g_exp[:, :, :], g_low[:, :, :], ACT.Exp).then_inc(s["g_exp"], 1)

            def values(b, q, to, part):
                if part == 1:
                    keep_sums(b, to)

            def square(i, n):
                act.wait_ge(ns["mid"], i * 2 + n)
                act.activation(n_sq[:, :, :], n_mid[:, :, :], ACT.Square).then_inc(ns["sq"], 1)

            def tail(i, q, n):
                if (q, n) == (0, 7):
                    square(i, 1)
                if (q, n) == (1, 1):
                    act.wait_ge(t["fxT_psum"], i + 1)
                    act.activation(fxT[:, :], p_kv[:, :], ACT.Copy).then_inc(t["fxT_ready"], 1)
                if (q, n) == (1, 2):
                    act.wait_ge(t["fc1_psum"], i + 1)
                    act.activation(fc1[:, :], p_kv[:, :], ACT.Relu, bias=b_fc1[:, 0:1]).then_inc(t["fc1_ready"], 1)
                if (q, n) == (1, 6):
                    square(i, 2)
                if (q, n) == (1, 11):
                    act.wait_ge(t["foT_psum"], i + 1)
                    act.activation(foT[:, :], p_kv[:, :], ACT.Copy).then_inc(t["foT_ready"], 1)
                if (q, n) == (1, JOBS + 1):
                    act.wait_ge(t["f_low"], i + 1)
                    act.activation(f_exp[:, :, :], f_low[:, :, :], ACT.Exp).then_inc(t["f_exp"], 1)

            every(act, prepare, turn_maxima, job, after_job, values, tail)

        @block.vector
        def _(dve):
            ln_dve(dve)
            dve.wait_ge(loaded, LOADED)
            split_rows(dve, row[:, :], row_work[:, :], [row_parts[:, n, :] for n in range(3)], parts_done)
            dve.wait_ge(norm_ready, 1)
            dve.wait_ge(masks, MASKS)
            dve.tensor_copy(ident16[:, :], ident[:, :]).then_inc(built, 1)

            def normalise(q, b):
                for j in range(J):
                    a = b * J + j
                    last = dve.tensor_scalar(xn[:, q, j, :], x[:, a, :], c["rstd"][:, bass.ds(a, 1)],
                                             c["shift"][:, bass.ds(a, 1)], ALU.mult, ALU.add)
                return last

            for n in range(H):
                if n >= 2:
                    dve.wait_ge(resid_out, 2 * (n - 2) + 1)
                if n:
                    dve.wait_ge(resid_in, 3 * n)
                normalise(n % 2, n).then_inc(resid_in, 1)
            dve.wait_ge(resid_ready, 1)

            def normalise_ahead(b, q):
                after(dve, s["xT_psum"], b - 1)
                normalise(q, b).then_inc(s["xn_ready"], 1)

            def prepare(b, q, part, tails):
                if part == 0 and isinstance(b, int) and b < 2:
                    normalise_ahead(b, q)
                elif part == 2:
                    dve.wait_ge(s["sx_ready"], b + 1)
                    dve.tensor_scalar(nonzero[:, q, :, :].rearrange("p j c -> p (j c)"), sxT[:, q, :], 0.0, None,
                                      ALU.not_equal).then_inc(s["nonzero_ready"], 1)
                    after(dve, s["s_psum"], b * JOBS)
                    dve.wait_ge(s["kv_ready"], b + 1)
                    dve.tensor_copy(k_round[:, :, :], kT[:, q, :, :])
                    dve.wait_ge(s["q_ready"], b + 1)
                    dve.tensor_copy(q_round[:, :, :], qT[:, q, :, :]).then_inc(s["round_ready"], 1)

            def turn_maxima(b):
                dve.wait_ge(s["top_ready"], (b + 1) * JOBS)
                high, low = [top2[:, :, :, n:2 * E:2].rearrange("p j h e -> p (j h) e") for n in range(2)]
                all_top = top[:, :, :, :].rearrange("p j h e -> p (j h) e")
                after(dve, s["topT_psum"], b)
                dve.tensor_copy(high, all_top).then_inc(s["top2_half"], 1)
                dve.wait_ge(s["top2_half"], b + 1)
                dve.tensor_tensor(low, all_top, high, ALU.subtract).then_inc(s["top2_ready"], 1)

            def job(b, q, n, top_too):
                if not top_too:
                    return
                to, first, count = TOP_ROUNDS[n // H]
                dve.wait_ge(s["s_psum"], (b + 1) * JOBS + n + 1)
                dve.tensor_reduce(top[:, to, n % H, first:first + count],
                                  p_s[:, n % 2, :].rearrange("p (e c) -> p e c", e=count), AX.X, ALU.max)\
                   .then_inc(s["top_ready"], 1)

            def outputs(b, q, to):
                dve.wait_ge(s["nonzero_ready"], b + 1)
                dve.wait_ge(s["values_psum"], b * 4 + to * 2 + 1)
                dve.tensor_tensor(outT[:, to, :, :], p_v[:, 0, :].rearrange("p (e c) -> p e c", e=E),
                                  nonzero[:, q, to:to + 1, :].broadcast_to([P, E, P]), ALU.mult)\
                   .then_inc(s["out_ready"], 1)

            def values(b, q, to, part):
                if part == 1:
                    outputs(b, q, to)

            def after_job(b, q, n):
                if n == 8 and not over(b):
                    outputs(b, q, 0)
                if n == 9 and not (isinstance(b, int) and b >= B - 2):
                    normalise_ahead(b + 2, q)
                if first(b):
                    return
                if n == 2:
                    dve.wait_ge(s["gate_psum"], b)
                    flat = J * E * H
                    dve.reciprocal(z_over[:, :], p_in[:, flat * E:flat * (E + 1)]).then_inc(s["z_over"], 1)
                    dve.wait_ge(s["z_over"], b)
                    dve.tensor_tensor(z_norm[:, :, :, :].rearrange("p j e (h g) -> p (j e h) g", h=H),
                                      p_in[:, 0:flat * E].rearrange("p (a g) -> p a g", g=E),
                                      spread(z_over[:, :], E), ALU.mult).then_inc(s["z_norm"], 1)
                    dve.wait_ge(s["z_norm"], b)
                    dve.tensor_reduce(z_sum[:, :, :], z_norm[:, :, :, :].rearrange("p j e a -> p j a e"), AX.X,
                                      ALU.add).then_inc(s["z_sum"], 1)
                    dve.wait_ge(s["z_sum"], b)
                    dve.tensor_tensor(logits[:, :, :], z_sum[:, :, :], b_gate[:, :, :], ALU.add)\
                       .then_inc(s["logits"], 1)
                    dve.wait_ge(s["logits"], b)
                    gate = logits[:, :, :].rearrange("p j (h g) -> p (j h) g", h=H)
                    dve.tensor_reduce(g_top[:, :], gate, AX.X, ALU.max).then_inc(s["g_top"], 1)
                    dve.wait_ge(s["g_top"], b)
                    dve.tensor_tensor(g_low[:, :, :], gate, spread(g_top[:, :], E), ALU.subtract).then_inc(s["g_low"], 1)
                if n == 3:
                    dve.wait_ge(s["g_exp"], b)
                    dve.tensor_reduce(g_sum[:, :], g_exp[:, :, :], AX.X, ALU.add).then_inc(s["g_sum"], 1)
                    dve.wait_ge(s["g_sum"], b)
                    dve.reciprocal(g_over[:, :], g_sum[:, :]).then_inc(s["g_over"], 1)
                    dve.wait_ge(s["g_over"], b)
                    dve.tensor_tensor(g_w[:, :, :], g_exp[:, :, :], spread(g_over[:, :], E), ALU.mult)\
                       .then_inc(s["g_w"], 1)
                    dve.wait_ge(s["g_w"], b)
                    for j in range(J):
                        last = dve.tensor_tensor(g_scaled[:, j * H:(j + 1) * H, :], g_w[:, j * H:(j + 1) * H, :],
                                                 z_over[:, j * E * H:(j + 1) * E * H].rearrange("p (e h) -> p h e", h=H),
                                                 ALU.mult)
                    last.then_inc(s["g_scaled"], 1)
                if n in (3, 4):
                    if n == 3:
                        dve.wait_ge(s["tok_psum"], b)
                        dve.wait_ge(s["g_scaled"], b)
                    for j in (n - 3,):
                        for e in range(E):
                            last = dve.tensor_tensor(prod[:, j, e, :].rearrange("p (h c) -> p h c", h=H),
                                                     p_v[:, j, e * P:(e + 1) * P].rearrange("p (h c) -> p h c", h=H),
                                                     g_scaled[:, j * H:(j + 1) * H, e:e + 1].broadcast_to([P, H, HD]),
                                                     ALU.mult)
                        last.then_inc(s["prod_ready"], 1)
                if n == 5:
                    dve.wait_ge(s["prod_ready"], b * J)
                    dve.tensor_reduce(mixed[:, :, :], prod[:, :, :, :].rearrange("p j e c -> p j c e"), AX.X, ALU.add)\
                       .then_inc(s["mixed_ready"], 1)
                    dve.wait_ge(s["mixed_ready"], b)
                    dve.tensor_tensor(u[:, 1 - q, :, :], mixed[:, :, :], resid[:, :, :], ALU.add)\
                       .then_inc(s["u_ready"], 1)

            def norm(i, n, src, part):
                k = i * 2 + n
                if part == 0:
                    dve.tensor_reduce(n_sum[:, :], src, AX.X, ALU.add).then_inc(ns["sum"], 1)
                    dve.wait_ge(ns["sum"], k)
                    dve.tensor_scalar(n_mean[:, :], n_sum[:, :], 1.0 / HD, None, ALU.mult).then_inc(ns["mean"], 1)
                    dve.wait_ge(ns["mean"], k)
                    dve.tensor_tensor(n_mid[:, :, :], src, spread(n_mean[:, :], HD), ALU.subtract)\
                       .then_inc(ns["mid"], 1)
                if part == 1:
                    dve.wait_ge(ns["sq"], k)
                    dve.tensor_reduce(n_ss[:, :], n_sq[:, :, :], AX.X, ALU.add).then_inc(ns["ss"], 1)
                    dve.wait_ge(ns["ss"], k)
                    dve.tensor_scalar(n_var[:, :], n_ss[:, :], 1.0 / HD, NORM_EPS, ALU.mult, ALU.add)\
                       .then_inc(ns["var"], 1)
                if part == 2:
                    dve.wait_ge(ns["rstd"], k)
                    dve.tensor_tensor(n_unit[:, :, :], n_mid[:, :, :], spread(n_rstd[:, :], HD), ALU.mult)\
                       .then_inc(ns["unit"], 1)
                    dve.wait_ge(ns["unit"], k)
                    dst, done = ((fx, t["fx_ready"]), (fout, t["fout_ready"]))[n - 1]
                    gain = norms[:, 2 * n - 2:2 * n - 1, :].broadcast_to([P, PG, HD])
                    offset = norms[:, 2 * n - 1:2 * n, :].broadcast_to([P, PG, HD])
                    dve.tensor_tensor(n_gain[:, :, :], n_unit[:, :, :], gain, ALU.mult).then_inc(ns["gain"], 1)
                    dve.wait_ge(ns["gain"], k)
                    dve.tensor_tensor(dst[:, :, :], n_gain[:, :, :], offset, ALU.add).then_inc(done, 1)

            def tail(i, q, n):
                groups = u[:, :, :, :].rearrange("p q j (h c) -> p (q j h) c", h=H)
                flat = "p g c -> p (g c)"
                if (q, n) == (0, 6):
                    dve.wait_ge(s["u_ready"], i * 2 + 2)
                    norm(i, 1, groups, 0)
                if (q, n) == (0, 8):
                    norm(i, 1, groups, 1)
                if (q, n) == (0, 11):
                    norm(i, 1, groups, 2)
                if (q, n) == (1, 2):
                    dve.wait_ge(t["fc1_ready"], i + 1)
                    dve.scalar_tensor_tensor(fc1n[:, :], fxT[:, :], 0.0, fc1[:, :], ALU.not_equal, ALU.mult)\
                       .then_inc(t["fc1n_ready"], 1)
                if (q, n) == (1, 5):
                    dve.wait_ge(t["fc2_psum"], i + 1)
                    dve.scalar_tensor_tensor(fc2[:, :, :].rearrange(flat), fx[:, :, :].rearrange(flat), 0.0, p_kv[:, :],
                                             ALU.not_equal, ALU.mult).then_inc(t["fc2_kept"], 1)
                    dve.wait_ge(t["fc2_kept"], i + 1)
                    dve.tensor_tensor(u2[:, :, :], fc2[:, :, :], fx[:, :, :], ALU.add).then_inc(t["u2_ready"], 1)
                    dve.wait_ge(t["u2_ready"], i + 1)
                    norm(i, 2, u2[:, :, :], 0)
                if (q, n) == (1, 7):
                    norm(i, 2, u2[:, :, :], 1)
                if (q, n) == (1, 9):
                    norm(i, 2, u2[:, :, :], 2)
                if (q, n) == (1, JOBS):
                    logits = p_t[:, 1, 0:2 * J * H].rearrange("p (a h) -> p a h", h=H)
                    dve.wait_ge(t["f_psum"], i + 1)
                    dve.tensor_reduce(f_top[:, :], logits, AX.X, ALU.max).then_inc(t["f_top"], 1)
                    dve.wait_ge(t["f_top"], i + 1)
                    dve.tensor_tensor(f_low[:, :, :], logits, spread(f_top[:, :], H), ALU.subtract)\
                       .then_inc(t["f_low"], 1)
                if (q, n) == (1, JOBS + 1):
                    dve.wait_ge(t["f_exp"], i + 1)
                    dve.tensor_reduce(f_sum[:, :], f_exp[:, :, :], AX.X, ALU.add).then_inc(t["f_sum"], 1)
                    dve.wait_ge(t["f_sum"], i + 1)
                    dve.reciprocal(f_over[:, :], f_sum[:, :]).then_inc(t["f_over"], 1)
                    dve.wait_ge(t["f_over"], i + 1)
                    dve.tensor_tensor(f_w[:, :].rearrange("p (a h) -> p a h", h=H), f_exp[:, :, :],
                                      spread(f_over[:, :], H), ALU.mult).then_inc(t["f_w"], 1)
                    dve.wait_ge(t["f_w"], i + 1)
                    dve.tensor_tensor(gated[:, :, :], fout[:, :, :], spread(f_w[:, :], HD), ALU.mult)\
                       .then_inc(t["gated_ready"], 1)

            every(dve, prepare, turn_maxima, job, after_job, values, tail)

        @block.gpsimd
        def _(pool):
            for a in (w_q, w_kv, w_gate, w_fc):
                pool.memset(a[:, :, :], 0.0).then_inc(zeroed, 1)
            pool.memset(head_row[:, :], 0.0).then_inc(zeroed, 1)
            pool.wait_ge(zeroed, 5)
            pool.memset(below[:, :], 0.0).then_inc(masks, 1)
            pool.memset(above[:, :], 0.0).then_inc(masks, 1)
            pool.memset(top2[:, :, :, :], 0.0).then_inc(masks, 1)
            pool.memset(pick[:, :, :, :], 0.0).then_inc(masks, 1)
            pool.memset(kT[:, :, :, :], 0.0).then_inc(masks, 1)
            pool.wait_ge(masks, 5)
            pool.affine_select(out=below[:, :], in_=below[:, :], compare_op=ALU.is_ge, fill=MASKED, base=0,
                               pattern=[[-1, P]], channel_multiplier=1).then_inc(masks, 1)
            pool.affine_select(out=above[:, :], in_=above[:, :], compare_op=ALU.is_ge, fill=MASKED, base=0,
                               pattern=[[1, P]], channel_multiplier=-1).then_inc(masks, 1)
            for k in range(2 * H):
                h, n = divmod(k, 2)
                pool.wait_ge(masks, 7 + k)
                pool.affine_select(out=pick[:, h, :, :], in_=pick[:, h, :, :], compare_op=ALU.not_equal, fill=-1.0,
                                   base=-n - h * HD, pattern=[[-2, E], [0, P]], channel_multiplier=1).then_inc(masks, 1)
            pool.affine_select(out=head_row[:, :], in_=head_row[:, :], compare_op=ALU.not_equal, fill=1.0, base=0,
                               pattern=[[-HD, H]], channel_multiplier=1).then_inc(masks, 1)
            pool.wait_ge(resid_ready, 1)
            pool.wait_ge(loaded, LOADED)

            def nothing(*_):
                pass

            def root(i, n):
                k = i * 2 + n
                pool.wait_ge(ns["var"], k)
                pool.tensor_tensor(n_rstd[:, :], n_var[:, :], c["minus_half"][:, 0:PG], ALU.pow).then_inc(ns["rstd"], 1)

            def tail(i, q, n):
                if (q, n) == (0, 6):
                    root(i, 1)
                if (q, n) == (1, 7):
                    root(i, 2)
                if (q, n) == (1, JOBS + 1):
                    pool.wait_ge(t["gated_ready"], i + 1)
                    xi = x[:, bass.ds(i * 2 * J, 2 * J), :]
                    pool.tensor_tensor(xi, xi, gated[:, :, :].rearrange("p (a h) c -> p a (h c)", h=H), ALU.add)\
                        .then_inc(t["x_ready"], 1)

            every(pool, nothing, nothing, nothing, nothing, nothing, tail)


STAGES = [stage_gated_conv, stage_recurrent, stage_graph_attention]
LAST = stage_expert_attention


def more(inputs, row, col, wide):
    import numpy as _np

    return {
        "ffn_w": inputs["L0_ffn_W"].T, "ffn_b": row("L0_ffn_b"),
        "ffn_ln_w": col("L0_ffn_ln_w"), "ffn_ln_b": col("L0_ffn_ln_b"),
        "att_lin": inputs["L1_gnn_W_lin"], "att_q": inputs["L1_gnn_W_q"], "att_k": inputs["L1_gnn_W_k"],
        "att_b": row("L1_gnn_b_lin"), "att_g": wide("L1_gnn_ln_g"), "att_o": wide("L1_gnn_ln_b"),
        "exp_hl": inputs["L1_ffn_hl_w"].reshape(D, D).T, "exp_hl_b": col("L1_ffn_hl_b"),
        "exp_q": inputs["L1_ffn_wq"].transpose(0, 3, 1, 2),
        "exp_kv": _np.stack([inputs["L1_ffn_wk"], inputs["L1_ffn_wv"]]).transpose(1, 3, 0, 2),
        "exp_gate": inputs["L1_ffn_gate_w"].reshape(H, E, E, HD).transpose(0, 3, 2, 1),
        "exp_gate_b": wide("L1_ffn_gate_b"), "exp_fc2_b": _np.concatenate([row("L1_ffn_fc2_b")] * H, axis=1),
        "exp_norms": _np.broadcast_to(_np.stack([inputs[f"L1_ffn_{n}"] for n in ("ln_g", "ln_b", "fnorm_g", "fnorm_b")]),
                                      (P, 4, HD)),
        "exp_fc": _np.stack([inputs["L1_ffn_fc1_w"], inputs["L1_ffn_fc2_w"]]).transpose(2, 0, 1),
        "exp_fc1_b": _np.concatenate([col("L1_ffn_fc1_b")] * H),
        "exp_fgate": inputs["L1_ffn_fgate_w"].T,
    }


def program(nc, d, out):
    with ExitStack() as ctx:
        def sb(n, s, t=F32):
            return ctx.enter_context(nc.sbuf_tensor(n, s, t))

        c = {
            "x": sb("x", [P, TILES, D]), "ident": sb("ident", [P, P]), "ones": sb("ones", [P, P]),
            "ones3": sb("ones3", [3, P], BF16), "minus_half": sb("minus_half", [P, 16]),
            "x_stats": sb("x_stats", [P, TILES, 2]), "rstd": sb("rstd", [P, TILES]), "shift": sb("shift", [P, TILES]),
        }
        stage_setup(nc, d, c)
        for stage in STAGES:
            stage(nc, d, c)
        LAST(nc, d, c, out)


def kernel(**inputs):
    import numpy as _np
    import concourse.bacc as _bacc
    from concourse import mybir as _mybir
    from concourse.bass_utils import run_bass_kernel_spmd as _run

    def row(name):
        return inputs[name].reshape(1, -1)

    def col(name):
        return inputs[name].reshape(-1, 1)

    def wide(name):
        return _np.broadcast_to(inputs[name].reshape(1, -1), (P, inputs[name].size))

    data = {
        "x": inputs["x"], "adj": inputs["adj"],
        "conv1": inputs["L0_gnn_conv1_w"][:, :, 0].T, "conv2": inputs["L0_gnn_conv2_w"].transpose(1, 2, 0),
        "wmsg": inputs["L0_gnn_w_msg"].T, "wih": inputs["L0_gnn_w_ih"].T, "whh": inputs["L0_gnn_w_hh"].T,
        "wse": inputs["L0_gnn_w_se"].T, "bse": col("L0_gnn_b_se"),
        "bih": row("L0_gnn_b_ih"), "bhh": row("L0_gnn_b_hh"), "bmsg": row("L0_gnn_b_msg"),
    }
    for n in ("bn1", "bn2"):
        for v in "gbmv":
            data[f"{n}_{v}"] = col(f"L0_gnn_{n}_{v}")
    data |= more(inputs, row, col, wide)
    nc = _bacc.Bacc("TRN2", target_bir_lowering=False, num_devices=1)
    arrays, d = {}, {}
    for name, a in data.items():
        a = _np.ascontiguousarray(a)
        arrays[f"in_{name}"] = a
        d[name] = nc.dram_tensor(f"in_{name}", a.shape, _mybir.dt.from_np(a.dtype), kind="ExternalInput").ap()
    out = nc.dram_tensor("out_0", (B, N, D), F32, kind="ExternalOutput").ap()
    program(nc, d, out)
    return _run(nc, [arrays], core_ids=[0]).results[0]["out_0"]
```
